# Optimizing a Trainium2 kernel written in Bass

```python
import numpy as np
import jax
import jax.numpy as jnp

def _softmax(x, axis=-1):
    return jax.nn.softmax(x, axis=axis)
def _gelu(x):
    return jax.nn.gelu(x, approximate=True)
def _silu(x):
    return jax.nn.silu(x)
def _sigmoid(x):
    return jax.nn.sigmoid(x)
def _layernorm(x, axis=-1, eps=1e-5):
    m = jnp.mean(x, axis=axis, keepdims=True)
    v = jnp.var(x, axis=axis, keepdims=True)
    return (x - m) / jnp.sqrt(v + eps)
def _scatter_add(tgt, idx, src, axis=0):
    return tgt.at[idx].add(src)
def _segment_sum(src, seg, n):
    return jax.ops.segment_sum(src, seg, n)

kernel_name = 'mk_metaformer_d1_conv_nchw256_b25313'

def setup_inputs(seed: int = 0):
    np.random.seed(seed)
    _w = jnp.asarray
    def _rec_inputs():
        import jax
        import jax.numpy as jnp
        _gk = jax.random.key(seed)
        x = -0.0001732 + 1 * jax.random.normal(jax.random.fold_in(_gk, 1), (2, 256, 96, 96), jnp.float32)
        return x
    x = _rec_inputs()
    def _L0_conv_setup():
        import jax, jax.numpy as jnp
        import numpy as np
        from jax import lax
        DILATIONS = (1, 4, 8, 12)
        GROUP = 1
        K = 9
        GN_GROUPS = 32
        GN_EPS = 1e-05

        def _branch(x, w, d):
            N, C, H, W = x.shape
            g, R = (GROUP, C // GROUP)
            f = lax.conv_general_dilated(x, w, (1, 1), [(d, d), (d, d)], rhs_dilation=(d, d), dimension_numbers=('NCHW', 'OIHW', 'NCHW'))
            f = jax.nn.softmax(f.reshape(N, g, K, H * W), axis=2)
            xp = jnp.pad(x, ((0, 0), (0, 0), (d, d), (d, d)))
            patches = jnp.stack([xp[:, :, i * d:i * d + H, j * d:j * d + W] for i in range(3) for j in range(3)], axis=2)
            patches = patches.reshape(N, g, R, K, H * W)
            out = jnp.einsum('ngrkp,ngkp->ngrp', patches, f)
            return out.reshape(N, C, H, W)

        def _group_norm(y, gamma, beta):
            N, C, H, W = y.shape
            yg = y.reshape(N, GN_GROUPS, -1)
            mu = yg.mean(axis=-1, keepdims=True)
            var = yg.var(axis=-1, keepdims=True)
            yn = ((yg - mu) * lax.rsqrt(var + GN_EPS)).reshape(N, C, H, W)
            return yn * gamma[None, :, None, None] + beta[None, :, None, None]
        key = jax.random.key(seed)
        ks = jax.random.split(key, 6)
        N, C, H, W = (2, 256, 96, 96)
        x = jax.random.normal(ks[0], (N, C, H, W), jnp.float32)
        sc = 0.05
        w_a = jax.random.normal(ks[1], (K * GROUP, C, 3, 3), jnp.float32) * sc
        w_b = jax.random.normal(ks[2], (K * GROUP, C, 3, 3), jnp.float32) * sc
        w_c = jax.random.normal(ks[3], (K * GROUP, C, 3, 3), jnp.float32) * sc
        w_d = jax.random.normal(ks[4], (K * GROUP, C, 3, 3), jnp.float32) * sc
        w_proj = jax.random.normal(ks[5], (C, 5 * C, 1, 1), jnp.float32) * sc
        b_proj = jnp.zeros((C,), jnp.float32)
        gn_gamma = jnp.ones((C,), jnp.float32)
        gn_beta = jnp.zeros((C,), jnp.float32)
        return {'x': x, 'w_a': w_a, 'w_b': w_b, 'w_c': w_c, 'w_d': w_d, 'w_proj': w_proj, 'b_proj': b_proj, 'gn_gamma': gn_gamma, 'gn_beta': gn_beta}
    _L0_conv_all = _L0_conv_setup()
    _L0_conv_in = {k: v for k, v in _L0_conv_all.items() if k in ('w_a', 'w_b', 'w_c', 'w_d', 'w_proj', 'b_proj', 'gn_gamma', 'gn_beta', )}
    del _L0_conv_all

    def _L0_ffn_setup():
        import jax, jax.numpy as jnp
        import numpy as np
        NUM_EXPERTS = 8
        TOP_K = 2
        B, S, D = (8, 8192, 256)

        def _moe(tokens, router_w, w1, b1, w2, b2):
            N = tokens.shape[0]
            E = router_w.shape[0]
            logits = tokens.astype(jnp.float32) @ router_w.astype(jnp.float32).T
            probs = jax.nn.softmax(logits, axis=-1)
            rw, re = jax.lax.top_k(probs, TOP_K)
            if TOP_K > 1:
                rw = rw / jnp.maximum(rw.sum(-1, keepdims=True), 1e-12)
            rw = rw.astype(tokens.dtype)
            combine = jnp.zeros((N, E), tokens.dtype).at[jnp.arange(N)[:, None], re].set(rw)
            out = tokens
            for e in range(E):
                h = jax.nn.gelu(tokens @ w1[e] + b1[e], approximate=False)
                y = h @ w2[e] + b2[e]
                out = out + combine[:, e:e + 1] * y
            return out
        key = jax.random.key(seed)
        ks = jax.random.split(key, 4)
        scale = 1.0 / np.sqrt(D).astype(np.float32)
        return {'input_embeddings': jax.random.normal(ks[0], (B, S, D), jnp.float32), 'router_w': jax.random.normal(ks[1], (NUM_EXPERTS, D), jnp.float32) * scale, 'w1': jax.random.normal(ks[2], (NUM_EXPERTS, D, D), jnp.float32) * scale, 'b1': jnp.zeros((NUM_EXPERTS, D), jnp.float32), 'w2': jax.random.normal(ks[3], (NUM_EXPERTS, D, D), jnp.float32) * scale, 'b2': jnp.zeros((NUM_EXPERTS, D), jnp.float32)}
    _L0_ffn_all = _L0_ffn_setup()
    _L0_ffn_in = {k: v for k, v in _L0_ffn_all.items() if k in ('router_w', 'w1', 'b1', 'w2', 'b2', )}
    del _L0_ffn_all

    return {
        "x": x,
        "L0_conv_w_a": _L0_conv_in["w_a"],
        "L0_conv_w_b": _L0_conv_in["w_b"],
        "L0_conv_w_c": _L0_conv_in["w_c"],
        "L0_conv_w_d": _L0_conv_in["w_d"],
        "L0_conv_w_proj": _L0_conv_in["w_proj"],
        "L0_conv_b_proj": _L0_conv_in["b_proj"],
        "L0_conv_gn_gamma": _L0_conv_in["gn_gamma"],
        "L0_conv_gn_beta": _L0_conv_in["gn_beta"],
        "L0_ffn_router_w": _L0_ffn_in["router_w"],
        "L0_ffn_w1": _L0_ffn_in["w1"],
        "L0_ffn_b1": _L0_ffn_in["b1"],
        "L0_ffn_w2": _L0_ffn_in["w2"],
        "L0_ffn_b2": _L0_ffn_in["b2"],
    }

def reference(x, L0_conv_w_a, L0_conv_w_b, L0_conv_w_c, L0_conv_w_d, L0_conv_w_proj, L0_conv_b_proj, L0_conv_gn_gamma, L0_conv_gn_beta, L0_ffn_router_w, L0_ffn_w1, L0_ffn_b1, L0_ffn_w2, L0_ffn_b2):
    import jax
    import jax.numpy as jnp
    def _L0_conv_ref(x, w_a, w_b, w_c, w_d, w_proj, b_proj, gn_gamma, gn_beta):
        import jax, jax.numpy as jnp
        import numpy as np
        from jax import lax
        DILATIONS = (1, 4, 8, 12)
        GROUP = 1
        K = 9
        GN_GROUPS = 32
        GN_EPS = 1e-05

        def _branch(x, w, d):
            N, C, H, W = x.shape
            g, R = (GROUP, C // GROUP)
            f = lax.conv_general_dilated(x, w, (1, 1), [(d, d), (d, d)], rhs_dilation=(d, d), dimension_numbers=('NCHW', 'OIHW', 'NCHW'))
            f = jax.nn.softmax(f.reshape(N, g, K, H * W), axis=2)
            xp = jnp.pad(x, ((0, 0), (0, 0), (d, d), (d, d)))
            patches = jnp.stack([xp[:, :, i * d:i * d + H, j * d:j * d + W] for i in range(3) for j in range(3)], axis=2)
            patches = patches.reshape(N, g, R, K, H * W)
            out = jnp.einsum('ngrkp,ngkp->ngrp', patches, f)
            return out.reshape(N, C, H, W)

        def _group_norm(y, gamma, beta):
            N, C, H, W = y.shape
            yg = y.reshape(N, GN_GROUPS, -1)
            mu = yg.mean(axis=-1, keepdims=True)
            var = yg.var(axis=-1, keepdims=True)
            yn = ((yg - mu) * lax.rsqrt(var + GN_EPS)).reshape(N, C, H, W)
            return yn * gamma[None, :, None, None] + beta[None, :, None, None]
        outs = [x]
        for w, d in zip((w_a, w_b, w_c, w_d), DILATIONS):
            outs.append(_branch(x, w, d))
        cat = jnp.concatenate(outs, axis=1)
        y = lax.conv_general_dilated(cat, w_proj, (1, 1), [(0, 0), (0, 0)], dimension_numbers=('NCHW', 'OIHW', 'NCHW'))
        y = y + b_proj[None, :, None, None]
        y = _group_norm(y, gn_gamma, gn_beta)
        return jax.nn.relu(y)

    def _L0_ffn_ref(input_embeddings, router_w, w1, b1, w2, b2):
        import jax, jax.numpy as jnp
        import numpy as np
        NUM_EXPERTS = 8
        TOP_K = 2
        B, S, D = (8, 8192, 256)

        def _moe(tokens, router_w, w1, b1, w2, b2):
            N = tokens.shape[0]
            E = router_w.shape[0]
            logits = tokens.astype(jnp.float32) @ router_w.astype(jnp.float32).T
            probs = jax.nn.softmax(logits, axis=-1)
            rw, re = jax.lax.top_k(probs, TOP_K)
            if TOP_K > 1:
                rw = rw / jnp.maximum(rw.sum(-1, keepdims=True), 1e-12)
            rw = rw.astype(tokens.dtype)
            combine = jnp.zeros((N, E), tokens.dtype).at[jnp.arange(N)[:, None], re].set(rw)
            out = tokens
            for e in range(E):
                h = jax.nn.gelu(tokens @ w1[e] + b1[e], approximate=False)
                y = h @ w2[e] + b2[e]
                out = out + combine[:, e:e + 1] * y
            return out
        b, s, d = input_embeddings.shape
        tokens = input_embeddings.reshape(b * s, d)
        return _moe(tokens, router_w, w1, b1, w2, b2).reshape(b, s, d)

    def _gn(v, G=32, eps=1e-5):
        B_, C_, H_, W_ = v.shape
        g = v.reshape(B_, G, C_ // G, H_, W_)
        m = jnp.mean(g, axis=(2, 3, 4), keepdims=True)
        s = jnp.var(g, axis=(2, 3, 4), keepdims=True)
        return ((g - m) / jnp.sqrt(s + eps)).reshape(v.shape)

    def _ln_c(v, eps=1e-6):
        m = jnp.mean(v, axis=1, keepdims=True)
        s = jnp.var(v, axis=1, keepdims=True)
        return (v - m) / jnp.sqrt(s + eps)

    def _ln_t(v, eps=1e-5):
        m = jnp.mean(v, axis=-1, keepdims=True)
        s = jnp.var(v, axis=-1, keepdims=True)
        return (v - m) / jnp.sqrt(s + eps)

    def _to_tokens(v):
        B_, C_, H_, W_ = v.shape
        return v.reshape(B_, C_, H_ * W_).transpose(0, 2, 1)
    def _from_tokens(t, like):
        B_, C_, H_, W_ = like.shape
        return t.transpose(0, 2, 1).reshape(B_, C_, H_, W_)

    x = x + _L0_conv_ref(_ln_c(x), L0_conv_w_a, L0_conv_w_b, L0_conv_w_c, L0_conv_w_d, L0_conv_w_proj, L0_conv_b_proj, L0_conv_gn_gamma, L0_conv_gn_beta)
    t = _to_tokens(x)
    t = t + _L0_ffn_ref(_ln_t(t), L0_ffn_router_w, L0_ffn_w1, L0_ffn_b1, L0_ffn_w2, L0_ffn_b2)
    x = _from_tokens(t, x)
    return x


_drawn_inputs = setup_inputs


def setup_inputs(seed=0):
    import zlib

    import numpy as np

    out = dict(_drawn_inputs(seed))
    spreads = {'L0_conv_b_proj': (0.0, 0.1),
     'L0_conv_gn_gamma': (1.0, 0.2),
     'L0_conv_gn_beta': (0.0, 0.1),
     'L0_ffn_b1': (0.0, 0.357),
     'L0_ffn_b2': (0.0, 0.1)}
    factors = {}
    for name, (base, spread) in spreads.items():
        noise = np.random.default_rng([zlib.crc32(name.encode()), seed]).standard_normal(out[name].shape)
        drawn = base * np.exp(spread * noise) if base else spread * noise
        out[name] = jnp.asarray(drawn.astype(out[name].dtype))
    for name, factor in factors.items():
        out[name] = (out[name] * factor).astype(out[name].dtype)
    return out
```

```python
from contextlib import ExitStack

import numpy as np

import concourse.bass as bass
from concourse import mybir

ALU = mybir.AluOpType
ACT = mybir.ActivationFunctionType
AX = mybir.AxisListType
F32 = mybir.dt.float32
F32R = mybir.dt.float32r
F16 = mybir.dt.float16
ds = bass.ds

IMAGES, C, H, W = 2, 256, 96, 96
CC = C // 128
PIX = H * W
TOKENS = IMAGES * PIX
DILS = (1, 4, 8, 12)
NB = len(DILS)
PAD = max(DILS)
ROWS = H + 2 * PAD
TAPS = 9
GCOL = 3 * NB * 3 * TAPS
HCOL = NB * 3 * TAPS
FCOL = NB * TAPS
R = 4
T = R * W
GROUPS = H // R
R2 = 12
BATCHES = H // R2
SCALE = 1024.0
LN1_EPS, LN2_EPS, GN_EPS = 1e-6, 1e-5, 1e-5
GN_GROUPS = 32
E = 8
TC = 512
TT = TC // 128
CGROUPS = PIX // TC
TILES = TOKENS // 128
BIG = 1e30


def shape_constants():
    x = np.arange(W)
    shift = np.zeros((W, 1 + 2 * NB, W), np.float32)
    shift[:, 0] = np.eye(W)
    for b, d in enumerate(DILS):
        for n, j in enumerate((0, 2)):
            q = x + (j - 1) * d
            ok = (q >= 0) & (q < W)
            shift[q[ok], 1 + 2 * b + n, x[ok]] = 1
    colour = np.stack([(x // d) % 3 for d in DILS])
    rot = np.zeros((W, 3, NB, 3, 3), np.float32)
    for j in range(3):
        for b in range(NB):
            rot[x, j, b, :, (colour[b] + j - 1) % 3] = 1
    sel = np.zeros((2, NB, 3, 3, NB, 3, 2, W), np.float16)
    for p in range(2):
        for b in range(NB):
            for i in range(3):
                for k in range(3):
                    sel[p, b, i, k, b, i, p] = colour[b] == k
    band = np.zeros((W, NB, W), np.float32)
    for b, d in enumerate(DILS):
        band[:, b] = np.isin(x[:, None] - x[None, :], (-d, 0, d))
    g = np.arange(128) // (C // GN_GROUPS)
    same = (g[:, None] == g[None, :]).astype(np.float32) / (C // GN_GROUPS)
    return {
        "k_ident": np.eye(128, dtype=np.float32),
        "k_ident16": np.stack([np.eye(W), SCALE * np.eye(W)], 1).astype(np.float16),
        "k_shift": shift,
        "k_rot": rot.reshape(W, 3, FCOL),
        "k_sel": sel.reshape(2 * FCOL, NB * 3 * 2, W),
        "k_band": band.astype(np.float16),
        "k_same": same,
        "k_order": np.tile(np.arange(E, 0, -1, dtype=np.float32), (128, 1)),
    }



def build(nc, a):
    with ExitStack() as ctx:
        def sbuf(on, name, shape, dt=F32):
            return on.enter_context(nc.sbuf_tensor(name, shape, dt))

        def psum(on, name, shape, dt=F32):
            return on.enter_context(nc.psum_tensor(name, shape, dt))

        def sem(name):
            return ctx.enter_context(nc.semaphore(name))

        def sems(names):
            return [sem(n) for n in names.split()]

        y_dram = nc.dram_tensor("y_scratch", [IMAGES, 128, CC, PIX], F32).ap()
        res_dram = nc.dram_tensor("res_scratch", [TOKENS // TC, 128, TT, C], F32).ap()
        ln_dram = nc.dram_tensor("ln_scratch", [TOKENS // TC, 128, CC, TC], F32).ap()
        wg_dram = nc.dram_tensor("wg_scratch", [2, 128, CC * GCOL], F32).ap()
        wp_dram = nc.dram_tensor("wp_scratch", [2, 128, 5 * CC * C], F32).ap()
        x_dram = a["x"].rearrange("m (cc p) h w -> m p cc (h w)", p=128)
        out_dram = a["out"].rearrange("m (cc p) h w -> m p cc (h w)", p=128)

        ident = sbuf(ctx, "ident", [128, 128])
        eps = sbuf(ctx, "eps", [128, 3])
        gn_par = sbuf(ctx, "gn_par", [128, 3, CC])
        gn_stat = sbuf(ctx, "gn_stat", [128, IMAGES * CC, GROUPS * 6])
        gn_scale = sbuf(ctx, "gn_scale", [128, IMAGES * CC])
        gn_bias = sbuf(ctx, "gn_bias", [128, IMAGES * CC])
        stats = sbuf(ctx, "stats", [128, 2, 4, 6])
        mv = sbuf(ctx, "mv", [128, 2, 4, 2])
        std = sbuf(ctx, "std", [128, 2, 4])
        rstd = sbuf(ctx, "rstd", [128, 2, 4])
        nmr = sbuf(ctx, "nmr", [128, 2, 4])

        conv = ExitStack()
        rows16 = sbuf(conv, "rows16", [W, H, 2, C], F16)
        ident16 = sbuf(conv, "ident16", [W, 2, W], F16)
        shift = sbuf(conv, "shift", [W, 1 + 2 * NB, W])
        rot = sbuf(conv, "rot", [W, 3, FCOL])
        sel = sbuf(conv, "sel", [2 * FCOL, NB * 3 * 2, W], F16)
        band = sbuf(conv, "band", [W, NB, W], F16)
        filt_t = sbuf(conv, "filt_t", [2 * FCOL, PIX], F16)
        with ExitStack() as r0:
            wg_stage = sbuf(r0, "wg_stage", [128, CC * GCOL])
            wp_stage = sbuf(r0, "wp_stage", [128, 5 * CC * C])
            wg_split = sbuf(r0, "wg_split", [128, 2, CC * GCOL], F32R)
            wp_split = sbuf(r0, "wp_split", [128, 2, 5 * CC * C], F32R)
        with ExitStack() as r1:
            taps = sbuf(r1, "taps", [W, ROWS, NB, 3, TAPS])
            with ExitStack() as r2:
                x_in = sbuf(r2, "x_in", [128, 2, CC, T])
                xn = sbuf(r2, "xn", [W, 2, R, C])
                xc_hi = sbuf(r2, "xc_hi", [128, CC, T], F32R)
                xc_lo = sbuf(r2, "xc_lo", [128, CC, T], F32R)
                wg = sbuf(r2, "wg", [128, 2, CC, GCOL], F32R)
                g_rows = sbuf(r2, "g_rows", [W, R, 3, NB, 3 * TAPS])
            with ExitStack() as r2:
                fa = sbuf(r2, "fa", [W, R2 * FCOL])
                fb = sbuf(r2, "fb", [W, R2 * FCOL])
                fr = sbuf(r2, "fr", [W, 3, R2 * FCOL])
                f16 = sbuf(r2, "f16", [W, R2, 2, FCOL], F16)
                fred = sbuf(r2, "fred", [W, 3, R2 * NB])
        with ExitStack() as r1:
            wp = sbuf(r1, "wp", [128, 2, 5 * CC, C], F32R)
            bands = sbuf(r1, "bands", [W, 2, 2, 3, T], F16)
            cat_hi = sbuf(r1, "cat_hi", [128, 2, CC, T], F32R)
            cat_lo = sbuf(r1, "cat_lo", [128, 2, CC, T], F32R)
            y_out = sbuf(r1, "y_out", [128, 2, CC, T])
        conv.close()

        logits = sbuf(ctx, "logits", [128, TILES, E])
        comb = sbuf(ctx, "comb", [128, TILES, E])
        with ExitStack() as r1:
            c_x = sbuf(r1, "c_x", [128, 2, CC, TC])
            c_y = sbuf(r1, "c_y", [128, 2, CC, TC])
            c_ln = sbuf(r1, "c_ln", [128, 2, TT, C])
            c_lnt = sbuf(r1, "c_lnt", [128, 2, CC, TC])
            c_res = sbuf(r1, "c_res", [128, 2, TT, C])
            same = sbuf(r1, "same", [128, 128])
            gn_mv = sbuf(r1, "gn_mv", [128, IMAGES * CC, 2])
            gn_tmp = sbuf(r1, "gn_tmp", [128, 6, IMAGES * CC])
            router = sbuf(r1, "router", [128, CC, E])
            t2 = sbuf(r1, "t2", [128, 4, TILES, E])
            m2 = sbuf(r1, "m2", [128, 4, TILES])
            order = sbuf(r1, "order", [128, E])
        w1 = sbuf(ctx, "w1", [128, 2, E, CC, C], F32R)
        w2 = sbuf(ctx, "w2", [128, 2, E, CC, C], F32R)
        w_stage = sbuf(ctx, "w_stage", [128, 2, E * CC * C])
        b1 = sbuf(ctx, "b1", [128, E * CC])
        b2 = sbuf(ctx, "b2", [E, C])
        m_x = sbuf(ctx, "m_x", [128, 2, CC, TC])
        m_hi = sbuf(ctx, "m_hi", [128, CC, TC], F32R)
        m_lo = sbuf(ctx, "m_lo", [128, CC, TC], F32R)
        m_acc = sbuf(ctx, "m_acc", [128, 2, TT, C])
        m_cw = sbuf(ctx, "m_cw", [128, TT, E])
        m_cwt = sbuf(ctx, "m_cwt", [E, TC])
        h_full = sbuf(ctx, "h_full", [128, 2, TC])
        h_hi = sbuf(ctx, "h_hi", [128, 2, CC, TC], F32R)
        h_lo = sbuf(ctx, "h_lo", [128, 2, CC, TC], F32R)
        m_out = sbuf(ctx, "m_out", [128, CC, TC])

        with ExitStack() as r1:
            ps_tok = psum(r1, "ps_tok", [128, 2, R, C])
            ps_ch = psum(r1, "ps_ch", [128, CC, 512])
            ps_g = psum(r1, "ps_g", [128, 2, 512])
        with ExitStack() as r1:
            ps_f = psum(r1, "ps_f", [128, 512])
            ps_ft = psum(r1, "ps_ft", [128, 2, 1024], F16)
        with ExitStack() as r1:
            ps_b = psum(r1, "ps_b", [128, 4, 512])
            ps_o = psum(r1, "ps_o", [128, CC, 512])
            ps_y = psum(r1, "ps_y", [128, CC, 512])
        with ExitStack() as r1:
            ps_ct = psum(r1, "ps_ct", [128, 2, TT, C])
            ps_cc = psum(r1, "ps_cc", [128, CC, TC])
            ps_r = psum(r1, "ps_r", [128, 512])
            ps_gn = psum(r1, "ps_gn", [128, 512])
        with ExitStack() as r1:
            ps_h = psum(r1, "ps_h", [128, 4, TC])
            ps_e = psum(r1, "ps_e", [128, TT, C])
            ps_t = psum(r1, "ps_t", [128, CC, TC])

        consts_in, phase_left, phase_entered = sems("consts_in phase_left phase_entered")
        w_loaded, w_hi_done, w_lo_done, w_stored = sems("w_loaded w_hi_done w_lo_done w_stored")
        x_loaded = sems("x_loaded0 x_loaded1")
        tok_ready, mv_done, std_done, rstd_done, nmr_done = sems(
            "tok_ready mv_done std_done rstd_done nmr_done")
        xn_done, rows_hi_done, ch_ready, xc_hi_done, xc_lo_done = sems(
            "xn_done rows_hi_done ch_ready xc_hi_done xc_lo_done")
        g_ready, g_copied, taps_centre, taps_near, taps_added = sems(
            "g_ready g_copied taps_centre taps_near taps_added")
        wg_loaded, wp_loaded = sems("wg_loaded wp_loaded")
        f_ready, f_dve, f_sub, f_exp, f_hi_done, f_split, ft_ready, ft_copied = sems(
            "f_ready f_dve f_sub f_exp f_hi_done f_split ft_ready ft_copied")
        bc_ready, masked, out_ready, cat_hi_done, cat_done = sems("bc_ready masked out_ready cat_hi_done cat_done")
        proj_done, y_done, y_seen = sems("proj_done y_done y_seen")
        y_stored = sems("y_stored0 y_stored1")
        gn_dve, gn_act, gn_pe, gn_late = sems("gn_dve gn_act gn_pe gn_late")
        c_loaded = sems("c_loaded0 c_loaded1")
        c_relu, c_x1, c_tok, c_mv, c_std, c_rstd, c_nmr, c_lnd = sems(
            "c_relu c_x1 c_tok c_mv c_std c_rstd c_nmr c_lnd")
        c_resd, c_cht, c_lntd, c_routed, c_logits = sems("c_resd c_cht c_lntd c_routed c_logits")
        c_stored = sems("c_stored0 c_stored1")
        top_dve, top_exp = sems("top_dve top_exp")
        m_loaded = sems("m_loaded0 m_loaded1")
        m_hi_done, m_lo_done, cw_done, cwt_ready, cwt_done = sems("m_hi_done m_lo_done cw_done cwt_ready cwt_done")
        h_ready, h_full_done, h_hi_done, h_lo_done = sems("h_ready h_full_done h_hi_done h_lo_done")
        e_ready, e_added, o_ready, o_copied, o_stored = sems("e_ready e_added o_ready o_copied o_stored")

        N_ENG = 5
        sync = nc.sync

        def leave(eng):
            if eng is sync:
                eng.sem_inc(phase_left, 1)
            else:
                eng.drain().then_inc(phase_left, 1)

        def enter(eng, phases):
            eng.wait_ge(phase_left, phases)
            eng.sem_inc(phase_entered, 1)

        def at_value(eng, x):
            return x if isinstance(x, int) else eng.snap(x)

        def three_passes(eng, out, lhs, rhs, start, stop):
            for n, (p, q) in enumerate(((0, 0), (0, 1), (1, 0))):
                mm = eng.matmul(out, lhs[p], rhs[q], start=start and n == 0, stop=stop and n == 2)
            return mm

        N_CONST = 11
        C_ALL = IMAGES * CGROUPS
        MASKS = GROUPS * NB * 6
        STEPS = GROUPS * (NB + 1)
        CATS = STEPS * CC
        UNSCALE = 1.0 / (SCALE * SCALE)
        TOP_EXP = 2
        counted = [
            bc_ready, c_cht, c_lnd, c_lntd, c_logits, c_mv, c_nmr, c_relu, c_resd, c_routed, c_rstd, c_std, c_tok,
            c_x1, cat_done, cat_hi_done, ch_ready, cw_done, cwt_done, cwt_ready, e_added, e_ready, f_dve, f_exp,
            f_hi_done, f_ready, f_split, f_sub, ft_copied, ft_ready, g_copied, g_ready, h_hi_done, h_lo_done,
            h_ready, m_hi_done, m_lo_done, masked, mv_done, nmr_done, o_copied, o_ready, o_stored, out_ready,
            proj_done, rows_hi_done, rstd_done, std_done, taps_added, taps_centre, taps_near, tok_ready, wg_loaded,
            wp_loaded, xc_hi_done, xc_lo_done, xn_done, y_done, y_seen, *c_loaded, *c_stored, *m_loaded, *x_loaded,
            *y_stored,
        ]

        def wait(eng, signal, count):
            eng.wait_ge(signal, count + 1)

        block = ctx.enter_context(nc.Block())

        @block.sync
        def _(sp):
            for signal in counted:
                sp.sem_inc(signal, 1)
            for dst, src in ((ident[:], a["k_ident"]), (ident16[:], a["k_ident16"]), (shift[:], a["k_shift"]),
                             (rot[:], a["k_rot"]), (sel[:], a["k_sel"]), (band[:], a["k_band"]),
                             (gn_par[:, 0], a["b_proj"]), (gn_par[:, 1], a["gamma"]), (gn_par[:, 2], a["beta"])):
                sp.dma_start(dst, src).then_inc(consts_in, 16)
            sp.dma_start(wg_stage[:], a["w_gen"]).then_inc(consts_in, 16)
            sp.dma_start(wp_stage[:], a["w_proj"]).then_inc(consts_in, 16)
            sp.wait_ge(w_hi_done, 2)
            sp.wait_ge(w_lo_done, 2)
            for p in range(2):
                sp.dma_start(wg_dram[p], wg_split[:, p].bitcast(F32)).then_inc(w_stored, 16)
                sp.dma_start(wp_dram[p], wp_split[:, p].bitcast(F32)).then_inc(w_stored, 16)
            sp.wait_ge(w_stored, 64)
            leave(sp)

            with sp.Fori(0, IMAGES) as m:
                enter(sp, m * (3 * N_ENG) + N_ENG)
                for p in range(2):
                    sp.dma_start(wg[:, p].rearrange("p a g -> p (a g)").bitcast(F32), wg_dram[p]).then_inc(wg_loaded, 16)
                with sp.Fori(0, GROUPS // 2) as t:
                    for u in range(2):
                        off = sp.snap(t * (2 * T) + u * T)
                        img = sp.snap(m)
                        count = sp.snap(m * GROUPS + t * 2 + (u + 1))
                        wait(sp, tok_ready, count)
                        sp.dma_start(x_in[:, u], x_dram[img, :, :, ds(off, T)]).then_inc(x_loaded[u], 16)
                leave(sp)
                enter(sp, m * (3 * N_ENG) + 2 * N_ENG)
                leave(sp)
                enter(sp, m * (3 * N_ENG) + 3 * N_ENG)
                for p in range(2):
                    sp.dma_start(wp[:, p].rearrange("p a g -> p (a g)").bitcast(F32), wp_dram[p]).then_inc(wp_loaded, 16)
                with sp.Fori(0, GROUPS // 2) as t:
                    for u in range(2):
                        off = sp.snap(t * (2 * T) + u * T)
                        img = sp.snap(m)
                        count = sp.snap(m * GROUPS + t * 2 + (u + 1))
                        wait(sp, y_done, count)
                        sp.dma_start(y_dram[img, :, :, ds(off, T)], y_out[:, u]).then_inc(y_stored[u], 16)
                for u in range(2):
                    wait(sp, y_stored[u], m * (8 * GROUPS) + 8 * GROUPS)
                leave(sp)

            enter(sp, 7 * N_ENG)
            for dst, src in ((same[:], a["k_same"]), (router[:], a["router"]), (order[:], a["k_order"])):
                sp.dma_start(dst, src).then_inc(consts_in, 16)

            def load(m, t, u):
                off, img = at_value(sp, t * (2 * TC) + u * TC), at_value(sp, m)
                wait(sp, c_tok, m * CGROUPS + t * 2 + (u + 1))
                sp.dma_start(c_x[:, u], x_dram[img, :, :, ds(off, TC)]).then_inc(c_loaded[u], 16)
                sp.dma_start(c_y[:, u], y_dram[img, :, :, ds(off, TC)]).then_inc(c_loaded[u], 16)

            def store(t, u):
                grp = at_value(sp, t * 2 + u)
                wait(sp, c_resd, t * 2 + (u + 1))
                sp.dma_start(res_dram[grp], c_res[:, u]).then_inc(c_stored[u], 16)
                wait(sp, c_lntd, t * 2 + (u + 1))
                sp.dma_start(ln_dram[grp], c_lnt[:, u]).then_inc(c_stored[u], 16)

            for m in range(IMAGES):
                if m:
                    for u in range(2):
                        load(m, 0, u)
                        store(m * (CGROUPS // 2) - 1, u)
                else:
                    for u in range(2):
                        load(0, 0, u)
                with sp.Fori(1, CGROUPS // 2) as t:
                    for u in range(2):
                        load(m, t, u)
                        store(t + (m * (CGROUPS // 2) - 1), u)
            for u in range(2):
                store(C_ALL // 2 - 1, u)
            for u in range(2):
                wait(sp, c_stored[u], 32 * (C_ALL // 2))
            leave(sp)

            enter(sp, 8 * N_ENG)
            sp.dma_start(w_stage[:, 0], a["w1"]).then_inc(w_loaded, 16)
            sp.dma_start(w_stage[:, 1], a["w2"]).then_inc(w_loaded, 16)
            sp.dma_start(b1[:], a["b1"]).then_inc(w_loaded, 16)
            sp.dma_start(b2[:], a["b2"]).then_inc(w_loaded, 16)
            with sp.Fori(0, C_ALL // 2) as t:
                for u in range(2):
                    grp = sp.snap(t * 2 + u)
                    count = sp.snap(t * 2 + (u + 1))
                    wait(sp, o_ready, count)
                    sp.dma_start(m_x[:, u], ln_dram[grp]).then_inc(m_loaded[u], 16)
                    sp.dma_start(m_acc[:, u], res_dram[grp]).then_inc(m_loaded[u], 16)

        @block.tensor
        def _(pe):
            pe.wait_ge(consts_in, 16 * N_CONST)
            pe.sem_inc(tok_ready, 2)
            pe.sem_inc(proj_done, 2)
            pe.sem_inc(c_tok, 2)
            pe.sem_inc(o_ready, 2)
            leave(pe)
            with pe.Fori(0, IMAGES) as m:
                wait(pe, wg_loaded, m * 32 + 32)
                enter(pe, m * (3 * N_ENG) + N_ENG)
                with pe.Fori(0, GROUPS // 2) as t:
                    for u in range(2):
                        wait(pe, x_loaded[u], m * (8 * GROUPS) + t * 16 + 16)
                        for r in range(R):
                            for c in range(CC):
                                mm = pe.transpose(ps_tok[0:W, u, r, c * 128:(c + 1) * 128],
                                                  x_in[:, u, c, r * W:(r + 1) * W], ident[:])
                        mm.then_inc(tok_ready, 1)
                    for u in range(2):
                        n = m * GROUPS + t * 2 + u
                        wait(pe, xn_done, n + 1)
                        wait(pe, xc_lo_done, n)
                        for r in range(R):
                            for c in range(CC):
                                mm = pe.transpose(ps_ch[:, c, r * W:(r + 1) * W],
                                                  xn[:, u, r, c * 128:(c + 1) * 128], ident[0:W, 0:W])
                        mm.then_inc(ch_ready, 1)
                        wait(pe, xc_lo_done, n + 1)
                        for r in range(R):
                            wait(pe, g_copied, (n * R) + (r + 1))
                            for c in range(CC):
                                mm = three_passes(pe, ps_g[0:W, r % 2, 0:GCOL],
                                                  [z[:, c, r * W:(r + 1) * W] for z in (xc_hi, xc_lo)],
                                                  [wg[:, p, c] for p in range(2)], c == 0, c == CC - 1)
                            mm.then_inc(g_ready, 1)
                leave(pe)
                enter(pe, m * (3 * N_ENG) + 2 * N_ENG)
                with pe.Fori(0, BATCHES) as k:
                    n = m * BATCHES + k
                    row = pe.snap(k * R2 + PAD)
                    out = ps_f[0:W, 0:R2 * FCOL].rearrange("p (r b k) -> p r b k", r=R2, b=NB)
                    wait(pe, f_split, n)
                    for b in range(NB):
                        for s, j in enumerate((0, 2)):
                            pe.matmul(out[:, :, b, :], shift[:, 1 + 2 * b + s], taps[:, ds(row, R2), b, j, :],
                                      start=(b == 0 and s == 0), stop=False, skip_group_check=True)
                    mm = pe.matmul(out, shift[:, 0], taps[:, ds(row, R2), :, 1, :], start=False, stop=True,
                                   skip_group_check=True)
                    mm.then_inc(f_ready, 1)
                    wait(pe, f_split, n + 1)
                    wait(pe, ft_copied, n)
                    for r in range(R2):
                        mm = pe.transpose(ps_ft[0:2 * FCOL, r // 6, (r % 6) * W:(r % 6 + 1) * W],
                                          f16[:, r].rearrange("p a f -> p (a f)"), ident16[:, 0])
                    mm.then_inc(ft_ready, 1)
                leave(pe)
                enter(pe, m * (3 * N_ENG) + 3 * N_ENG)
                wait(pe, wp_loaded, m * 32 + 32)

                def broadcast(g, b):
                    for i in range(3):
                        for p in range(2):
                            k = (g * NB + b) * 6 + i * 2 + p
                            wait(pe, masked, m * MASKS + (k + 1))
                            pe.matmul(ps_b[0:W, k % 4, 0:T], sel[:, (b * 3 + i) * 2 + p], filt_t[:, g * T:(g + 1) * T],
                                      start=True, stop=True).then_inc(bc_ready, 1)

                def branch(g, b):
                    if b < NB:
                        wait(pe, masked, m * MASKS + ((g * NB + b) * 6 + 6 + 4))
                    for c in range(CC):
                        k = (g * (NB + 1) + b) * 2 + c
                        wait(pe, cat_done, m * CATS + (k + 1))
                        for r in range(R):
                            y = g * R + r
                            if b == NB:
                                todo = [(y, p, ident16[:, 1]) for p in range(2)]
                            else:
                                todo = [(y + (i - 1) * DILS[b], p, bands[:, b % 2, q, i, r * W:(r + 1) * W])
                                        for i in range(3) for p, q in ((0, 0), (0, 1), (1, 0))
                                        if 0 <= y + (i - 1) * DILS[b] < H]
                            for n, (src, p, rhs) in enumerate(todo):
                                mm = pe.matmul(ps_o[:, c, r * W:(r + 1) * W], rows16[:, src, p, c * 128:(c + 1) * 128],
                                               rhs, start=n == 0, stop=n == len(todo) - 1)
                        mm.then_inc(out_ready, 1)

                def project(g, b):
                    s = g * (NB + 1) + b
                    wait(pe, cat_done, m * CATS + (2 * s + 4))
                    if b == 0:
                        wait(pe, y_done, m * GROUPS + g)
                    blk = (b + 1) % (NB + 1)
                    for o in range(CC):
                        for c in range(CC):
                            mm = three_passes(pe, ps_y[:, o, 0:T],
                                              [wp[:, p, blk * CC + c, o * 128:(o + 1) * 128] for p in range(2)],
                                              [z[:, s % 2, c] for z in (cat_hi, cat_lo)],
                                              b == 0 and c == 0, b == NB and c == CC - 1)
                    mm.then_inc(proj_done, 1)

                broadcast(0, 0)
                for g in range(GROUPS):
                    for b in range(NB):
                        if b + 1 < NB:
                            broadcast(g, b + 1)
                        branch(g, b)
                        if b:
                            project(g, b - 1)
                    branch(g, NB)
                    if g + 1 < GROUPS:
                        broadcast(g + 1, 0)
                    project(g, NB - 1)
                    project(g, NB)
                leave(pe)

            enter(pe, 7 * N_ENG)
            pe.wait_ge(consts_in, 16 * (N_CONST + 3))
            pe.wait_ge(gn_dve, 1)
            pe.matmul(ps_gn[:, 0:4], same[:], gn_mv[:, :, 0], start=True, stop=True).then_inc(gn_pe, 1)
            pe.wait_ge(gn_dve, 4)
            pe.matmul(ps_gn[:, 4:8], same[:], gn_tmp[:, 2], start=True, stop=True).then_inc(gn_pe, 1)
            with pe.Fori(0, C_ALL // 2) as t:
                for u in range(2):
                    wait(pe, c_x1, t * 2 + (u + 1))
                    wait(pe, c_resd, t * 2)
                    for k in range(TT):
                        for c in range(CC):
                            mm = pe.transpose(ps_ct[:, u, k, c * 128:(c + 1) * 128],
                                              c_x[:, u, c, k * 128:(k + 1) * 128], ident[:])
                    mm.then_inc(c_tok, 1)
                for u in range(2):
                    n = t * 2 + u
                    wait(pe, c_lnd, n + 1)
                    wait(pe, c_lntd, n)
                    for k in range(TT):
                        for c in range(CC):
                            mm = pe.transpose(ps_cc[:, c, k * 128:(k + 1) * 128],
                                              c_ln[:, u, k, c * 128:(c + 1) * 128], ident[:])
                    mm.then_inc(c_cht, 1)
                    wait(pe, c_lntd, n + 1)
                    wait(pe, c_logits, n)
                    for k in range(TT):
                        for c in range(CC):
                            mm = pe.matmul(ps_r[:, k * E:(k + 1) * E], c_lnt[:, u, c, k * 128:(k + 1) * 128],
                                           router[:, c], start=c == 0, stop=c == CC - 1)
                    mm.then_inc(c_routed, 1)
            leave(pe)

            enter(pe, 8 * N_ENG)
            pe.wait_ge(w_lo_done, 4)
            with pe.Fori(0, C_ALL // 2) as t:
                for u in range(2):
                    n = t * 2 + u
                    wait(pe, cw_done, n + 1)
                    wait(pe, o_copied, n)
                    for k in range(TT):
                        mm = pe.transpose(ps_t[0:E, 0, k * 128:(k + 1) * 128], m_cw[:, k], ident[:])
                    mm.then_inc(cwt_ready, 1)
                    wait(pe, m_lo_done, n + 1)

                    def hidden(e):
                        for f in range(CC):
                            k = e * CC + f
                            wait(pe, h_hi_done, n * (E * CC) + (k + 1))
                            for c in range(CC):
                                mm = three_passes(pe, ps_h[:, k % 4],
                                                  [w1[:, p, e, c, f * 128:(f + 1) * 128] for p in range(2)],
                                                  [m_hi[:, c], m_lo[:, c]], c == 0, c == CC - 1)
                            mm.then_inc(h_ready, 1)

                    def outer(e):
                        if e >= 0:
                            wait(pe, h_lo_done, n * (E * CC) + (e * CC + 4))
                        for k in range(TT):
                            if k % 2 == 0:
                                wait(pe, e_added, n * (TT * (E + 1)) + ((e + 1) * TT + k + 2))
                            if e < 0:
                                mm = pe.matmul(ps_e[:, k], m_cwt[:, k * 128:(k + 1) * 128], b2[:], start=True, stop=True)
                            else:
                                for f in range(CC):
                                    mm = three_passes(pe, ps_e[:, k],
                                                      [z[:, e % 2, f, k * 128:(k + 1) * 128] for z in (h_hi, h_lo)],
                                                      [w2[:, p, e, f] for p in range(2)], f == 0, f == CC - 1)
                            if k % 2:
                                mm.then_inc(e_ready, 2)

                    hidden(0)
                    wait(pe, cwt_done, n + 1)
                    outer(-1)
                    for e in range(E):
                        if e + 1 < E:
                            hidden(e + 1)
                        outer(e)
                    wait(pe, e_added, n * (TT * (E + 1)) + (TT * (E + 1) + TT))
                    for k in range(TT):
                        for c in range(CC):
                            mm = pe.transpose(ps_t[:, c, k * 128:(k + 1) * 128],
                                              m_acc[:, u, k, c * 128:(c + 1) * 128], ident[:])
                    mm.then_inc(o_ready, 1)

        @block.scalar
        def _(act):
            act.sem_inc(g_copied, 2)
            act.sem_inc(h_hi_done, 4)
            act.wait_ge(consts_in, 16 * N_CONST)
            act.activation(wg_split[:, 0], wg_stage[:], ACT.Copy).then_inc(w_hi_done, 1)
            act.activation(wp_split[:, 0], wp_stage[:], ACT.Copy).then_inc(w_hi_done, 1)
            leave(act)
            with act.Fori(0, IMAGES) as m:
                enter(act, m * (3 * N_ENG) + N_ENG)
                with act.Fori(0, GROUPS // 2) as t:
                    for u in range(2):
                        n = m * GROUPS + t * 2 + u
                        wait(act, mv_done, n + 1)
                        act.activation(std[0:W, u], mv[0:W, u, :, 1], ACT.Sqrt, bias=eps[0:W, 0:1]).then_inc(std_done, 1)
                    for u in range(2):
                        n = m * GROUPS + t * 2 + u
                        wait(act, nmr_done, n + 1)
                        for r in range(R):
                            last = act.activation(xn[:, u, r], ps_tok[0:W, u, r], ACT.Identity,
                                                  bias=nmr[0:W, u, r:r + 1], scale=rstd[0:W, u, r:r + 1])
                        last.then_inc(xn_done, 1)
                    for u in range(2):
                        n = m * GROUPS + t * 2 + u
                        wait(act, ch_ready, n + 1)
                        act.activation(xc_hi[:], ps_ch[:, :, 0:T], ACT.Copy).then_inc(xc_hi_done, 1)
                        wait(act, taps_added, n)
                        for r in range(R):
                            wait(act, g_ready, n * R + (r + 1))
                            act.activation(g_rows[:, r].rearrange("p i b k -> p (i b k)"),
                                           ps_g[0:W, r % 2, 0:GCOL], ACT.Copy).then_inc(g_copied, 1)
                leave(act)
                enter(act, m * (3 * N_ENG) + 2 * N_ENG)
                with act.Fori(0, BATCHES) as k:
                    n = m * BATCHES + k
                    col = act.snap(k * (R2 * W))
                    col2 = act.snap(k * (R2 * W) + R2 * W // 2)
                    wait(act, f_sub, n + 1)
                    act.activation(fb[:], fa[:], ACT.Exp).then_inc(f_exp, 1)
                    wait(act, ft_ready, n + 1)
                    act.activation(filt_t[:, ds(col, R2 * W // 2)], ps_ft[0:2 * FCOL, 0, 0:R2 * W // 2], ACT.Copy)
                    act.activation(filt_t[:, ds(col2, R2 * W // 2)], ps_ft[0:2 * FCOL, 1, 0:R2 * W // 2],
                                   ACT.Copy).then_inc(ft_copied, 1)
                leave(act)
                enter(act, m * (3 * N_ENG) + 3 * N_ENG)
                with act.Fori(0, GROUPS // 2) as t:
                    for u in range(2):
                        for b in range(NB + 1):
                            s = u * (NB + 1) + b
                            wait(act, proj_done, m * STEPS + t * (2 * NB + 2) + (s + 1))
                            for c in range(CC):
                                wait(act, out_ready, m * CATS + t * (4 * NB + 4) + (2 * s + c + 1))
                                act.activation(cat_hi[:, s % 2, c], ps_o[:, c, 0:T], ACT.Copy,
                                               scale=UNSCALE).then_inc(cat_hi_done, 1)
                        wait(act, proj_done, m * STEPS + t * (2 * NB + 2) + ((u + 1) * (NB + 1) + 2))
                        wait(act, y_stored[u], m * (8 * GROUPS) + t * 16)
                        wait(act, y_seen, m * GROUPS + t * 2 + (u + 1))
                        for o in range(CC):
                            last = act.activation(y_out[:, u, o], ps_y[:, o, 0:T], ACT.Identity,
                                                  bias=gn_par[:, 0, o:o + 1])
                        last.then_inc(y_done, 1)
                leave(act)

            enter(act, 7 * N_ENG)
            act.wait_ge(gn_dve, 5)
            act.activation(gn_tmp[:, 4], gn_tmp[:, 3], ACT.Sqrt, bias=eps[:, 2:3]).then_inc(gn_act, 1)
            act.wait_ge(gn_dve, 8)
            for m in range(IMAGES):
                with act.Fori(0, CGROUPS // 2) as t:
                    for u in range(2):
                        wait(act, c_loaded[u], m * (16 * CGROUPS) + t * 32 + 32)
                        for c in range(CC):
                            at = m * CC + c
                            last = act.activation(c_y[:, u, c], c_y[:, u, c], ACT.Relu,
                                                  bias=gn_bias[:, at:at + 1], scale=gn_scale[:, at:at + 1])
                        last.then_inc(c_relu, 1)
                    for u in range(2):
                        n = m * CGROUPS + t * 2 + u
                        wait(act, c_mv, n + 1)
                        act.activation(std[:, u], mv[:, u, :, 1], ACT.Sqrt, bias=eps[:, 1:2]).then_inc(c_std, 1)
                    for u in range(2):
                        n = m * CGROUPS + t * 2 + u
                        wait(act, c_nmr, n + 1)
                        for k in range(TT):
                            last = act.activation(c_ln[:, u, k], ps_ct[:, u, k], ACT.Identity,
                                                  bias=nmr[:, u, k:k + 1], scale=rstd[:, u, k:k + 1])
                        last.then_inc(c_lnd, 1)
                    for u in range(2):
                        n = m * CGROUPS + t * 2 + u
                        wait(act, c_cht, n + 1)
                        wait(act, c_stored[u], m * (16 * CGROUPS) + t * 32)
                        act.activation(c_lnt[:, u], ps_cc[:], ACT.Copy).then_inc(c_lntd, 1)
            act.wait_ge(top_dve, TOP_EXP)
            act.activation(t2[:, 1], t2[:, 0], ACT.Exp).then_inc(top_exp, 1)
            leave(act)

            enter(act, 8 * N_ENG)
            act.wait_ge(w_loaded, 64)
            for k, w in enumerate((w1, w2)):
                act.activation(w[:, 0].rearrange("p e c f -> p (e c f)"), w_stage[:, k], ACT.Copy).then_inc(w_hi_done, 1)
            with act.Fori(0, IMAGES) as m:
                with act.Fori(0, CGROUPS // 2) as t:
                    for u in range(2):
                        n = m * CGROUPS + t * 2 + u
                        off = act.snap(t * (2 * TC) + u * TC)
                        img = act.snap(m)
                        wait(act, m_loaded[u], m * (16 * CGROUPS) + t * 32 + 32)
                        wait(act, h_ready, n * (E * CC))
                        act.activation(m_hi[:], m_x[:, u], ACT.Copy).then_inc(m_hi_done, 1)
                        wait(act, cwt_ready, n + 1)
                        act.activation(m_cwt[:], ps_t[0:E, 0], ACT.Copy).then_inc(cwt_done, 1)
                        for e in range(E):
                            for f in range(CC):
                                k = e * CC + f
                                wait(act, h_ready, n * (E * CC) + (k + 1))
                                wait(act, h_lo_done, n * (E * CC) + (k + 1))
                                act.activation(h_full[:, f], ps_h[:, k % 4], ACT.Gelu,
                                               bias=b1[:, k:k + 1]).then_inc(h_full_done, 1)
                                if f == 0:
                                    wait(act, e_ready, n * (TT * (E + 1)) + e * TT)
                                act.activation(h_hi[:, e % 2, f], ps_h[:, k % 4], ACT.Gelu,
                                               bias=b1[:, k:k + 1]).then_inc(h_hi_done, 1)
                        wait(act, o_ready, n + 3)
                        wait(act, o_stored, n * 16)
                        act.activation(m_out[:], ps_t[:], ACT.Copy).then_inc(o_copied, 1)
                        wait(act, o_copied, n + 1)
                        act.dma_start(out_dram[img, :, :, ds(off, TC)], m_out[:]).then_inc(o_stored, 16)
            wait(act, o_stored, 16 * C_ALL)

        @block.vector
        def _(dve):
            dve.memset(eps[:, 0:1], LN1_EPS)
            dve.memset(eps[:, 1:2], LN2_EPS)
            dve.memset(eps[:, 2:3], GN_EPS)
            dve.sem_inc(masked, 4)
            dve.sem_inc(cat_done, 2)
            dve.sem_inc(y_seen, 2)
            dve.sem_inc(h_lo_done, 2)
            dve.sem_inc(e_added, 4)
            for k, (stage, split) in enumerate(((wg_stage, wg_split), (wp_stage, wp_split))):
                dve.wait_ge(w_hi_done, k + 1)
                dve.tensor_tensor(split[:, 1], stage[:], split[:, 0].bitcast(F32), ALU.subtract).then_inc(w_lo_done, 1)
            leave(dve)
            with dve.Fori(0, IMAGES) as m:
                enter(dve, m * (3 * N_ENG) + N_ENG)
                with dve.Fori(0, GROUPS // 2) as t:
                    for u in range(2):
                        n = m * GROUPS + t * 2 + u
                        wait(dve, tok_ready, n + 3)
                        for r in range(R):
                            dve.bn_stats(stats[0:W, u, r], ps_tok[0:W, u, r])
                    dve.drain()
                    for u in range(2):
                        for r in range(R):
                            last = dve.bn_aggr(mv[0:W, u, r], stats[0:W, u, r])
                        last.then_inc(mv_done, 1)
                    for u in range(2):
                        n = m * GROUPS + t * 2 + u
                        wait(dve, std_done, n + 1)
                        dve.reciprocal(rstd[0:W, u], std[0:W, u]).then_inc(rstd_done, 1)
                    for u in range(2):
                        n = m * GROUPS + t * 2 + u
                        wait(dve, rstd_done, n + 1)
                        dve.scalar_tensor_tensor(out=nmr[0:W, u], in0=mv[0:W, u, :, 0], scalar=-1.0, in1=rstd[0:W, u],
                                                 op0=ALU.mult, op1=ALU.mult).then_inc(nmr_done, 1)
                    for u in range(2):
                        n = m * GROUPS + t * 2 + u
                        row = dve.snap(t * (2 * R) + u * R)
                        wait(dve, xn_done, n + 1)
                        dve.tensor_scalar(rows16[:, ds(row, R), 0, :], xn[:, u], SCALE, None,
                                          ALU.mult).then_inc(rows_hi_done, 1)
                        wait(dve, xc_hi_done, n + 1)
                        dve.tensor_tensor(xc_lo[:], ps_ch[:, :, 0:T], xc_hi[:].bitcast(F32),
                                          ALU.subtract).then_inc(xc_lo_done, 1)
                        wait(dve, rows_hi_done, n + 1)
                        for r in range(R):
                            at = dve.snap(t * (2 * R) + (u * R + r))
                            dve.scalar_tensor_tensor(out=rows16[:, ds(at, 1), 1, :], in0=xn[:, u, r:r + 1], scalar=SCALE,
                                                     in1=rows16[:, ds(at, 1), 0, :], op0=ALU.mult, op1=ALU.subtract)
                leave(dve)
                enter(dve, m * (3 * N_ENG) + 2 * N_ENG)
                nine = lambda z: z.rearrange("p (g k) -> p g k", k=TAPS)
                with dve.Fori(0, BATCHES) as k:
                    n = m * BATCHES + k
                    base = dve.snap(n * 7)
                    wait(dve, f_ready, n + 1)
                    logit = nine(ps_f[0:W, 0:R2 * FCOL])
                    dve.tensor_reduce(fred[:, 0], logit, AX.X, ALU.max).then_inc(f_dve, 1)
                    wait(dve, f_dve, base + 1)
                    dve.tensor_tensor(nine(fa[:]), logit, fred[:, 0].unsqueeze(2).broadcast_to([W, R2 * NB, TAPS]),
                                      ALU.subtract).then_inc(f_sub, 1)
                    wait(dve, f_exp, n + 1)
                    dve.tensor_reduce(fred[:, 1], nine(fb[:]), AX.X, ALU.add).then_inc(f_dve, 1)
                    wait(dve, f_dve, base + 2)
                    dve.reciprocal(fred[:, 2], fred[:, 1]).then_inc(f_dve, 1)
                    wait(dve, f_dve, base + 3)
                    dve.scalar_tensor_tensor(out=nine(fa[:]), in0=nine(fb[:]), scalar=SCALE,
                                             in1=fred[:, 2].unsqueeze(2).broadcast_to([W, R2 * NB, TAPS]),
                                             op0=ALU.mult, op1=ALU.mult).then_inc(f_dve, 1)
                    wait(dve, f_dve, base + 4)
                    for j in range(3):
                        tap = fa[:].rearrange("p (r g j) -> p r g j", r=R2, j=3)[:, :, :, j:j + 1]
                        last = dve.tensor_tensor(
                            fr[:, j].rearrange("p (r g j) -> p r g j", r=R2, j=3),
                            tap.broadcast_to([W, R2, NB * 3, 3]),
                            rot[:, j].rearrange("p (r g j) -> p r g j", r=1, j=3).broadcast_to([W, R2, NB * 3, 3]), ALU.mult)
                    last.then_inc(f_dve, 1)
                    wait(dve, f_dve, base + 5)
                    dve.tensor_tensor(fa[:], fr[:, 0], fr[:, 1], ALU.add).then_inc(f_dve, 1)
                    wait(dve, f_dve, base + 6)
                    dve.tensor_tensor(fb[:], fa[:], fr[:, 2], ALU.add).then_inc(f_dve, 1)
                    wait(dve, f_dve, base + 7)
                    flat = fb[:].rearrange("p (r f) -> p r f", r=R2)
                    dve.tensor_copy(f16[:, :, 0], flat).then_inc(f_hi_done, 1)
                    wait(dve, f_hi_done, n + 1)
                    dve.tensor_tensor(f16[:, :, 1], flat, f16[:, :, 0], ALU.subtract).then_inc(f_split, 1)
                leave(dve)
                enter(dve, m * (3 * N_ENG) + 3 * N_ENG)

                def mask(t, u, b):
                    k = (u * NB + b) * 6
                    s = u * (NB + 1) + b
                    prev = s - 2 if b >= 2 else s - 3
                    wait(dve, out_ready, m * CATS + t * (4 * NB + 4) + max(2 * prev + 2, 0))
                    for i in range(3):
                        for p in range(2):
                            n = k + i * 2 + p
                            wait(dve, bc_ready, m * MASKS + t * (12 * NB) + (n + 1))
                            dve.tensor_tensor(bands[:, b % 2, p, i].rearrange("p (r w) -> p r w", r=R),
                                              ps_b[0:W, n % 4, 0:T].rearrange("p (r w) -> p r w", r=R),
                                              band[:, b:b + 1].broadcast_to([W, R, W]), ALU.mult).then_inc(masked, 1)

                def split(t, u, b):
                    for c in range(CC):
                        s = u * (NB + 1) + b
                        wait(dve, cat_hi_done, m * CATS + t * (4 * NB + 4) + (2 * s + c + 1))
                        dve.scalar_tensor_tensor(out=cat_lo[:, s % 2, c], in0=ps_o[:, c, 0:T], scalar=UNSCALE,
                                                 in1=cat_hi[:, s % 2, c].bitcast(F32),
                                                 op0=ALU.mult, op1=ALU.subtract).then_inc(cat_done, 1)

                def group(t, u, more):
                    for b in range(NB):
                        if b + 1 < NB:
                            mask(t, u, b + 1)
                        split(t, u, b)
                    split(t, u, NB)
                    if more:
                        mask(t + u, 1 - u, 0)
                    wait(dve, y_done, m * GROUPS + t * 2 + (u + 1))
                    g = at_value(dve, t * 12 + u * 6)
                    at = [dve.snap(m * CC + o) for o in range(CC)]
                    for o in range(CC):
                        last = dve.bn_stats(gn_stat[:, ds(at[o], 1), ds(g, 6)], y_out[:, u, o])
                    last.then_inc(y_seen, 1)

                mask(0, 0, 0)
                with dve.Fori(0, GROUPS // 2 - 1) as t:
                    for u in range(2):
                        group(t, u, True)
                group(GROUPS // 2 - 1, 0, True)
                group(GROUPS // 2 - 1, 1, False)
                leave(dve)

            enter(dve, 7 * N_ENG)
            for k in range(IMAGES * CC):
                last = dve.bn_aggr(gn_mv[:, k], gn_stat[:, k])
            last.then_inc(gn_dve, 1)
            dve.wait_ge(gn_pe, 1)
            dve.tensor_tensor(gn_tmp[:, 0], gn_mv[:, :, 0], ps_gn[:, 0:4], ALU.subtract).then_inc(gn_dve, 1)
            dve.wait_ge(gn_dve, 2)
            dve.tensor_tensor(gn_tmp[:, 1], gn_tmp[:, 0], gn_tmp[:, 0], ALU.mult).then_inc(gn_dve, 1)
            dve.wait_ge(gn_dve, 3)
            dve.tensor_tensor(gn_tmp[:, 2], gn_tmp[:, 1], gn_mv[:, :, 1], ALU.add).then_inc(gn_dve, 1)
            dve.wait_ge(gn_pe, 2)
            dve.tensor_copy(gn_tmp[:, 3], ps_gn[:, 4:8]).then_inc(gn_dve, 1)
            dve.wait_ge(gn_act, 1)
            dve.reciprocal(gn_tmp[:, 5], gn_tmp[:, 4]).then_inc(gn_dve, 1)
            dve.wait_ge(gn_dve, 6)
            gamma = gn_par[:, 1:2].broadcast_to([128, IMAGES, CC])
            beta = gn_par[:, 2:3].broadcast_to([128, IMAGES, CC])
            pair = lambda z: z.rearrange("p (m c) -> p m c", m=IMAGES)
            dve.tensor_tensor(pair(gn_scale[:]), pair(gn_tmp[:, 5]), gamma, ALU.mult).then_inc(gn_dve, 1)
            dve.wait_ge(gn_dve, 7)
            dve.tensor_tensor(gn_tmp[:, 0], ps_gn[:, 0:4], gn_scale[:], ALU.mult).then_inc(gn_late, 1)
            dve.wait_ge(gn_late, 1)
            dve.tensor_tensor(pair(gn_bias[:]), beta, pair(gn_tmp[:, 0]), ALU.subtract).then_inc(gn_dve, 1)
            with dve.Fori(0, C_ALL // 2) as t:
                for u in range(2):
                    wait(dve, c_relu, t * 2 + (u + 1))
                    dve.tensor_tensor(c_x[:, u], c_x[:, u], c_y[:, u], ALU.add).then_inc(c_x1, 1)
                for u in range(2):
                    wait(dve, c_tok, t * 2 + (u + 3))
                    for k in range(TT):
                        dve.bn_stats(stats[:, u, k], ps_ct[:, u, k])
                dve.drain()
                for u in range(2):
                    for k in range(TT):
                        last = dve.bn_aggr(mv[:, u, k], stats[:, u, k])
                    last.then_inc(c_mv, 1)
                for u in range(2):
                    wait(dve, c_std, t * 2 + (u + 1))
                    dve.reciprocal(rstd[:, u], std[:, u]).then_inc(c_rstd, 1)
                for u in range(2):
                    wait(dve, c_rstd, t * 2 + (u + 1))
                    dve.scalar_tensor_tensor(out=nmr[:, u], in0=mv[:, u, :, 0], scalar=-1.0, in1=rstd[:, u],
                                             op0=ALU.mult, op1=ALU.mult).then_inc(c_nmr, 1)
                for u in range(2):
                    wait(dve, c_lnd, t * 2 + (u + 1))
                    wait(dve, c_stored[u], t * 32)
                    dve.tensor_tensor(c_res[:, u], ps_ct[:, u], c_ln[:, u], ALU.add).then_inc(c_resd, 1)
                for u in range(2):
                    tile = dve.snap(t * (2 * TT) + u * TT)
                    wait(dve, c_routed, t * 2 + (u + 1))
                    dve.tensor_copy(logits[:, ds(tile, TT)].rearrange("p t e -> p (t e)"), ps_r[:, 0:TT * E]).then_inc(c_logits, 1)

            steps = [0]

            def step(ins):
                ins.then_inc(top_dve, 1)
                steps[0] += 1
                dve.wait_ge(top_dve, steps[0])

            every = lambda z: z.unsqueeze(2).broadcast_to([128, TILES, E])
            ranks = order[:].rearrange("p (o e) -> p o e", o=1).broadcast_to([128, TILES, E])
            dve.wait_ge(consts_in, 16 * (N_CONST + 3))
            wait(dve, c_logits, C_ALL)
            step(dve.tensor_reduce(m2[:, 0], logits[:], AX.X, ALU.max))
            step(dve.tensor_tensor(t2[:, 0], logits[:], every(m2[:, 0]), ALU.subtract))
            assert steps[0] == TOP_EXP
            dve.wait_ge(top_exp, 1)
            step(dve.tensor_reduce(m2[:, 1], t2[:, 1], AX.X, ALU.add))
            step(dve.reciprocal(m2[:, 2], m2[:, 1]))
            step(dve.tensor_tensor(t2[:, 2], t2[:, 1], every(m2[:, 2]), ALU.mult))
            step(dve.scalar_tensor_tensor(out=t2[:, 1], in0=t2[:, 0], scalar=0.0, in1=ranks, op0=ALU.is_equal, op1=ALU.mult))
            step(dve.tensor_reduce(m2[:, 0], t2[:, 1], AX.X, ALU.max))
            step(dve.tensor_tensor(t2[:, 3], ranks, every(m2[:, 0]), ALU.is_equal))
            step(dve.scalar_tensor_tensor(out=t2[:, 1], in0=t2[:, 3], scalar=-BIG, in1=t2[:, 0], op0=ALU.mult, op1=ALU.add))
            step(dve.tensor_reduce(m2[:, 1], t2[:, 1], AX.X, ALU.max))
            step(dve.tensor_tensor(t2[:, 0], t2[:, 1], every(m2[:, 1]), ALU.is_equal))
            step(dve.tensor_tensor(t2[:, 1], t2[:, 0], ranks, ALU.mult))
            step(dve.tensor_reduce(m2[:, 1], t2[:, 1], AX.X, ALU.max))
            step(dve.tensor_tensor(t2[:, 0], ranks, every(m2[:, 1]), ALU.is_equal))
            step(dve.tensor_tensor(t2[:, 1], t2[:, 0], t2[:, 3], ALU.add))
            step(dve.tensor_tensor(t2[:, 0], t2[:, 1], t2[:, 2], ALU.mult))
            step(dve.tensor_reduce(m2[:, 0], t2[:, 0], AX.X, ALU.add))
            step(dve.tensor_scalar(m2[:, 1], m2[:, 0], 1e-12, None, ALU.max))
            step(dve.reciprocal(m2[:, 2], m2[:, 1]))
            dve.tensor_tensor(comb[:], t2[:, 0], every(m2[:, 2]), ALU.mult)
            leave(dve)

            enter(dve, 8 * N_ENG)
            for k, w in enumerate((w1, w2)):
                dve.wait_ge(w_hi_done, k + 3)
                dve.tensor_tensor(w[:, 1].rearrange("p e c f -> p (e c f)"), w_stage[:, k],
                                  w[:, 0].rearrange("p e c f -> p (e c f)").bitcast(F32), ALU.subtract).then_inc(w_lo_done, 1)
            with dve.Fori(0, C_ALL // 2) as t:
                for u in range(2):
                    n = t * 2 + u
                    tile = dve.snap(t * (2 * TT) + u * TT)
                    wait(dve, cwt_ready, n)
                    wait(dve, e_added, n * (TT * (E + 1)) + TT)
                    dve.tensor_copy(m_cw[:].rearrange("p t e -> p (t e)"),
                                    comb[:, ds(tile, TT)].rearrange("p t e -> p (t e)")).then_inc(cw_done, 1)
                    wait(dve, m_hi_done, n + 1)
                    dve.tensor_tensor(m_lo[:], m_x[:, u], m_hi[:].bitcast(F32), ALU.subtract).then_inc(m_lo_done, 1)
                    wait(dve, cw_done, n + 1)
                    for e in range(-1, E):
                        if e >= 0:
                            for f in range(CC):
                                wait(dve, h_hi_done, n * (E * CC) + (e * CC + f + 5))
                                dve.tensor_tensor(h_lo[:, e % 2, f], h_full[:, f], h_hi[:, e % 2, f].bitcast(F32),
                                                  ALU.subtract).then_inc(h_lo_done, 1)
                        for k in range(TT):
                            wait(dve, e_ready, n * (TT * (E + 1)) + ((e + 1) * TT + k // 2 * 2 + 2))
                            wait(dve, e_added, n * (TT * (E + 1)) + ((e + 1) * TT + k + 1))
                            if e < 0:
                                dve.tensor_tensor(m_acc[:, u, k], m_acc[:, u, k], ps_e[:, k], ALU.add).then_inc(e_added, 1)
                            else:
                                dve.scalar_tensor_tensor(out=m_acc[:, u, k], in0=ps_e[:, k], scalar=m_cw[:, k, e:e + 1],
                                                         in1=m_acc[:, u, k], op0=ALU.mult, op1=ALU.add).then_inc(e_added, 1)

        @block.gpsimd
        def _(pool):
            leave(pool)
            with pool.Fori(0, IMAGES) as m:
                enter(pool, m * (3 * N_ENG) + N_ENG)
                flat = taps[:].rearrange("p y b j k -> p y (b j k)")
                wide = 3 * TAPS
                pool.memset(taps[:], 0.0)
                pool.drain()
                with pool.Fori(0, GROUPS) as t:
                    n = m * GROUPS + t
                    wait(pool, taps_added, n)
                    wait(pool, g_copied, n * R + (R + 2))

                    def add(i, b, nb):
                        d = DILS[b] if i != 1 else 0
                        row = pool.snap(t * R + (PAD - (i - 1) * d))
                        at = flat[:, ds(row, R), b * wide:(b + nb) * wide]
                        return pool.tensor_tensor(at, at, g_rows[:, :, i, b:b + nb].rearrange("p r b k -> p r (b k)"), ALU.add)

                    add(1, 0, NB).then_inc(taps_centre, 1)
                    for b in range(NB - 1, 0, -1):
                        add(0, b, 1)
                        add(2, b, 1)
                    wait(pool, taps_centre, n + 1)
                    add(0, 0, 1).then_inc(taps_near, 1)
                    wait(pool, taps_near, n + 1)
                    add(2, 0, 1).then_inc(taps_added, 1)
                leave(pool)
                enter(pool, m * (3 * N_ENG) + 2 * N_ENG)
                leave(pool)
                enter(pool, m * (3 * N_ENG) + 3 * N_ENG)
                leave(pool)
            enter(pool, 7 * N_ENG)
            leave(pool)


_INS = [
    ("x", lambda i: i["x"]),
    ("w_gen", lambda i: np.stack([i[f"L0_conv_w_{z}"] for z in "abcd"])
        .reshape(NB, TAPS, CC, 128, 3, 3).transpose(3, 2, 4, 0, 5, 1).reshape(128, CC * GCOL)),
    ("w_proj", lambda i: i["L0_conv_w_proj"].reshape(C, 5 * CC, 128).transpose(2, 1, 0).reshape(128, -1)),
    ("b_proj", lambda i: i["L0_conv_b_proj"].reshape(CC, 128).T),
    ("gamma", lambda i: i["L0_conv_gn_gamma"].reshape(CC, 128).T),
    ("beta", lambda i: i["L0_conv_gn_beta"].reshape(CC, 128).T),
    ("router", lambda i: i["L0_ffn_router_w"].reshape(E, CC, 128).transpose(2, 1, 0)),
    ("w1", lambda i: i["L0_ffn_w1"].reshape(E, CC, 128, C).transpose(2, 0, 1, 3).reshape(128, -1)),
    ("b1", lambda i: i["L0_ffn_b1"].reshape(E * CC, 128).T),
    ("w2", lambda i: i["L0_ffn_w2"].reshape(E, CC, 128, C).transpose(2, 0, 1, 3).reshape(128, -1)),
    ("b2", lambda i: i["L0_ffn_b2"]),
]


def kernel(**inputs):
    import numpy as _np
    import concourse.bacc as _bacc
    from concourse import mybir as _mybir
    from concourse.bass_utils import run_bass_kernel_spmd as _run

    nc = _bacc.Bacc("TRN2", target_bir_lowering=False, num_devices=1)
    host = {k: _np.asarray(v) for k, v in inputs.items()}
    given = {name: _np.ascontiguousarray(lay(host)) for name, lay in _INS}
    given.update(shape_constants())
    arrays, aps = {}, {}
    for name, array in given.items():
        arrays[f"in_{name}"] = array
        aps[name] = nc.dram_tensor(f"in_{name}", array.shape, _mybir.dt.from_np(array.dtype), kind="ExternalInput").ap()
    aps["out"] = nc.dram_tensor("out_0", (IMAGES, C, H, W), F32, kind="ExternalOutput").ap()
    build(nc, aps)
    r = _run(nc, [arrays], core_ids=[0])
    return r.results[0]["out_0"]
```

```python
from contextlib import ExitStack

import numpy as np

import concourse.bass as bass
from concourse import mybir

ALU = mybir.AluOpType
ACT = mybir.ActivationFunctionType
AX = mybir.AxisListType
F32 = mybir.dt.float32
F32R = mybir.dt.float32r
F16 = mybir.dt.float16
I32 = mybir.dt.int32
ds = bass.ds

IMAGES, C, H, W = 2, 256, 96, 96
CC = C // 128
PIX = H * W
TOKENS = IMAGES * PIX
DILS = (1, 4, 8, 12)
NB = len(DILS)
PAD = max(DILS)
ROWS = H + 2 * PAD
TAPS = 9
GCOL = 3 * NB * 3 * TAPS
HCOL = NB * 3 * TAPS
FCOL = NB * TAPS
R = 4
T = R * W
GROUPS = H // R
R2 = 12
BATCHES = H // R2
SCALE = 1024.0
LN1_EPS, LN2_EPS, GN_EPS = 1e-6, 1e-5, 1e-5
GN_GROUPS = 32
E = 8
TC = 384
TT = TC // 128
TP = 2 * TT
CPAIRS = PIX // (2 * TC)
PAIRS = IMAGES * CPAIRS
TILES = TOKENS // 128
TOP = 2
S = 256
CAP = TOKENS + S
ETILES = TOKENS * TOP // S + E
XC = C + 4
MARK = C
XROWS = E * CAP + E * S
BIG = 1e30


def shape_constants():
    x = np.arange(W)
    shift = np.zeros((W, 1 + 2 * NB, W), np.float32)
    shift[:, 0] = np.eye(W)
    for b, d in enumerate(DILS):
        for n, j in enumerate((0, 2)):
            q = x + (j - 1) * d
            ok = (q >= 0) & (q < W)
            shift[q[ok], 1 + 2 * b + n, x[ok]] = 1
    colour = np.stack([(x // d) % 3 for d in DILS])
    rot = np.zeros((W, 3, NB, 3, 3), np.float32)
    for j in range(3):
        for b in range(NB):
            rot[x, j, b, :, (colour[b] + j - 1) % 3] = 1
    sel = np.zeros((2, NB, 3, 3, NB, 3, 2, W), np.float16)
    for p in range(2):
        for b in range(NB):
            for i in range(3):
                for k in range(3):
                    sel[p, b, i, k, b, i, p] = colour[b] == k
    band = np.zeros((W, NB, W), np.float32)
    for b, d in enumerate(DILS):
        band[:, b] = np.isin(x[:, None] - x[None, :], (-d, 0, d))
    fill = np.zeros((2 * E, S, XC), np.float32)
    fill[:, :, MARK + 1] = TOP * TOKENS + np.arange(2 * E * S).reshape(2 * E, S)
    g = np.arange(128) // (C // GN_GROUPS)
    same = (g[:, None] == g[None, :]).astype(np.float32) / (C // GN_GROUPS)
    return {
        "k_ident": np.eye(128, dtype=np.float32),
        "k_ident16": np.stack([np.eye(W), SCALE * np.eye(W)], 1).astype(np.float16),
        "k_shift": shift,
        "k_rot": rot.reshape(W, 3, FCOL),
        "k_sel": sel.reshape(2 * FCOL, NB * 3 * 2, W),
        "k_band": band.astype(np.float16),
        "k_same": same,
        "k_order": np.tile(np.arange(E, 0, -1, dtype=np.float32), (128, 1)),
        "k_before": np.stack([np.triu(np.ones((128, 128)), 1), np.ones((128, 128))], 1).astype(np.float16),
        "k_region": np.tile(np.arange(E, dtype=np.float32) * CAP, (128, 1)),
        "k_etiles": np.tile(np.arange(ETILES, dtype=np.float32), (128, 1)),
        "k_fill": fill,
        "k_token": 2.0 * (np.arange(TILES)[None, :] * 128 + np.arange(128)[:, None]).astype(np.float32),
    }



def build(nc, a):
    with ExitStack() as ctx:
        def sbuf(on, name, shape, dt=F32):
            return on.enter_context(nc.sbuf_tensor(name, shape, dt))

        def psum(on, name, shape, dt=F32):
            return on.enter_context(nc.psum_tensor(name, shape, dt))

        def sem(name):
            return ctx.enter_context(nc.semaphore(name))

        def sems(names):
            return [sem(n) for n in names.split()]

        y_dram = nc.dram_tensor("y_scratch", [IMAGES, 128, CC, PIX], F32).ap()
        res_dram = nc.dram_tensor("res_scratch", [2 * PAIRS, 128, TT * C], F32).ap()
        xs_dram = nc.dram_tensor("expert_in", [XROWS, XC], F32).ap()
        ys_dram = nc.dram_tensor("expert_out", [TOP * TOKENS + 2 * E * S, C], F32).ap()
        wg_dram = nc.dram_tensor("wg_scratch", [2, 128, CC * GCOL], F32).ap()
        wp_dram = nc.dram_tensor("wp_scratch", [2, 128, 5 * CC * C], F32).ap()
        x_dram = a["x"].rearrange("m (cc p) h w -> m p cc (h w)", p=128)
        out_dram = a["out"].rearrange("m (cc p) h w -> m p cc (h w)", p=128)

        ident = sbuf(ctx, "ident", [128, 128])
        eps = sbuf(ctx, "eps", [128, 3])
        gn_par = sbuf(ctx, "gn_par", [128, 3, CC])
        gn_stat = sbuf(ctx, "gn_stat", [128, IMAGES * CC, GROUPS * 6])
        gn_scale = sbuf(ctx, "gn_scale", [128, IMAGES * CC])
        gn_bias = sbuf(ctx, "gn_bias", [128, IMAGES * CC])
        stats = sbuf(ctx, "stats", [128, 2, 4, 6])
        mv = sbuf(ctx, "mv", [128, 2, 4, 2])
        std = sbuf(ctx, "std", [128, 2, 4])
        rstd = sbuf(ctx, "rstd", [128, 2, 4])
        nmr = sbuf(ctx, "nmr", [128, 2, 4])

        conv = ExitStack()
        rows16 = sbuf(conv, "rows16", [W, H, 2, C], F16)
        ident16 = sbuf(conv, "ident16", [W, 2, W], F16)
        with ExitStack() as r0:
            wg_stage = sbuf(r0, "wg_stage", [128, CC * GCOL])
            wp_stage = sbuf(r0, "wp_stage", [128, 5 * CC * C])
            wg_split = sbuf(r0, "wg_split", [128, 2, CC * GCOL], F32R)
            wp_split = sbuf(r0, "wp_split", [128, 2, 5 * CC * C], F32R)
        with ExitStack() as r1:
            taps = sbuf(r1, "taps", [W, ROWS, NB, 3, TAPS])
            with ExitStack() as r2:
                x_in = sbuf(r2, "x_in", [128, 2, CC, T])
                xn = sbuf(r2, "xn", [W, 2, R, C])
                xc_hi = sbuf(r2, "xc_hi", [128, 2, CC, T], F32R)
                xc_lo = sbuf(r2, "xc_lo", [128, 2, CC, T], F32R)
                wg = sbuf(r2, "wg", [128, 2, CC, GCOL], F32R)
                g_rows = sbuf(r2, "g_rows", [W, 2, R, 3, NB, 3 * TAPS])
            filt_t = sbuf(r1, "filt_t", [2 * FCOL, PIX], F16)
            with ExitStack() as r2:
                shift = sbuf(r2, "shift", [W, 1 + 2 * NB, W])
                rot = sbuf(r2, "rot", [W, 3, FCOL])
                fa = sbuf(r2, "fa", [W, R2 * FCOL])
                fb = sbuf(r2, "fb", [W, R2 * FCOL])
                fr = sbuf(r2, "fr", [W, 3, R2 * FCOL])
                f16 = sbuf(r2, "f16", [W, R2, 2, FCOL], F16)
                fred = sbuf(r2, "fred", [W, 3, R2 * NB])
        with ExitStack() as r1:
            sel = sbuf(r1, "sel", [2 * FCOL, NB * 3 * 2, W], F16)
            band = sbuf(r1, "band", [W, NB, W], F16)
            wp = sbuf(r1, "wp", [128, 2, 5 * CC, C], F32R)
            bands = sbuf(r1, "bands", [W, 2, 2, 3, T], F16)
            cat_hi = sbuf(r1, "cat_hi", [128, 2, CC, T], F32R)
            cat_lo = sbuf(r1, "cat_lo", [128, 2, CC, T], F32R)
            used = 2 * NB * 3 * 2 * W + 2 * NB * W + 4 * 2 * 5 * CC * C + 2 * 2 * 2 * 3 * T + 2 * 4 * 2 * CC * T
            sbuf(r1, "gap_before_filt_t", [128, 4 * ROWS * NB * 3 * TAPS - used], mybir.dt.uint8)
            sbuf(r1, "place_of_filt_t", [128, PIX], F16)
            y_out = sbuf(r1, "y_out", [128, 2, CC, T])
        conv.close()

        gate = sbuf(ctx, "gate", [128, TOP, TILES])
        etable = sbuf(ctx, "etable", [1, 2, ETILES], I32)
        erank = sbuf(ctx, "erank", [128, ETILES])
        w1 = sbuf(ctx, "w1", [128, E, 2, CC * C], F32R)
        w2 = sbuf(ctx, "w2", [128, E, 2, CC * C], F32R)
        with ExitStack() as r1:
            c_x = sbuf(r1, "c_x", [128, 2, 2, CC, TC])
            c_y = sbuf(r1, "c_y", [128, 2, 2, CC, TC])
            c_ln = sbuf(r1, "c_ln", [128, 4, 2, TT, XC])
            c_lnt = sbuf(r1, "c_lnt", [128, 2, CC, TC])
            c_res = sbuf(r1, "c_res", [128, 2, TT, C])
            w_stage = sbuf(r1, "w_stage", [128, E, CC * C])
            same = sbuf(r1, "same", [128, 128])
            gn_mv = sbuf(r1, "gn_mv", [128, IMAGES * CC, 2])
            gn_tmp = sbuf(r1, "gn_tmp", [128, 6, IMAGES * CC])
            pair_scale = sbuf(r1, "pair_scale", [128, PAIRS, CC])
            pair_bias = sbuf(r1, "pair_bias", [128, PAIRS, CC])
            router = sbuf(r1, "router", [128, CC, E])
            order = sbuf(r1, "order", [128, E])
            before = sbuf(r1, "before", [128, 2, 128], F16)
            region = sbuf(r1, "region", [128, E])
            etiles = sbuf(r1, "etiles", [128, ETILES])
            token = sbuf(r1, "token", [128, TILES])
            region_end = sbuf(r1, "region_end", [1, E], I32)
            gap = sbuf(r1, "gap", [128, TILES, E])
            gap_two = sbuf(r1, "gap_two", [128, TOP, TILES])
            next_slot = sbuf(r1, "next_slot", [128, E])
            largest = sbuf(r1, "largest", [128, 6, TP])
            pick = sbuf(r1, "pick", [128, 3, TP, E])
            chosen = sbuf(r1, "chosen", [128, TOP, TP, E])
            either = sbuf(r1, "either", [128, TP + 1, E], F16)
            slot = sbuf(r1, "slot", [128, TP, E])
            slot_of = sbuf(r1, "slot_of", [128, TOP, TP, E])
            pos_f = sbuf(r1, "pos_f", [128, TOP, TP])
            pos = sbuf(r1, "pos", [128, 4, TOP, TP], I32)
            soft = sbuf(r1, "soft", [128, TILES, E])
            soft1 = sbuf(r1, "soft1", [128, 8, TILES])
            tab = sbuf(r1, "tab", [128, 8, E])
            tab_i = sbuf(r1, "tab_i", [128, 2, E], I32)
            tab_ge = sbuf(r1, "tab_ge", [128, 2, ETILES, E])
            tab_row = sbuf(r1, "tab_row", [128, 4, ETILES])
        with ExitStack() as r1:
            b1 = sbuf(r1, "b1", [128, E, CC])
            b2 = sbuf(r1, "b2", [128, E, C])
            e_x = sbuf(r1, "e_x", [128, 2, S // 128, XC])
            e_dest = sbuf(r1, "e_dest", [128, ETILES, S // 128], I32)
            w1_now = sbuf(r1, "w1_now", [128, 2, 2, CC, C], F32R)
            b1_now = sbuf(r1, "b1_now", [128, 2, CC])
            e_hi = sbuf(r1, "e_hi", [128, 2, CC, S], F32R)
            e_lo = sbuf(r1, "e_lo", [128, 2, CC, S], F32R)
            e_act = sbuf(r1, "e_act", [128, 2, CC, S])
            h_hi = sbuf(r1, "h_hi", [128, 2, CC, S], F32R)
            h_lo = sbuf(r1, "h_lo", [128, 2, CC, S], F32R)
            e_out = sbuf(r1, "e_out", [128, 2, S // 128, C])
            dest = sbuf(r1, "dest", [128, 2, S // 128], I32)
        with ExitStack() as r1:
            o_y = sbuf(r1, "o_y", [128, 2, TT, TOP, C])
            o_acc = sbuf(r1, "o_acc", [128, 2, TT, C])
            o_sum = sbuf(r1, "o_sum", [128, 2, TT, C])
            o_out = sbuf(r1, "o_out", [128, 2, CC, TC])

        with ExitStack() as r1:
            ps_tok = psum(r1, "ps_tok", [128, 2, R, C])
            ps_ch = psum(r1, "ps_ch", [128, CC, 512])
            ps_g = psum(r1, "ps_g", [128, 2, 512])
        with ExitStack() as r1:
            ps_f = psum(r1, "ps_f", [128, 512])
            ps_ft = psum(r1, "ps_ft", [128, 2, 1024], F16)
        with ExitStack() as r1:
            ps_b = psum(r1, "ps_b", [128, 4, 512])
            ps_o = psum(r1, "ps_o", [128, CC, 512])
            ps_y = psum(r1, "ps_y", [128, CC, 512])
        with ExitStack() as r1:
            ps_ct = psum(r1, "ps_ct", [128, 2, 4, C])
            ps_cc = psum(r1, "ps_cc", [128, CC, 512])
            ps_r = psum(r1, "ps_r", [128, 512])
            ps_p = psum(r1, "ps_p", [128, 512])
        with ExitStack() as r1:
            ps_x = psum(r1, "ps_x", [128, 2, CC, S])
            ps_1 = psum(r1, "ps_1", [128, 2, CC, S])
            ps_2 = psum(r1, "ps_2", [128, 2, S // 128, C])
        with ExitStack() as r1:
            ps_t = psum(r1, "ps_t", [128, 2, CC, 512])

        consts_in, phase_left, phase_entered = sems("consts_in phase_left phase_entered")
        w_loaded, w_hi_done, w_lo_done, w_stored = sems("w_loaded w_hi_done w_lo_done w_stored")
        x_loaded = sems("x_loaded0 x_loaded1")
        tok_ready, mv_done, std_done, rstd_done, nmr_done = sems(
            "tok_ready mv_done std_done rstd_done nmr_done")
        xn_done, rows_hi_done, rows_lo_done, ch_ready, xc_hi_done, xc_lo_done = sems(
            "xn_done rows_hi_done rows_lo_done ch_ready xc_hi_done xc_lo_done")
        g_ready, g_copied, taps_centre, taps_near, taps_added = sems(
            "g_ready g_copied taps_centre taps_near taps_added")
        wg_loaded, wp_loaded, shift_loaded = sems("wg_loaded wp_loaded shift_loaded")
        f_ready, f_dve, f_sub, f_exp, f_hi_done, f_split, ft_ready, ft_copied = sems(
            "f_ready f_dve f_sub f_exp f_hi_done f_split ft_ready ft_copied")
        bc_ready, masked, out_ready, cat_hi_done, cat_done = sems("bc_ready masked out_ready cat_hi_done cat_done")
        proj_done, y_done, y_seen = sems("proj_done y_done y_seen")
        y_stored = sems("y_stored0 y_stored1")
        gn_dve, gn_act, gn_pe, gn_late = sems("gn_dve gn_act gn_pe gn_late")
        c_loaded = sems("c_loaded00 c_loaded01 c_loaded10 c_loaded11")
        c_relu, c_x1, c_tok, c_mv, c_std, c_rstd, c_nmr, c_lnd = sems(
            "c_relu c_x1 c_tok c_mv c_std c_rstd c_nmr c_lnd")
        c_resd, c_cht, c_lntd, c_routed, c_either, c_ranked, c_pick, c_based, c_pos, c_gap = sems(
            "c_resd c_cht c_lntd c_routed c_either c_ranked c_pick c_based c_pos c_gap")
        c_stored = sems("c_stored0 c_stored1")
        c_scattered, c_slotted = sems("c_scattered c_slotted")
        passed, top_dve, top_exp, zeroed, cw_hi, cw_lo = sems("passed top_dve top_exp zeroed cw_hi cw_lo")
        e_loaded = sems("e_loaded0 e_loaded1")
        e_turned, e_hi_done, e_lo_done, e_used, w_ready, e_first, e_act_done = sems(
            "e_turned e_hi_done e_lo_done e_used w_ready e_first e_act_done")
        h_hi_done, h_lo_done, e_second, e_out_done, e_sent = sems("h_hi_done h_lo_done e_second e_out_done e_sent")
        e_scattered = sems("e_scattered0 e_scattered1")
        o_loaded = sems("o_loaded0 o_loaded1")
        o_first, o_summed, o_turned, o_copied = sems("o_first o_summed o_turned o_copied")
        o_stored = sems("o_stored0 o_stored1")

        N_ENG = 5
        sync = nc.sync

        def leave(eng):
            if eng is sync:
                eng.sem_inc(phase_left, 1)
            else:
                eng.drain().then_inc(phase_left, 1)

        def enter(eng, phases):
            eng.wait_ge(phase_left, phases)
            eng.sem_inc(phase_entered, 1)

        def at_value(eng, x):
            return x if isinstance(x, int) else eng.snap(x)

        def three_passes(eng, out, lhs, rhs, start, stop):
            for n, (p, q) in enumerate(((0, 0), (0, 1), (1, 0))):
                mm = eng.matmul(out, lhs[p], rhs[q], start=start and n == 0, stop=stop and n == 2)
            return mm

        N_CONST = 7
        MASKS = GROUPS * NB * 6
        STEPS = GROUPS * (NB + 1)
        CATS = STEPS * CC
        TOP_ENDS = 1
        UNSCALE = 1.0 / (SCALE * SCALE)
        counted = [
            bc_ready, c_based, c_cht, c_either, c_gap, c_lnd, c_lntd, c_mv, c_nmr, c_pick, c_pos, c_ranked, c_relu, c_resd,
            c_routed, c_rstd, c_slotted, c_std, c_tok, c_x1, cat_done, cat_hi_done, ch_ready, e_act_done, e_first,
            e_hi_done, e_lo_done, e_out_done, e_second, e_sent, e_turned, e_used, f_dve, f_exp, f_hi_done, f_ready,
            f_split, f_sub, ft_copied, ft_ready, g_copied, g_ready, h_hi_done, h_lo_done, masked, mv_done, nmr_done,
            o_copied, o_first, o_summed, o_turned, out_ready, proj_done, rows_hi_done, rows_lo_done, rstd_done, std_done,
            taps_added, taps_centre, taps_near, tok_ready, w_ready, wg_loaded, wp_loaded, shift_loaded, xc_hi_done, xc_lo_done,
            xn_done, y_done, y_seen, *c_loaded, *c_stored, *e_loaded, *o_loaded, *o_stored, *x_loaded, *y_stored,
        ]

        def wait(eng, signal, count):
            eng.wait_ge(signal, count + 1)

        def wait_first(eng, signal, count):
            wait(eng, signal, count)
            eng.sem_inc(passed, 1)

        block = ctx.enter_context(nc.Block())

        @block.sync
        def _(sp):
            for signal in counted:
                sp.sem_inc(signal, 1)
            for dst, src in ((ident[:], a["k_ident"]), (ident16[:], a["k_ident16"]),
                             (gn_par[:, 0], a["b_proj"]), (gn_par[:, 1], a["gamma"]), (gn_par[:, 2], a["beta"])):
                sp.dma_start(dst, src).then_inc(consts_in, 16)
            sp.dma_start(wg_stage[:], a["w_gen"]).then_inc(consts_in, 16)
            sp.dma_start(wp_stage[:], a["w_proj"]).then_inc(consts_in, 16)
            sp.wait_ge(w_hi_done, 2)
            sp.wait_ge(w_lo_done, 2)
            for p in range(2):
                sp.dma_start(wg_dram[p], wg_split[:, p].bitcast(F32)).then_inc(w_stored, 16)
                sp.dma_start(wp_dram[p], wp_split[:, p].bitcast(F32)).then_inc(w_stored, 16)
            sp.wait_ge(w_stored, 64)
            leave(sp)

            with sp.Fori(0, IMAGES) as m:
                enter(sp, m * (3 * N_ENG) + N_ENG)
                for p in range(2):
                    sp.dma_start(wg[:, p].rearrange("p a g -> p (a g)").bitcast(F32), wg_dram[p]).then_inc(wg_loaded, 16)
                with sp.Fori(0, GROUPS // 2) as t:
                    for u in range(2):
                        off = sp.snap(t * (2 * T) + u * T)
                        img = sp.snap(m)
                        count = sp.snap(m * GROUPS + t * 2 + (u + 1))
                        wait(sp, tok_ready, count)
                        sp.dma_start(x_in[:, u], x_dram[img, :, :, ds(off, T)]).then_inc(x_loaded[u], 16)
                leave(sp)
                enter(sp, m * (3 * N_ENG) + 2 * N_ENG)
                sp.dma_start(shift[:], a["k_shift"]).then_inc(shift_loaded, 16)
                sp.dma_start(rot[:], a["k_rot"]).then_inc(shift_loaded, 16)
                leave(sp)
                enter(sp, m * (3 * N_ENG) + 3 * N_ENG)
                for p in range(2):
                    sp.dma_start(wp[:, p].rearrange("p a g -> p (a g)").bitcast(F32), wp_dram[p]).then_inc(wp_loaded, 16)
                sp.dma_start(sel[:], a["k_sel"]).then_inc(wp_loaded, 16)
                sp.dma_start(band[:], a["k_band"]).then_inc(wp_loaded, 16)
                with sp.Fori(0, GROUPS // 2) as t:
                    for u in range(2):
                        off = sp.snap(t * (2 * T) + u * T)
                        img = sp.snap(m)
                        count = sp.snap(m * GROUPS + t * 2 + (u + 1))
                        wait(sp, y_done, count)
                        sp.dma_start(y_dram[img, :, :, ds(off, T)], y_out[:, u]).then_inc(y_stored[u], 16)
                for u in range(2):
                    wait(sp, y_stored[u], m * (8 * GROUPS) + 8 * GROUPS)
                leave(sp)

            enter(sp, 7 * N_ENG)

            def load(m, k, v):
                for u in range(2):
                    off, img = at_value(sp, k * (2 * TC) + u * TC), m
                    wait(sp, c_tok, k * 2 + (m * (2 * CPAIRS) + u + 1))
                    sp.dma_start(c_x[:, v, u], x_dram[img, :, :, ds(off, TC)]).then_inc(c_loaded[2 * v + u], 16)
                    sp.dma_start(c_y[:, v, u], y_dram[img, :, :, ds(off, TC)]).then_inc(c_loaded[2 * v + u], 16)

            def store(pair):
                for u in range(2):
                    grp = at_value(sp, pair * 2 + u)
                    wait(sp, c_resd, pair * 2 + (u + 1))
                    sp.dma_start(res_dram[grp], c_res[:, u].rearrange("p k c -> p (k c)")).then_inc(c_stored[u], 16)

            for dst, src in ((same[:], a["k_same"]), (router[:], a["router"]), (order[:], a["k_order"]),
                             (before[:], a["k_before"]), (region[:], a["k_region"]), (etiles[:], a["k_etiles"]),
                             (token[:], a["k_token"])):
                sp.dma_start(dst, src).then_inc(consts_in, 16)
            load(0, 0, 0)
            sp.dma_start(w_stage[:].rearrange("p e c -> p (e c)"), a["w1"]).then_inc(w_loaded, 16)
            for e in range(E):
                sp.dma_start(xs_dram[E * CAP + e * S:E * CAP + (e + 1) * S], a["k_fill"][E + e]).then_inc(zeroed, 16)
            load(0, 1, 1)
            sp.wait_ge(cw_lo, 1)
            sp.dma_start(w_stage[:].rearrange("p e c -> p (e c)"), a["w2"]).then_inc(w_loaded, 16)
            for m in range(IMAGES):
                with sp.Fori(1 - m, CPAIRS // 2) as t:
                    for v in range(2):
                        load(m, t * 2 + v, v)
                        store(t * 2 + (m * CPAIRS + v - 2))
            store(PAIRS - 2)
            store(PAIRS - 1)
            for u in range(2):
                wait(sp, c_stored[u], 16 * PAIRS)
            wait(sp, c_slotted, PAIRS + 4)
            sp.wait_ge(top_dve, TOP_ENDS)
            for e in range(E):
                end = sp.value_load(region_end[0:1, e:e + 1], min_val=e * CAP, max_val=e * CAP + TOKENS)
                sp.dma_start(xs_dram[ds(end, S)], a["k_fill"][e]).then_inc(zeroed, 16)
            sp.wait_ge(zeroed, 16 * 2 * E)
            leave(sp)

            enter(sp, 8 * N_ENG)
            sp.dma_start(b1[:], a["b1"]).then_inc(w_loaded, 16)
            sp.dma_start(b2[:].rearrange("p e c -> p (e c)"), a["b2"].partition_broadcast(128)).then_inc(w_loaded, 16)
            with sp.Fori(0, ETILES // 2) as t:
                for u in range(2):
                    row = sp.value_load(etable[0:1, 1, ds(t * 2 + u, 1)], min_val=0, max_val=XROWS - S)
                    wait(sp, e_used, t * 2 + (u + 1))
                    sp.dma_start(e_x[:, u].rearrange("p j c -> p (j c)"),
                                 xs_dram[ds(row, S)].rearrange("(p j) c -> p (j c)", p=128)).then_inc(e_loaded[u], 16)
            leave(sp)

            enter(sp, 9 * N_ENG)
            with sp.Fori(0, PAIRS) as t:
                for u in range(2):
                    grp = sp.snap(t * 2 + u)
                    row = sp.snap(t * (4 * TC) + u * (2 * TC))
                    wait(sp, o_summed, t * 2 + (u + 1))
                    sp.dma_start(o_acc[:, u].rearrange("p k c -> p (k c)"), res_dram[grp]).then_inc(o_loaded[u], 16)
                    sp.dma_start(o_y[:, u].rearrange("p k z c -> p k (z c)"),
                                 ys_dram[ds(row, 2 * TC)].rearrange("(k p z) c -> p k (z c)", k=TT, p=128)
                                 ).then_inc(o_loaded[u], 16)

        @block.tensor
        def _(pe):
            pe.wait_ge(consts_in, 16 * N_CONST)
            pe.sem_inc(tok_ready, 2)
            pe.sem_inc(proj_done, 2)
            pe.sem_inc(c_tok, 4)
            pe.sem_inc(o_turned, 2)
            leave(pe)
            with pe.Fori(0, IMAGES) as m:
                wait(pe, wg_loaded, m * 32 + 32)
                enter(pe, m * (3 * N_ENG) + N_ENG)
                at = lambda k: m * GROUPS + k

                def tokens(k, u):
                    wait(pe, x_loaded[u], m * (8 * GROUPS) + (k - u) * 8 + 16)
                    for r in range(R):
                        for c in range(CC):
                            mm = pe.transpose(ps_tok[0:W, u, r, c * 128:(c + 1) * 128],
                                              x_in[:, u, c, r * W:(r + 1) * W], ident[:])
                    mm.then_inc(tok_ready, 1)

                def channels(k, u):
                    wait(pe, xn_done, at(k) + 1)
                    wait(pe, xc_lo_done, at(k))
                    for r in range(R):
                        for c in range(CC):
                            mm = pe.transpose(ps_ch[:, c, r * W:(r + 1) * W],
                                              xn[:, u, r, c * 128:(c + 1) * 128], ident[0:W, 0:W])
                    mm.then_inc(ch_ready, 1)

                def tap_products(k, u, rows):
                    wait(pe, xc_lo_done, at(k) + 1)
                    for r in rows:
                        wait(pe, g_copied, at(k) * R + (r + 1))
                        for c in range(CC):
                            mm = three_passes(pe, ps_g[0:W, r % 2, 0:GCOL],
                                              [z[:, u, c, r * W:(r + 1) * W] for z in (xc_hi, xc_lo)],
                                              [wg[:, p, c] for p in range(2)], c == 0, c == CC - 1)
                        mm.then_inc(g_ready, 1)

                def step(k, u, first=False, last=False):
                    channels(k, u)
                    if not last:
                        tokens(k + 2, u)
                    if not first:
                        tap_products(k - 1, 1 - u, (2, 3))
                    tap_products(k, u, (0, 1))

                tokens(0, 0)
                tokens(1, 1)
                step(0, 0, first=True)
                step(1, 1)
                with pe.Fori(1, GROUPS // 2 - 1) as t:
                    for u in range(2):
                        step(t * 2 + u, u)
                step(GROUPS - 2, 0, last=True)
                step(GROUPS - 1, 1, last=True)
                tap_products(GROUPS - 1, 1, (2, 3))
                leave(pe)
                enter(pe, m * (3 * N_ENG) + 2 * N_ENG)
                wait_first(pe, shift_loaded, m * 32 + 32)
                with pe.Fori(0, BATCHES) as k:
                    n = m * BATCHES + k
                    row = pe.snap(k * R2 + PAD)
                    out = ps_f[0:W, 0:R2 * FCOL].rearrange("p (r b k) -> p r b k", r=R2, b=NB)
                    wait(pe, f_split, n)
                    for b in range(NB):
                        for s, j in enumerate((0, 2)):
                            pe.matmul(out[:, :, b, :], shift[:, 1 + 2 * b + s], taps[:, ds(row, R2), b, j, :],
                                      start=(b == 0 and s == 0), stop=False, skip_group_check=True)
                    mm = pe.matmul(out, shift[:, 0], taps[:, ds(row, R2), :, 1, :], start=False, stop=True,
                                   skip_group_check=True)
                    mm.then_inc(f_ready, 1)
                    wait(pe, f_split, n + 1)
                    wait(pe, ft_copied, n)
                    for r in range(R2):
                        mm = pe.transpose(ps_ft[0:2 * FCOL, r // 6, (r % 6) * W:(r % 6 + 1) * W],
                                          f16[:, r].rearrange("p a f -> p (a f)"), ident16[:, 0])
                    mm.then_inc(ft_ready, 1)
                leave(pe)
                enter(pe, m * (3 * N_ENG) + 3 * N_ENG)
                wait(pe, wp_loaded, m * 64 + 64)

                def broadcast(g, b, parts):
                    for n in parts:
                        k = (g * NB + b) * 6 + n
                        wait(pe, masked, m * MASKS + (k + 1))
                        pe.matmul(ps_b[0:W, k % 4, 0:T], sel[:, b * 6 + n], filt_t[:, g * T:(g + 1) * T],
                                  start=True, stop=True).then_inc(bc_ready, 1)

                def branch(g, b, chunks):
                    if b < NB:
                        wait(pe, masked, m * MASKS + ((g * NB + b) * 6 + 6 + 4))
                    for c in chunks:
                        k = (g * (NB + 1) + b) * 2 + c
                        wait(pe, cat_done, m * CATS + (k + 1))
                        for r in range(R):
                            y = g * R + r
                            if b == NB:
                                todo = [(y, p, ident16[:, 1]) for p in range(2)]
                            else:
                                todo = [(y + (i - 1) * DILS[b], p, bands[:, b % 2, q, i, r * W:(r + 1) * W])
                                        for i in range(3) for p, q in ((0, 0), (0, 1), (1, 0))
                                        if 0 <= y + (i - 1) * DILS[b] < H]
                            for n, (src, p, rhs) in enumerate(todo):
                                mm = pe.matmul(ps_o[:, c, r * W:(r + 1) * W], rows16[:, src, p, c * 128:(c + 1) * 128],
                                               rhs, start=n == 0, stop=n == len(todo) - 1)
                        mm.then_inc(out_ready, 1)

                def project(g, b):
                    s = g * (NB + 1) + b
                    wait(pe, cat_done, m * CATS + (2 * s + 4))
                    if b == 0:
                        wait(pe, y_done, m * GROUPS + g)
                    blk = (b + 1) % (NB + 1)
                    for o in range(CC):
                        for c in range(CC):
                            mm = three_passes(pe, ps_y[:, o, 0:T],
                                              [wp[:, p, blk * CC + c, o * 128:(o + 1) * 128] for p in range(2)],
                                              [z[:, s % 2, c] for z in (cat_hi, cat_lo)],
                                              b == 0 and c == 0, b == NB and c == CC - 1)
                    mm.then_inc(proj_done, 1)

                broadcast(0, 0, range(6))
                for g in range(GROUPS):
                    for b in range(NB):
                        if b + 1 < NB:
                            broadcast(g, b + 1, range(4))
                        branch(g, b, (0,))
                        if b + 1 < NB:
                            broadcast(g, b + 1, (4, 5))
                        branch(g, b, (1,))
                        if b:
                            project(g, b - 1)
                    if g + 1 < GROUPS:
                        broadcast(g + 1, 0, range(4))
                    branch(g, NB, range(CC))
                    project(g, NB - 1)
                    if g + 1 < GROUPS:
                        broadcast(g + 1, 0, (4, 5))
                    project(g, NB)
                leave(pe)

            enter(pe, 7 * N_ENG)
            pe.wait_ge(consts_in, 16 * (N_CONST + 7))
            pe.wait_ge(gn_dve, 1)
            pe.matmul(ps_p[:, 0:4], same[:], gn_mv[:, :, 0], start=True, stop=True).then_inc(gn_pe, 1)
            pe.wait_ge(gn_dve, 4)
            pe.matmul(ps_r[:, 0:4], same[:], gn_tmp[:, 2], start=True, stop=True).then_inc(gn_pe, 1)

            def rank(pair):
                wait(pe, c_either, pair + 1)
                pe.matmul(ps_p[:, 0:(TP + 1) * E], before[:, 0], either[:].rearrange("p t e -> p (t e)"),
                          start=True, stop=False, skip_group_check=True)
                for k in range(TP):
                    pe.matmul(ps_p[:, (k + 1) * E:(TP + 1) * E].rearrange("p (t e) -> p t e", e=E), before[:, 1],
                              either[:, k:k + 1].broadcast_to([128, TP - k, E]),
                              start=False, stop=False, skip_group_check=True)
                pe.matmul(ps_p[:, 0:(TP + 1) * E].rearrange("p (t e) -> p t e", e=E), before[:, 1],
                          either[:, TP:TP + 1].broadcast_to([128, TP + 1, E]),
                          start=False, stop=True, skip_group_check=True).then_inc(c_ranked, 1)

            def turn(pair, v, first=False):
                for u in range(2):
                    wait(pe, c_x1, pair * 2 + (u + 1))
                    if not first:
                        wait(pe, c_resd, pair * 2 + (u - 1))
                    for k in range(TT):
                        for c in range(CC):
                            mm = pe.transpose(ps_ct[:, u, k, c * 128:(c + 1) * 128],
                                              c_x[:, v % 2, u, c, k * 128:(k + 1) * 128], ident[:])
                    mm.then_inc(c_tok, 1)

            def route(pair, v, first=False):
                for u in range(2):
                    wait(pe, c_lnd, pair * 2 + (u + 1))
                    wait(pe, c_lntd, pair * 2 + u)
                    for k in range(TT):
                        for c in range(CC):
                            mm = pe.transpose(ps_cc[:, c, k * 128:(k + 1) * 128],
                                              c_ln[:, v, u, k, c * 128:(c + 1) * 128], ident[:])
                    mm.then_inc(c_cht, 1)
                wait(pe, c_lntd, pair * 2 + 2)
                if not first:
                    wait(pe, c_gap, pair * 2)
                for u in range(2):
                    for k in range(TT):
                        for c in range(CC):
                            mm = pe.matmul(ps_r[:, (u * TT + k) * E:(u * TT + k + 1) * E],
                                           c_lnt[:, u, c, k * 128:(k + 1) * 128], router[:, c],
                                           start=c == 0, stop=c == CC - 1)
                mm.then_inc(c_routed, 1)

            def step(pair, v):
                turn(pair, v)
                rank(pair - 3)
                route(pair - 1, (v + 3) % 4)

            turn(0, 0, True)
            turn(1, 1)
            route(0, 0, True)
            turn(2, 2)
            route(1, 1)
            with pe.Fori(0, (PAIRS - 4) // 4) as t:
                for k in range(3, 7):
                    step(t * 4 + k, k % 4)
            step(PAIRS - 1, 3)
            rank(PAIRS - 3)
            route(PAIRS - 1, 3)
            rank(PAIRS - 2)
            rank(PAIRS - 1)
            leave(pe)

            enter(pe, 8 * N_ENG)

            def turn_in(n, u):
                wait(pe, e_loaded[u], (n - u) * 8 + 16)
                for j in range(S // 128):
                    for c in range(CC):
                        mm = pe.transpose(ps_x[:, u, c, j * 128:(j + 1) * 128], e_x[:, u, j, c * 128:(c + 1) * 128],
                                          ident[:])
                mm.then_inc(e_turned, 1)

            def first_product(n, u):
                wait(pe, e_lo_done, n + 1)
                wait(pe, w_ready, n + 1)
                for f in range(CC):
                    for c in range(CC):
                        mm = three_passes(pe, ps_1[:, u, f], [w1_now[:, u, p, c, f * 128:(f + 1) * 128] for p in range(2)],
                                          [z[:, u, c] for z in (e_hi, e_lo)], c == 0, c == CC - 1)
                mm.then_inc(e_first, 1)

            def second_product(n, u):
                e = pe.value_load(etable[0:1, 0, ds(n, 1)], min_val=0, max_val=E - 1)
                wait(pe, h_lo_done, n + 1)
                for j in range(S // 128):
                    for f in range(CC):
                        mm = three_passes(pe, ps_2[:, u, j], [z[:, u, f, j * 128:(j + 1) * 128] for z in (h_hi, h_lo)],
                                          [w2[:, ds(e, 1), p, f * C:(f + 1) * C].rearrange("p o f -> p (o f)")
                                           for p in range(2)], f == 0, f == CC - 1)
                mm.then_inc(e_second, 1)

            turn_in(0, 0)
            turn_in(1, 1)
            first_product(0, 0)
            turn_in(2, 0)
            with pe.Fori(0, (ETILES - 4) // 2) as t:
                for v in range(2):
                    n, u = t * 2 + (v + 1), (v + 1) % 2
                    first_product(n, u)
                    turn_in(n + 2, u)
                    second_product(n - 1, 1 - u)
            n = ETILES - 3
            first_product(n, 1)
            turn_in(n + 2, 1)
            second_product(n - 1, 0)
            for n, u in ((ETILES - 2, 0), (ETILES - 1, 1)):
                first_product(n, u)
                second_product(n - 1, 1 - u)
            second_product(ETILES - 1, 1)
            leave(pe)

            enter(pe, 9 * N_ENG)
            with pe.Fori(0, PAIRS) as t:
                for u in range(2):
                    wait(pe, o_summed, t * 2 + (u + 3))
                    wait(pe, o_copied, t * 2 + (u + 1))
                    for k in range(TT):
                        for c in range(CC):
                            mm = pe.transpose(ps_t[:, u, c, k * 128:(k + 1) * 128],
                                              o_sum[:, u, k, c * 128:(c + 1) * 128], ident[:])
                    mm.then_inc(o_turned, 1)

        @block.scalar
        def _(act):
            act.sem_inc(g_copied, 2)
            act.sem_inc(o_copied, 2)
            act.wait_ge(consts_in, 16 * N_CONST)
            act.activation(wg_split[:, 0], wg_stage[:], ACT.Copy).then_inc(w_hi_done, 1)
            act.activation(wp_split[:, 0], wp_stage[:], ACT.Copy).then_inc(w_hi_done, 1)
            leave(act)
            with act.Fori(0, IMAGES) as m:
                enter(act, m * (3 * N_ENG) + N_ENG)
                at = lambda k: m * GROUPS + k

                def deviation(k, u):
                    wait(act, mv_done, at(k) + 1)
                    act.activation(std[0:W, u], mv[0:W, u, :, 1], ACT.Sqrt, bias=eps[0:W, 0:1]).then_inc(std_done, 1)

                def normalise(k, u, rows, wait_rows=True):
                    wait(act, nmr_done, at(k) + 1)
                    if wait_rows:
                        wait(act, rows_lo_done, at(k) - 1)
                    for r in rows:
                        last = act.activation(xn[:, u, r], ps_tok[0:W, u, r], ACT.Identity,
                                              bias=nmr[0:W, u, r:r + 1], scale=rstd[0:W, u, r:r + 1])
                    if R - 1 in rows:
                        last.then_inc(xn_done, 1)

                def keep_products(k, u, rows):
                    wait(act, taps_added, at(k))
                    for r in rows:
                        wait(act, g_ready, at(k) * R + (r + 1))
                        act.activation(g_rows[:, u, r].rearrange("p i b k -> p (i b k)"),
                                       ps_g[0:W, r % 2, 0:GCOL], ACT.Copy).then_inc(g_copied, 1)

                def step(k, u, first=False, last=0):
                    wait(act, ch_ready, at(k) + 1)
                    act.activation(xc_hi[:, u], ps_ch[:, :, 0:T], ACT.Copy).then_inc(xc_hi_done, 1)
                    if last < 2:
                        normalise(k + 1, 1 - u, (0, 1), not first)
                    if not first:
                        keep_products(k - 1, 1 - u, (2,))
                    if last < 2:
                        normalise(k + 1, 1 - u, (2, 3), not first)
                    if not first:
                        keep_products(k - 1, 1 - u, (3,))
                    if last < 1:
                        deviation(k + 2, u)
                    keep_products(k, u, (0, 1))

                deviation(0, 0)
                deviation(1, 1)
                normalise(0, 0, range(R), False)
                step(0, 0, first=True)
                step(1, 1)
                with act.Fori(1, GROUPS // 2 - 1) as t:
                    for u in range(2):
                        step(t * 2 + u, u)
                step(GROUPS - 2, 0, last=1)
                step(GROUPS - 1, 1, last=2)
                keep_products(GROUPS - 1, 1, (2, 3))
                leave(act)
                enter(act, m * (3 * N_ENG) + 2 * N_ENG)
                with act.Fori(0, BATCHES) as k:
                    n = m * BATCHES + k
                    col = act.snap(k * (R2 * W))
                    col2 = act.snap(k * (R2 * W) + R2 * W // 2)
                    wait(act, f_sub, n + 1)
                    act.activation(fb[:], fa[:], ACT.Exp).then_inc(f_exp, 1)
                    wait(act, ft_ready, n + 1)
                    act.activation(filt_t[:, ds(col, R2 * W // 2)], ps_ft[0:2 * FCOL, 0, 0:R2 * W // 2], ACT.Copy)
                    act.activation(filt_t[:, ds(col2, R2 * W // 2)], ps_ft[0:2 * FCOL, 1, 0:R2 * W // 2],
                                   ACT.Copy).then_inc(ft_copied, 1)
                leave(act)
                enter(act, m * (3 * N_ENG) + 3 * N_ENG)
                with act.Fori(0, GROUPS // 2) as t:
                    for u in range(2):
                        for b in range(NB + 1):
                            s = u * (NB + 1) + b
                            wait(act, proj_done, m * STEPS + t * (2 * NB + 2) + (s + 1))
                            for c in range(CC):
                                wait(act, out_ready, m * CATS + t * (4 * NB + 4) + (2 * s + c + 1))
                                act.activation(cat_hi[:, s % 2, c], ps_o[:, c, 0:T], ACT.Copy,
                                               scale=UNSCALE).then_inc(cat_hi_done, 1)
                        wait(act, proj_done, m * STEPS + t * (2 * NB + 2) + ((u + 1) * (NB + 1) + 2))
                        wait(act, y_stored[u], m * (8 * GROUPS) + t * 16)
                        wait(act, y_seen, m * GROUPS + t * 2 + (u + 1))
                        for o in range(CC):
                            last = act.activation(y_out[:, u, o], ps_y[:, o, 0:T], ACT.Identity,
                                                  bias=gn_par[:, 0, o:o + 1])
                        last.then_inc(y_done, 1)
                leave(act)

            enter(act, 7 * N_ENG)
            act.wait_ge(gn_dve, 5)
            act.activation(gn_tmp[:, 4], gn_tmp[:, 3], ACT.Sqrt, bias=eps[:, 2:3]).then_inc(gn_act, 1)
            act.wait_ge(gn_dve, 10)

            def relu(pair, v):
                for u in range(2):
                    at = [at_value(act, pair * CC + c) for c in range(CC)]
                    wait_first(act, c_loaded[v % 2 * 2 + u], (pair - v % 2) * 16 + 32)
                    for c in range(CC):
                        last = act.activation(c_y[:, v % 2, u, c], c_y[:, v % 2, u, c], ACT.Relu,
                                              bias=pair_bias[:].rearrange("p n c -> p (n c)")[:, ds(at[c], 1)],
                                              scale=pair_scale[:].rearrange("p n c -> p (n c)")[:, ds(at[c], 1)])
                    last.then_inc(c_relu, 1)

            def to_route(pair, u):
                wait(act, c_cht, pair * 2 + (u + 1))
                act.activation(c_lnt[:, u], ps_cc[:, :, 0:TC], ACT.Copy).then_inc(c_lntd, 1)

            def norm(pair, v, route=True):
                if route:
                    to_route(pair - 1, 0)
                for u in range(2):
                    wait(act, c_mv, pair * 2 + (u + 1))
                    act.activation(std[:, u, 0:TT], mv[:, u, 0:TT, 1], ACT.Sqrt, bias=eps[:, 1:2]).then_inc(c_std, 1)
                if route:
                    to_route(pair - 1, 1)
                wait(act, c_slotted, pair + 1)
                for u in range(2):
                    wait(act, c_nmr, pair * 2 + (u + 1))
                    for k in range(TT):
                        last = act.activation(c_ln[:, v, u, k, 0:C], ps_ct[:, u, k], ACT.Identity,
                                              bias=nmr[:, u, k:k + 1], scale=rstd[:, u, k:k + 1])
                    last.then_inc(c_lnd, 1)

            def weights_hi(k, w):
                act.wait_ge(w_loaded, 16 * (k + 1))
                act.activation(w[:, :, 0], w_stage[:], ACT.Copy).then_inc(cw_hi, 1)

            def step(pair, v):
                relu(pair + 1, v + 1)
                norm(pair, v)

            relu(0, 0)
            relu(1, 1)
            norm(0, 0, False)
            weights_hi(0, w1)
            step(1, 1)
            step(2, 2)
            with act.Fori(0, (PAIRS - 4) // 4) as t:
                for k in range(3, 7):
                    step(t * 4 + k, k % 4)
            weights_hi(1, w2)
            norm(PAIRS - 1, 3)
            to_route(PAIRS - 1, 0)
            to_route(PAIRS - 1, 1)
            act.wait_ge(top_dve, 1)
            act.activation(soft[:], gap[:], ACT.Exp)
            act.activation(soft1[:, 0:2], gap_two[:], ACT.Exp).then_inc(top_exp, 1)
            leave(act)

            enter(act, 8 * N_ENG)

            def input_hi(n, u):
                wait(act, e_turned, n + 1)
                act.activation(e_hi[:, u], ps_x[:, u], ACT.Copy).then_inc(e_hi_done, 1)

            def hidden(n, u):
                wait(act, e_first, n + 1)
                for f in range(CC):
                    last = act.activation(e_act[:, u, f], ps_1[:, u, f], ACT.Gelu, bias=b1_now[:, u, f:f + 1])
                last.then_inc(e_act_done, 1)
                wait(act, e_act_done, n + 1)
                act.activation(h_hi[:, u], e_act[:, u], ACT.Copy).then_inc(h_hi_done, 1)

            input_hi(0, 0)
            input_hi(1, 1)
            with act.Fori(0, (ETILES - 2) // 2) as t:
                for u in range(2):
                    hidden(t * 2 + u, u)
                    input_hi(t * 2 + (u + 2), u)
            hidden(ETILES - 2, 0)
            hidden(ETILES - 1, 1)
            leave(act)

            enter(act, 9 * N_ENG)
            for m in range(IMAGES):
                with act.Fori(0, CPAIRS) as t:
                    for u in range(2):
                        off, img = act.snap(t * (2 * TC) + u * TC), m
                        wait(act, o_turned, t * 2 + (m * (2 * CPAIRS) + u + 3))
                        wait(act, o_stored[u], t * 16 + m * (16 * CPAIRS))
                        act.activation(o_out[:, u], ps_t[:, u, :, 0:TC], ACT.Copy).then_inc(o_copied, 1)
                        wait(act, o_copied, t * 2 + (m * (2 * CPAIRS) + u + 3))
                        act.dma_start(out_dram[img, :, :, ds(off, TC)], o_out[:, u]).then_inc(o_stored[u], 16)
            for u in range(2):
                wait(act, o_stored[u], 16 * PAIRS)

        @block.vector
        def _(dve):
            dve.memset(eps[:, 0:1], LN1_EPS)
            dve.memset(eps[:, 1:2], LN2_EPS)
            dve.memset(eps[:, 2:3], GN_EPS)
            dve.sem_inc(masked, 4)
            dve.sem_inc(cat_done, 2)
            dve.sem_inc(y_seen, 2)
            dve.sem_inc(e_used, 2)
            dve.sem_inc(o_summed, 2)
            for k, (stage, split) in enumerate(((wg_stage, wg_split), (wp_stage, wp_split))):
                dve.wait_ge(w_hi_done, k + 1)
                dve.tensor_tensor(split[:, 1], stage[:], split[:, 0].bitcast(F32), ALU.subtract).then_inc(w_lo_done, 1)
            leave(dve)
            with dve.Fori(0, IMAGES) as m:
                enter(dve, m * (3 * N_ENG) + N_ENG)
                at = lambda k: m * GROUPS + k

                def statistics(k, u):
                    wait(dve, tok_ready, at(k) + 3)
                    for r in range(R):
                        dve.bn_stats(stats[0:W, u, r], ps_tok[0:W, u, r])
                    dve.drain()
                    for r in range(R):
                        last = dve.bn_aggr(mv[0:W, u, r], stats[0:W, u, r])
                    last.then_inc(mv_done, 1)

                def factors(k, u):
                    wait(dve, std_done, at(k) + 1)
                    dve.reciprocal(rstd[0:W, u], std[0:W, u]).then_inc(rstd_done, 1)
                    wait(dve, rstd_done, at(k) + 1)
                    dve.scalar_tensor_tensor(out=nmr[0:W, u], in0=mv[0:W, u, :, 0], scalar=-1.0, in1=rstd[0:W, u],
                                             op0=ALU.mult, op1=ALU.mult).then_inc(nmr_done, 1)

                def step(k, u, last=False):
                    row = at_value(dve, k * R)
                    wait(dve, xn_done, at(k) + 1)
                    dve.tensor_scalar(rows16[:, ds(row, R), 0, :], xn[:, u], SCALE, None,
                                      ALU.mult).then_inc(rows_hi_done, 1)
                    wait(dve, xc_hi_done, at(k) + 1)
                    dve.tensor_tensor(xc_lo[:, u], ps_ch[:, :, 0:T], xc_hi[:, u].bitcast(F32),
                                      ALU.subtract).then_inc(xc_lo_done, 1)
                    if not last:
                        statistics(k + 2, u)
                    wait(dve, rows_hi_done, at(k) + 1)
                    for r in range(R):
                        line = at_value(dve, k * R + r)
                        ins = dve.scalar_tensor_tensor(out=rows16[:, ds(line, 1), 1, :], in0=xn[:, u, r:r + 1],
                                                       scalar=SCALE, in1=rows16[:, ds(line, 1), 0, :],
                                                       op0=ALU.mult, op1=ALU.subtract)
                    ins.then_inc(rows_lo_done, 1)
                    if not last:
                        factors(k + 2, u)

                statistics(0, 0)
                factors(0, 0)
                statistics(1, 1)
                factors(1, 1)
                with dve.Fori(0, GROUPS // 2 - 1) as t:
                    for u in range(2):
                        step(t * 2 + u, u)
                step(GROUPS - 2, 0, True)
                step(GROUPS - 1, 1, True)
                leave(dve)
                enter(dve, m * (3 * N_ENG) + 2 * N_ENG)
                nine = lambda z: z.rearrange("p (g k) -> p g k", k=TAPS)
                wait_first(dve, shift_loaded, m * 32 + 32)
                with dve.Fori(0, BATCHES) as k:
                    n = m * BATCHES + k
                    base = dve.snap(n * 7)
                    wait(dve, f_ready, n + 1)
                    logit = nine(ps_f[0:W, 0:R2 * FCOL])
                    dve.tensor_reduce(fred[:, 0], logit, AX.X, ALU.max).then_inc(f_dve, 1)
                    wait(dve, f_dve, base + 1)
                    dve.tensor_tensor(nine(fa[:]), logit, fred[:, 0].unsqueeze(2).broadcast_to([W, R2 * NB, TAPS]),
                                      ALU.subtract).then_inc(f_sub, 1)
                    wait(dve, f_exp, n + 1)
                    dve.tensor_reduce(fred[:, 1], nine(fb[:]), AX.X, ALU.add).then_inc(f_dve, 1)
                    wait(dve, f_dve, base + 2)
                    dve.reciprocal(fred[:, 2], fred[:, 1]).then_inc(f_dve, 1)
                    wait(dve, f_dve, base + 3)
                    dve.scalar_tensor_tensor(out=nine(fa[:]), in0=nine(fb[:]), scalar=SCALE,
                                             in1=fred[:, 2].unsqueeze(2).broadcast_to([W, R2 * NB, TAPS]),
                                             op0=ALU.mult, op1=ALU.mult).then_inc(f_dve, 1)
                    wait(dve, f_dve, base + 4)
                    for j in range(3):
                        tap = fa[:].rearrange("p (r g j) -> p r g j", r=R2, j=3)[:, :, :, j:j + 1]
                        last = dve.tensor_tensor(
                            fr[:, j].rearrange("p (r g j) -> p r g j", r=R2, j=3),
                            tap.broadcast_to([W, R2, NB * 3, 3]),
                            rot[:, j].rearrange("p (r g j) -> p r g j", r=1, j=3).broadcast_to([W, R2, NB * 3, 3]), ALU.mult)
                    last.then_inc(f_dve, 1)
                    wait(dve, f_dve, base + 5)
                    dve.tensor_tensor(fa[:], fr[:, 0], fr[:, 1], ALU.add).then_inc(f_dve, 1)
                    wait(dve, f_dve, base + 6)
                    dve.tensor_tensor(fb[:], fa[:], fr[:, 2], ALU.add).then_inc(f_dve, 1)
                    wait(dve, f_dve, base + 7)
                    flat = fb[:].rearrange("p (r f) -> p r f", r=R2)
                    dve.tensor_copy(f16[:, :, 0], flat).then_inc(f_hi_done, 1)
                    wait(dve, f_hi_done, n + 1)
                    dve.tensor_tensor(f16[:, :, 1], flat, f16[:, :, 0], ALU.subtract).then_inc(f_split, 1)
                leave(dve)
                enter(dve, m * (3 * N_ENG) + 3 * N_ENG)

                wait_first(dve, wp_loaded, m * 64 + 64)

                def mask(t, u, b, parts):
                    k = (u * NB + b) * 6
                    s = u * (NB + 1) + b
                    prev = s - 2 if b >= 2 else s - 3
                    wait(dve, out_ready, m * CATS + t * (4 * NB + 4) + max(2 * prev + 2, 0))
                    for part in parts:
                        i, p = part // 2, part % 2
                        n = k + part
                        wait(dve, bc_ready, m * MASKS + t * (12 * NB) + (n + 1))
                        dve.tensor_tensor(bands[:, b % 2, p, i].rearrange("p (r w) -> p r w", r=R),
                                          ps_b[0:W, n % 4, 0:T].rearrange("p (r w) -> p r w", r=R),
                                          band[:, b:b + 1].broadcast_to([W, R, W]), ALU.mult).then_inc(masked, 1)

                def split(t, u, b, chunks):
                    for c in chunks:
                        s = u * (NB + 1) + b
                        wait(dve, cat_hi_done, m * CATS + t * (4 * NB + 4) + (2 * s + c + 1))
                        dve.scalar_tensor_tensor(out=cat_lo[:, s % 2, c], in0=ps_o[:, c, 0:T], scalar=UNSCALE,
                                                 in1=cat_hi[:, s % 2, c].bitcast(F32),
                                                 op0=ALU.mult, op1=ALU.subtract).then_inc(cat_done, 1)

                def group(t, u, more):
                    for b in range(NB):
                        if b + 1 < NB:
                            mask(t, u, b + 1, range(4))
                        split(t, u, b, (0,))
                        if b + 1 < NB:
                            mask(t, u, b + 1, (4, 5))
                        split(t, u, b, (1,))
                    if more:
                        mask(t + u, 1 - u, 0, range(4))
                    split(t, u, NB, range(CC))
                    if more:
                        mask(t + u, 1 - u, 0, (4, 5))
                    wait(dve, y_done, m * GROUPS + t * 2 + (u + 1))
                    g = at_value(dve, t * 12 + u * 6)
                    at = [dve.snap(m * CC + o) for o in range(CC)]
                    for o in range(CC):
                        last = dve.bn_stats(gn_stat[:, ds(at[o], 1), ds(g, 6)], y_out[:, u, o])
                    last.then_inc(y_seen, 1)

                mask(0, 0, 0, range(6))
                with dve.Fori(0, GROUPS // 2 - 1) as t:
                    for u in range(2):
                        group(t, u, True)
                group(GROUPS // 2 - 1, 0, True)
                group(GROUPS // 2 - 1, 1, False)
                leave(dve)

            enter(dve, 7 * N_ENG)
            dve.memset(c_ln[:, :, :, :, MARK:XC], 0.0)
            dve.memset(either[:], 0.0)
            for k in range(IMAGES * CC):
                last = dve.bn_aggr(gn_mv[:, k], gn_stat[:, k])
            last.then_inc(gn_dve, 1)
            dve.wait_ge(gn_pe, 1)
            dve.tensor_tensor(gn_tmp[:, 0], gn_mv[:, :, 0], ps_p[:, 0:4], ALU.subtract).then_inc(gn_dve, 1)
            dve.wait_ge(gn_dve, 2)
            dve.tensor_tensor(gn_tmp[:, 1], gn_tmp[:, 0], gn_tmp[:, 0], ALU.mult).then_inc(gn_dve, 1)
            dve.wait_ge(gn_dve, 3)
            dve.tensor_tensor(gn_tmp[:, 2], gn_tmp[:, 1], gn_mv[:, :, 1], ALU.add).then_inc(gn_dve, 1)
            dve.wait_ge(gn_pe, 2)
            dve.tensor_copy(gn_tmp[:, 3], ps_r[:, 0:4]).then_inc(gn_dve, 1)
            dve.wait_ge(gn_act, 1)
            dve.reciprocal(gn_tmp[:, 5], gn_tmp[:, 4]).then_inc(gn_dve, 1)
            dve.wait_ge(gn_dve, 6)
            gamma = gn_par[:, 1:2].broadcast_to([128, IMAGES, CC])
            beta = gn_par[:, 2:3].broadcast_to([128, IMAGES, CC])
            pair = lambda z: z.rearrange("p (m c) -> p m c", m=IMAGES)
            dve.tensor_tensor(pair(gn_scale[:]), pair(gn_tmp[:, 5]), gamma, ALU.mult).then_inc(gn_dve, 1)
            dve.wait_ge(gn_dve, 7)
            dve.tensor_tensor(gn_tmp[:, 0], ps_p[:, 0:4], gn_scale[:], ALU.mult).then_inc(gn_late, 1)
            dve.wait_ge(gn_late, 1)
            dve.tensor_tensor(pair(gn_bias[:]), beta, pair(gn_tmp[:, 0]), ALU.subtract).then_inc(gn_dve, 1)
            dve.wait_ge(gn_dve, 8)
            for table, source in ((pair_scale, gn_scale), (pair_bias, gn_bias)):
                dve.tensor_copy(table[:].rearrange("p (m n) c -> p m n c", m=IMAGES),
                                source[:].rearrange("p (m n c) -> p m n c", m=IMAGES, n=1)
                                .broadcast_to([128, IMAGES, CPAIRS, CC])).then_inc(gn_dve, 1)
            dve.wait_ge(consts_in, 16 * (N_CONST + 7))
            dve.tensor_copy(next_slot[:], region[:])

            every = lambda z: z.unsqueeze(2).broadcast_to([128, TP, E])
            ranks = order[:].rearrange("p (o e) -> p o e", o=1).broadcast_to([128, TP, E])
            N_PICK = 12

            def compare(pair):
                tile = at_value(dve, pair * TP)
                logits = ps_r[:, 0:TP * E].rearrange("p (t e) -> p t e", e=E)
                wait(dve, c_routed, pair + 1)
                dve.tensor_reduce(largest[:, 0], logits, AX.X, ALU.max).then_inc(c_gap, 1)
                wait(dve, c_gap, pair * 2 + 1)
                dve.tensor_tensor(gap[:, ds(tile, TP)], logits, every(largest[:, 0]), ALU.subtract).then_inc(c_gap, 1)

            def choose(pair):
                tile = at_value(dve, pair * TP)
                count = [0]

                def step(ins):
                    ins.then_inc(c_pick, 1)
                    count[0] += 1
                    wait(dve, c_pick, pair * N_PICK + count[0])

                here = gap[:, ds(tile, TP)]
                wait(dve, c_gap, pair * 2 + 2)
                step(dve.scalar_tensor_tensor(out=pick[:, 0], in0=here, scalar=0.0, in1=ranks,
                                              op0=ALU.is_equal, op1=ALU.mult))
                step(dve.tensor_reduce(largest[:, 1], pick[:, 0], AX.X, ALU.max))
                step(dve.tensor_tensor(chosen[:, 0], ranks, every(largest[:, 1]), ALU.is_equal))
                step(dve.scalar_tensor_tensor(out=pick[:, 1], in0=chosen[:, 0], scalar=-BIG, in1=here,
                                              op0=ALU.mult, op1=ALU.add))
                second = largest[:, 3]
                step(dve.tensor_reduce(second, pick[:, 1], AX.X, ALU.max))
                step(dve.tensor_tensor(pick[:, 2], pick[:, 1], every(second), ALU.is_equal))
                step(dve.tensor_tensor(pick[:, 0], pick[:, 2], ranks, ALU.mult))
                step(dve.tensor_reduce(largest[:, 2], pick[:, 0], AX.X, ALU.max))
                step(dve.tensor_tensor(chosen[:, 1], ranks, every(largest[:, 2]), ALU.is_equal))
                step(dve.tensor_tensor(largest[:, 4], largest[:, 1], largest[:, 2], ALU.is_lt))
                step(dve.tensor_tensor(gap_two[:, 0, ds(tile, TP)], largest[:, 4], second, ALU.mult))
                step(dve.tensor_tensor(gap_two[:, 1, ds(tile, TP)], second, gap_two[:, 0, ds(tile, TP)], ALU.subtract))
                assert count[0] == N_PICK
                dve.tensor_tensor(either[:, 0:TP], chosen[:, 0], chosen[:, 1], ALU.add).then_inc(c_either, 1)

            def place(pair, v):
                tile = at_value(dve, pair * TP)
                wait(dve, c_ranked, pair + 1)
                wait(dve, c_slotted, pair + 1)
                counts = ps_p[:, 0:(TP + 1) * E].rearrange("p (t e) -> p t e", e=E)
                dve.tensor_tensor(slot[:], counts[:, 0:TP], next_slot[:].rearrange("p (o e) -> p o e", o=1)
                                  .broadcast_to([128, TP, E]), ALU.add).then_inc(c_based, 1)
                marks = c_ln[:, v].rearrange("p u k c -> p (u k) c")
                dve.tensor_tensor(marks[:, :, MARK], largest[:, 1], largest[:, 2], ALU.max)
                dve.tensor_copy(marks[:, :, MARK + 1], token[:, ds(tile, TP)])
                wait(dve, c_based, pair * 3 + 1)
                dve.tensor_tensor(next_slot[:], next_slot[:], counts[:, TP], ALU.add)
                dve.tensor_tensor(slot_of[:].rearrange("p a t e -> p a (t e)"),
                                  chosen[:].rearrange("p a t e -> p a (t e)"),
                                  slot[:].rearrange("p (a t) e -> p a (t e)", a=1).broadcast_to([128, TOP, TP * E]),
                                  ALU.mult).then_inc(c_based, 1)
                wait(dve, c_based, pair * 3 + 2)
                dve.tensor_reduce(pos_f[:].rearrange("p a t -> p (a t)"),
                                  slot_of[:].rearrange("p a t e -> p (a t) e"), AX.X, ALU.add).then_inc(c_based, 1)
                wait(dve, c_based, pair * 3 + 3)
                dve.tensor_copy(pos[:, v], pos_f[:]).then_inc(c_pos, 1)

            def residual(pair, v):
                for u in range(2):
                    wait(dve, c_relu, pair * 2 + (u + 1))
                    x = c_x[:, v % 2, u]
                    dve.tensor_tensor(x, x, c_y[:, v % 2, u], ALU.add).then_inc(c_x1, 1)

            def statistics(pair):
                for u in range(2):
                    wait(dve, c_tok, pair * 2 + (u + 5))
                    for k in range(TT):
                        dve.bn_stats(stats[:, u, k], ps_ct[:, u, k])
                dve.drain()
                for u in range(2):
                    for k in range(TT):
                        last = dve.bn_aggr(mv[:, u, k], stats[:, u, k])
                    last.then_inc(c_mv, 1)
                for u in range(2):
                    wait(dve, c_std, pair * 2 + (u + 1))
                    dve.reciprocal(rstd[:, u, 0:TT], std[:, u, 0:TT]).then_inc(c_rstd, 1)
                for u in range(2):
                    wait(dve, c_rstd, pair * 2 + (u + 1))
                    dve.scalar_tensor_tensor(out=nmr[:, u, 0:TT], in0=mv[:, u, 0:TT, 0], scalar=-1.0,
                                             in1=rstd[:, u, 0:TT], op0=ALU.mult, op1=ALU.mult).then_inc(c_nmr, 1)

            def keep(pair, v, stored=True):
                for u in range(2):
                    wait(dve, c_lnd, pair * 2 + (u + 1))
                    if stored:
                        wait(dve, c_stored[u], pair * 16)
                    dve.tensor_tensor(c_res[:, u], ps_ct[:, u, 0:TT], c_ln[:, v, u, :, 0:C], ALU.add).then_inc(c_resd, 1)

            def weights_lo(k, w):
                dve.wait_ge(cw_hi, k + 1)
                dve.tensor_tensor(w[:, :, 1], w_stage[:], w[:, :, 0].bitcast(F32), ALU.subtract).then_inc(cw_lo, 1)

            def step(pair, v, last=False):
                statistics(pair)
                compare(pair - 2)
                place(pair - 3, (v + 1) % 4)
                if not last:
                    residual(pair + 1, v + 1)
                keep(pair, v)
                choose(pair - 2)

            residual(0, 0)
            residual(1, 1)
            statistics(0)
            keep(0, 0, False)
            weights_lo(0, w1)
            statistics(1)
            residual(2, 2)
            keep(1, 1)
            statistics(2)
            compare(0)
            residual(3, 3)
            keep(2, 2)
            choose(0)
            with dve.Fori(0, (PAIRS - 4) // 4) as t:
                for k in range(3, 7):
                    step(t * 4 + k, k % 4)
            weights_lo(1, w2)
            step(PAIRS - 1, 3, True)
            place(PAIRS - 3, 1)
            compare(PAIRS - 2)
            choose(PAIRS - 2)
            place(PAIRS - 2, 2)
            compare(PAIRS - 1)
            choose(PAIRS - 1)
            place(PAIRS - 1, 3)

            steps = [0]

            def step(ins):
                ins.then_inc(top_dve, 1)
                steps[0] += 1
                dve.wait_ge(top_dve, steps[0])

            step(dve.tensor_copy(region_end[:], next_slot[0:1]))
            assert steps[0] == TOP_ENDS
            counts, whole, delta = tab[:, 0], tab[:, 1], tab[:, 2]
            step(dve.tensor_tensor(counts, next_slot[:], region[:], ALU.subtract))
            step(dve.tensor_scalar(tab_i[:, 0], counts, float(S - 1), None, ALU.add))
            step(dve.tensor_scalar(tab_i[:, 1], tab_i[:, 0], S.bit_length() - 1, None, ALU.logical_shift_right))
            step(dve.tensor_copy(whole, tab_i[:, 1]))
            step(dve.tensor_scalar(delta, whole, -float(S), float(CAP), ALU.mult, ALU.add))
            src = whole
            for n, d in enumerate((1, 2, 4)):
                dst = tab[:, 3 + n]
                step(dve.tensor_copy(dst[:, 0:d], src[:, 0:d]))
                step(dve.tensor_tensor(dst[:, d:E], src[:, d:E], src[:, 0:E - d], ALU.add))
                src = dst
            over = lambda z: z.rearrange("p (o e) -> p o e", o=1).broadcast_to([128, ETILES, E])
            step(dve.tensor_tensor(tab_ge[:, 0], etiles[:].unsqueeze(2).broadcast_to([128, ETILES, E]), over(src), ALU.is_ge))
            step(dve.tensor_reduce(tab_row[:, 0], tab_ge[:, 0], AX.X, ALU.add))
            step(dve.tensor_scalar(etable[:, 0], tab_row[0:1, 0], float(E - 1), None, ALU.min))
            step(dve.tensor_scalar(tab_row[:, 2], tab_row[:, 0], -1.0, float(E), ALU.mult, ALU.add))
            step(dve.tensor_scalar(erank[:], tab_row[:, 2], 1.0, None, ALU.max))
            step(dve.tensor_tensor(tab_ge[:, 1], tab_ge[:, 0], over(delta), ALU.mult))
            step(dve.tensor_reduce(tab_row[:, 1], tab_ge[:, 1], AX.X, ALU.add))
            step(dve.scalar_tensor_tensor(out=etable[:, 1], in0=etiles[0:1], scalar=float(S), in1=tab_row[0:1, 1],
                                          op0=ALU.mult, op1=ALU.add))
            dve.wait_ge(top_exp, 1)
            step(dve.tensor_reduce(soft1[:, 2], soft[:], AX.X, ALU.add))
            step(dve.reciprocal(soft1[:, 3], soft1[:, 2]))
            step(dve.tensor_tensor(soft1[:, 4], soft1[:, 0], soft1[:, 3], ALU.mult))
            step(dve.tensor_tensor(soft1[:, 5], soft1[:, 1], soft1[:, 3], ALU.mult))
            step(dve.tensor_tensor(soft1[:, 6], soft1[:, 4], soft1[:, 5], ALU.add))
            step(dve.tensor_scalar(soft1[:, 7], soft1[:, 6], 1e-12, None, ALU.max))
            step(dve.reciprocal(soft1[:, 2], soft1[:, 7]))
            dve.tensor_tensor(gate[:, 0], soft1[:, 4], soft1[:, 2], ALU.mult)
            dve.tensor_tensor(gate[:, 1], soft1[:, 5], soft1[:, 2], ALU.mult)
            leave(dve)

            enter(dve, 8 * N_ENG)

            def input_lo(n, u):
                at = at_value(dve, n)
                wait(dve, e_hi_done, n + 1)
                dve.tensor_tensor(e_lo[:, u], ps_x[:, u], e_hi[:, u].bitcast(F32), ALU.subtract).then_inc(e_lo_done, 1)
                dve.scalar_tensor_tensor(out=e_dest[:, ds(at, 1)], in0=e_x[:, u:u + 1, :, MARK], scalar=erank[:, ds(at, 1)],
                                         in1=e_x[:, u:u + 1, :, MARK + 1], op0=ALU.is_gt, op1=ALU.add).then_inc(e_used, 1)

            def weights(n, u):
                e = dve.value_load(etable[0:1, 0, ds(n, 1)], min_val=0, max_val=E - 1)
                if not isinstance(n, int) or n > 1:
                    wait(dve, e_act_done, n - 1)
                dve.tensor_copy(b1_now[:, u:u + 1], b1[:, ds(e, 1)])
                dve.tensor_copy(w1_now[:, u:u + 1].rearrange("p u a c f -> p u (a c f)"),
                                w1[:, ds(e, 1)].rearrange("p e a c -> p e (a c)")).then_inc(w_ready, 1)

            def hidden_lo(n, u):
                wait(dve, h_hi_done, n + 1)
                dve.tensor_tensor(h_lo[:, u], e_act[:, u], h_hi[:, u].bitcast(F32), ALU.subtract).then_inc(h_lo_done, 1)

            def output(n, u):
                e = dve.value_load(etable[0:1, 0, ds(n, 1)], min_val=0, max_val=E - 1)
                at = at_value(dve, n)
                wait(dve, e_sent, n + 1)
                wait(dve, e_used, n + 3)
                dve.tensor_copy(dest[:, u:u + 1], e_dest[:, ds(at, 1)])
                wait(dve, e_second, n + 1)
                dve.tensor_tensor(e_out[:, u], ps_2[:, u], b2[:, ds(e, 1)].broadcast_to([128, S // 128, C]),
                                  ALU.add).then_inc(e_out_done, 1)

            dve.wait_ge(w_loaded, 64)
            weights(0, 0)
            weights(1, 1)
            input_lo(0, 0)
            input_lo(1, 1)
            hidden_lo(0, 0)
            input_lo(2, 0)
            weights(2, 0)
            with dve.Fori(0, (ETILES - 4) // 2) as t:
                for v in range(2):
                    n, u = t * 2 + (v + 1), (v + 1) % 2
                    hidden_lo(n, u)
                    input_lo(n + 2, u)
                    weights(n + 2, u)
                    output(n - 1, 1 - u)
            n = ETILES - 3
            hidden_lo(n, 1)
            input_lo(n + 2, 1)
            weights(n + 2, 1)
            output(n - 1, 0)
            for n, u in ((ETILES - 2, 0), (ETILES - 1, 1)):
                hidden_lo(n, u)
                output(n - 1, 1 - u)
            output(ETILES - 1, 1)
            leave(dve)

            enter(dve, 9 * N_ENG)

            def combine(t, u):
                at = [at_value(dve, t * TP + (u * TT + k)) for k in range(TT)]
                wait(dve, o_loaded[u], t * 32 + 32)
                for k in range(TT):
                    dve.scalar_tensor_tensor(out=o_acc[:, u, k], in0=o_y[:, u, k, 0], scalar=gate[:, 0, ds(at[k], 1)],
                                             in1=o_acc[:, u, k], op0=ALU.mult, op1=ALU.add).then_inc(o_first, 1)
                wait(dve, o_turned, t * 2 + (u + 1))
                for k in range(TT):
                    wait(dve, o_first, t * TP + (u * TT + k + 1))
                    last = dve.scalar_tensor_tensor(out=o_sum[:, u, k], in0=o_y[:, u, k, 1],
                                                    scalar=gate[:, 1, ds(at[k], 1)], in1=o_acc[:, u, k],
                                                    op0=ALU.mult, op1=ALU.add)
                last.then_inc(o_summed, 1)

            with dve.Fori(0, PAIRS) as t:
                for u in range(2):
                    combine(t, u)

        @block.gpsimd
        def _(pool):
            pool.sem_inc(c_slotted, 4)
            pool.sem_inc(taps_added, 1)
            pool.sem_inc(e_sent, 2)
            leave(pool)
            with pool.Fori(0, IMAGES) as m:
                enter(pool, m * (3 * N_ENG) + N_ENG)
                flat = taps[:].rearrange("p y b j k -> p y (b j k)")
                wide = 3 * TAPS
                pool.memset(taps[:], 0.0)
                pool.drain()
                with pool.Fori(0, GROUPS // 2) as t:
                    for u in range(2):
                        n = m * GROUPS + t * 2 + u

                        def add(i, b, nb):
                            d = DILS[b] if i != 1 else 0
                            row = pool.snap(t * (2 * R) + (u * R + PAD - (i - 1) * d))
                            at = flat[:, ds(row, R), b * wide:(b + nb) * wide]
                            return pool.tensor_tensor(at, at, g_rows[:, u, :, i, b:b + nb].rearrange("p r b k -> p r (b k)"),
                                                      ALU.add)

                        wait(pool, taps_added, n + 1)
                        wait(pool, g_copied, n * R + (R + 2))
                        add(1, 0, NB).then_inc(taps_centre, 1)
                        for b in range(NB - 1, 0, -1):
                            add(0, b, 1)
                            add(2, b, 1)
                        wait(pool, taps_centre, n + 1)
                        add(0, 0, 1).then_inc(taps_near, 1)
                        wait(pool, taps_near, n + 1)
                        add(2, 0, 1).then_inc(taps_added, 1)
                leave(pool)
                enter(pool, m * (3 * N_ENG) + 2 * N_ENG)
                leave(pool)
                enter(pool, m * (3 * N_ENG) + 3 * N_ENG)
                leave(pool)
            enter(pool, 7 * N_ENG)
            with pool.Fori(0, PAIRS // 4) as t:
                for v in range(4):
                    wait_first(pool, c_pos, t * 4 + (v + 1))
                    for u in range(2):
                        for k in range(TT):
                            for z in range(TOP):
                                at = pos[:, v, z, u * TT + k:u * TT + k + 1]
                                pool.indirect_dma_start(out=xs_dram, out_offset=bass.IndirectOffsetOnAxis(ap=at, axis=0),
                                                        in_=c_ln[:, v, u, k], in_offset=None).then_inc(c_scattered, 16)
                    pool.wait_ge(c_scattered, t * (64 * TP * TOP) + (v + 1) * (16 * TP * TOP))
                    pool.sem_inc(c_slotted, 1)
            pool.sem_inc(phase_left, 1)
            enter(pool, 8 * N_ENG)

            def send(n, u, sent):
                wait_first(pool, e_out_done, n + 1)
                for j in range(S // 128):
                    at = dest[:, u, j:j + 1]
                    pool.indirect_dma_start(out=ys_dram, out_offset=bass.IndirectOffsetOnAxis(ap=at, axis=0),
                                            in_=e_out[:, u, j], in_offset=None).then_inc(e_scattered[u], 16)
                    if j == 0 and sent is not None:
                        pool.wait_ge(e_scattered[1 - u], sent)
                        pool.sem_inc(e_sent, 1)

            BATCH = 16 * (S // 128)
            send(0, 0, None)
            with pool.Fori(0, (ETILES - 2) // 2) as t:
                for v in range(2):
                    send(t * 2 + (v + 1), (v + 1) % 2, t * BATCH + BATCH)
            send(ETILES - 1, 1, BATCH * ETILES // 2)
            pool.wait_ge(e_scattered[1], BATCH * ETILES // 2)
            pool.sem_inc(phase_left, 1)
            enter(pool, 9 * N_ENG)


_INS = [
    ("x", lambda i: i["x"]),
    ("w_gen", lambda i: np.stack([i[f"L0_conv_w_{z}"] for z in "abcd"])
        .reshape(NB, TAPS, CC, 128, 3, 3).transpose(3, 2, 4, 0, 5, 1).reshape(128, CC * GCOL)),
    ("w_proj", lambda i: i["L0_conv_w_proj"].reshape(C, 5 * CC, 128).transpose(2, 1, 0).reshape(128, -1)),
    ("b_proj", lambda i: i["L0_conv_b_proj"].reshape(CC, 128).T),
    ("gamma", lambda i: i["L0_conv_gn_gamma"].reshape(CC, 128).T),
    ("beta", lambda i: i["L0_conv_gn_beta"].reshape(CC, 128).T),
    ("router", lambda i: i["L0_ffn_router_w"].reshape(E, CC, 128).transpose(2, 1, 0)),
    ("w1", lambda i: i["L0_ffn_w1"].reshape(E, CC, 128, C).transpose(2, 0, 1, 3).reshape(128, -1)),
    ("b1", lambda i: i["L0_ffn_b1"].reshape(E, CC, 128).transpose(2, 0, 1)),
    ("w2", lambda i: i["L0_ffn_w2"].reshape(E, CC, 128, C).transpose(2, 0, 1, 3).reshape(128, -1)),
    ("b2", lambda i: i["L0_ffn_b2"].reshape(-1)),
]


def kernel(**inputs):
    import numpy as _np
    import concourse.bacc as _bacc
    from concourse import mybir as _mybir
    from concourse.bass_utils import run_bass_kernel_spmd as _run

    nc = _bacc.Bacc("TRN2", target_bir_lowering=False, num_devices=1)
    host = {k: _np.asarray(v) for k, v in inputs.items()}
    given = {name: _np.ascontiguousarray(lay(host)) for name, lay in _INS}
    given.update(shape_constants())
    arrays, aps = {}, {}
    for name, array in given.items():
        arrays[f"in_{name}"] = array
        aps[name] = nc.dram_tensor(f"in_{name}", array.shape, _mybir.dt.from_np(array.dtype), kind="ExternalInput").ap()
    aps["out"] = nc.dram_tensor("out_0", (IMAGES, C, H, W), F32, kind="ExternalOutput").ap()
    build(nc, aps)
    r = _run(nc, [arrays], core_ids=[0])
    return r.results[0]["out_0"]
```

```python
from contextlib import ExitStack

import numpy as np

import concourse.bass as bass
from concourse import mybir

ALU = mybir.AluOpType
ACT = mybir.ActivationFunctionType
AX = mybir.AxisListType
F32 = mybir.dt.float32
F32R = mybir.dt.float32r
F16 = mybir.dt.float16
I32 = mybir.dt.int32
ds = bass.ds

IMAGES, C, H, W = 2, 256, 96, 96
CC = C // 128
PIX = H * W
TOKENS = IMAGES * PIX
DILS = (1, 4, 8, 12)
NB = len(DILS)
PAD = max(DILS)
ROWS = H + 2 * PAD
TAPS = 9
GCOL = 3 * NB * 3 * TAPS
HCOL = NB * 3 * TAPS
FCOL = NB * TAPS
R = 4
T = R * W
GROUPS = H // R
R2 = 12
BATCHES = H // R2
SCALE = 1024.0
LN1_EPS, LN2_EPS, GN_EPS = 1e-6, 1e-5, 1e-5
GN_GROUPS = 32
E = 8
TC = 384
TT = TC // 128
TP = 2 * TT
CPAIRS = PIX // (2 * TC)
PAIRS = IMAGES * CPAIRS
KEPT = 6
TILES = TOKENS // 128
TOP = 2
S = 256
CAP = TOKENS + S
ETILES = TOKENS * TOP // S + E
XC = C + 4
MARK = C
XROWS = E * CAP + E * S
EARLY = 30
BIG = 1e30


def shape_constants():
    x = np.arange(W)
    shift = np.zeros((W, 1 + 2 * NB, W), np.float32)
    shift[:, 0] = np.eye(W)
    for b, d in enumerate(DILS):
        for n, j in enumerate((0, 2)):
            q = x + (j - 1) * d
            ok = (q >= 0) & (q < W)
            shift[q[ok], 1 + 2 * b + n, x[ok]] = 1
    colour = np.stack([(x // d) % 3 for d in DILS])
    rot = np.zeros((W, 3, NB, 3, 3), np.float32)
    for j in range(3):
        for b in range(NB):
            rot[x, j, b, :, (colour[b] + j - 1) % 3] = 1
    sel = np.zeros((2, NB, 3, 3, NB, 3, W), np.float16)
    for b in range(NB):
        for i in range(3):
            for k in range(3):
                sel[:, b, i, k, b, i] = colour[b] == k
    band = np.zeros((W, NB, W), np.float32)
    for b, d in enumerate(DILS):
        band[:, b] = np.isin(x[:, None] - x[None, :], (-d, 0, d))
    fill = np.zeros((2 * E, S, XC), np.float32)
    fill[:, :, MARK + 1] = TOP * TOKENS + np.arange(2 * E * S).reshape(2 * E, S)
    g = np.arange(128) // (C // GN_GROUPS)
    same = (g[:, None] == g[None, :]).astype(np.float32) / (C // GN_GROUPS)
    return {
        "k_ident": np.eye(128, dtype=np.float32),
        "k_ident16": np.stack([np.eye(W), SCALE * np.eye(W)], 1).astype(np.float16),
        "k_shift": shift,
        "k_rot": rot.reshape(W, 3, FCOL),
        "k_sel": sel.reshape(2 * FCOL, NB * 3, W),
        "k_band": band.astype(np.float16),
        "k_same": same,
        "k_order": np.tile(np.arange(E, 0, -1, dtype=np.float32), (128, 1)),
        "k_before": np.stack([np.triu(np.ones((128, 128)), 1), np.ones((128, 128))], 1).astype(np.float16),
        "k_region": np.tile(np.arange(E, dtype=np.float32) * CAP, (128, 1)),
        "k_etiles": np.tile(np.arange(ETILES, dtype=np.float32), (128, 1)),
        "k_fill": fill,
        "k_token": 2.0 * (np.arange(TILES)[None, :] * 128 + np.arange(128)[:, None]).astype(np.float32),
    }


def build(nc, a):
    with ExitStack() as ctx:
        def sbuf(on, name, shape, dt=F32):
            return on.enter_context(nc.sbuf_tensor(name, shape, dt))

        def psum(on, name, shape, dt=F32):
            return on.enter_context(nc.psum_tensor(name, shape, dt))

        def sem(name):
            return ctx.enter_context(nc.semaphore(name))

        def sems(names):
            return [sem(n) for n in names.split()]

        wp_dram = nc.dram_tensor("wp_scratch", [2, 128, 5 * CC * C], F32).ap()
        y_dram = nc.dram_tensor("y_scratch", [IMAGES, 128, CC, PIX], F32).ap()
        res_dram = nc.dram_tensor("res_scratch", [2 * PAIRS, 128, TT * C], F32).ap()
        xs_dram = nc.dram_tensor("expert_in", [XROWS, XC], F32).ap()
        ys_dram = nc.dram_tensor("expert_out", [TOP * TOKENS + 2 * E * S, C], F32).ap()
        x_dram = a["x"].rearrange("m (cc p) h w -> m p cc (h w)", p=128)
        out_dram = a["out"].rearrange("m (cc p) h w -> m p cc (h w)", p=128)

        ident = sbuf(ctx, "ident", [128, 128])
        eps = sbuf(ctx, "eps", [128, 3])
        gn_par = sbuf(ctx, "gn_par", [128, 3, CC])
        gn_stat = sbuf(ctx, "gn_stat", [128, IMAGES * CC, GROUPS * 6])
        gn_scale = sbuf(ctx, "gn_scale", [128, IMAGES * CC])
        gn_bias = sbuf(ctx, "gn_bias", [128, IMAGES * CC])
        stats = sbuf(ctx, "stats", [128, 2, 4, 6])
        mv = sbuf(ctx, "mv", [128, 2, 4, 2])
        std = sbuf(ctx, "std", [128, 2, 4])
        rstd = sbuf(ctx, "rstd", [128, 2, 4])
        nmr = sbuf(ctx, "nmr", [128, 2, 4])

        conv = ExitStack()
        with ExitStack() as r0:
            wg_stage = sbuf(r0, "wg_stage", [128, CC * GCOL])
            wp_stage = sbuf(r0, "wp_stage", [128, 5 * CC * C])
            wp_split = sbuf(r0, "wp_split", [128, 2, 5 * CC * C], F32R)
        rows16 = sbuf(conv, "rows16", [W, H, 2, C], F16)
        ident16 = sbuf(conv, "ident16", [W, 2, W], F16)
        wg = sbuf(conv, "wg", [128, 2, CC, GCOL], F32R)
        with ExitStack() as r1:
            taps = sbuf(r1, "taps", [W, ROWS, NB, 3, TAPS])
            with ExitStack() as r2:
                x_in = sbuf(r2, "x_in", [128, 2, CC, T])
                xn = sbuf(r2, "xn", [W, 2, R, C])
                xc_hi = sbuf(r2, "xc_hi", [128, 2, CC, T], F32R)
                xc_lo = sbuf(r2, "xc_lo", [128, 2, CC, T], F32R)
                g_rows = sbuf(r2, "g_rows", [W, 2, R, 3, NB, 3 * TAPS])
            filt_t = sbuf(r1, "filt_t", [2 * FCOL, PIX], F16)
            with ExitStack() as r2:
                shift = sbuf(r2, "shift", [W, 1 + 2 * NB, W])
                rot = sbuf(r2, "rot", [W, 3, FCOL])
                fa = sbuf(r2, "fa", [W, R2 * FCOL])
                fb = sbuf(r2, "fb", [W, R2 * FCOL])
                f_low = sbuf(r2, "f_low", [W, 2, R2 * FCOL])
                f_pow = sbuf(r2, "f_pow", [W, 2, R2 * FCOL])
                fr = sbuf(r2, "fr", [W, 3, R2 * FCOL])
                f16 = sbuf(r2, "f16", [W, R2, 2, FCOL], F16)
                fred = sbuf(r2, "fred", [W, 4, R2 * NB])
        with ExitStack() as r1:
            sel = sbuf(r1, "sel", [2 * FCOL, NB * 3, W], F16)
            band = sbuf(r1, "band", [W, NB, W], F16)
            wp = sbuf(r1, "wp", [128, 2, 5 * CC, C], F32R)
            bands = sbuf(r1, "bands", [W, 2, 2, 3, T], F16)
            cat_hi = sbuf(r1, "cat_hi", [128, 2, CC, T], F32R)
            cat_lo = sbuf(r1, "cat_lo", [128, 2, CC, T], F32R)
            masked_w = sbuf(r1, "masked_w", [W, 3, T])
            in_2_bytes = NB * 3 * W + NB * W + 2 * 2 * 3 * T
            in_4_bytes = 2 * 5 * CC * C + 2 * 2 * CC * T + 3 * T
            used = 2 * in_2_bytes + 4 * in_4_bytes
            sbuf(r1, "gap_before_filt_t", [128, 4 * ROWS * NB * 3 * TAPS - used], mybir.dt.uint8)
            sbuf(r1, "place_of_filt_t", [128, PIX], F16)
            y_out = sbuf(r1, "y_out", [128, 2, CC, T])
        conv.close()

        gate = sbuf(ctx, "gate", [128, TOP, TILES])
        etable = sbuf(ctx, "etable", [1, 2, ETILES], I32)
        erank = sbuf(ctx, "erank", [128, ETILES])
        w1 = sbuf(ctx, "w1", [128, E, 2, CC * C], F32R)
        w2 = sbuf(ctx, "w2", [128, E, 2, CC * C], F32R)
        b1 = sbuf(ctx, "b1", [128, E, CC])
        b2 = sbuf(ctx, "b2", [128, E, C])
        with ExitStack() as r1:
            c_x = sbuf(r1, "c_x", [128, 2, 2, CC, TC])
            c_y = sbuf(r1, "c_y", [128, 2, 2, CC, TC])
            c_ln = sbuf(r1, "c_ln", [128, KEPT, 2, TT, XC])
            c_lnt = sbuf(r1, "c_lnt", [128, 2, CC, TC])
            c_res = sbuf(r1, "c_res", [128, 2, TT, C])
            w_stage = sbuf(r1, "w_stage", [128, E, CC * C])
            same = sbuf(r1, "same", [128, 128])
            gn_mv = sbuf(r1, "gn_mv", [128, IMAGES * CC, 2])
            gn_tmp = sbuf(r1, "gn_tmp", [128, 6, IMAGES * CC])
            pair_scale = sbuf(r1, "pair_scale", [128, PAIRS, CC])
            pair_bias = sbuf(r1, "pair_bias", [128, PAIRS, CC])
            router = sbuf(r1, "router", [128, CC, E])
            order = sbuf(r1, "order", [128, E])
            before = sbuf(r1, "before", [128, 2, 128], F16)
            region = sbuf(r1, "region", [128, E])
            etiles = sbuf(r1, "etiles", [128, ETILES])
            token = sbuf(r1, "token", [128, TILES])
            region_end = sbuf(r1, "region_end", [1, E], I32)
            gap = sbuf(r1, "gap", [128, TILES, E])
            gap_two = sbuf(r1, "gap_two", [128, TOP, TILES])
            next_slot = sbuf(r1, "next_slot", [128, E])
            largest = sbuf(r1, "largest", [128, 6, TP])
            pick = sbuf(r1, "pick", [128, 3, TP, E])
            chosen = sbuf(r1, "chosen", [128, TOP, TP, E])
            either = sbuf(r1, "either", [128, TP + 1, E], F16)
            slot = sbuf(r1, "slot", [128, TP, E])
            slot_of = sbuf(r1, "slot_of", [128, TOP, TP, E])
            pos_f = sbuf(r1, "pos_f", [128, TOP, TP])
            pos = sbuf(r1, "pos", [128, KEPT, TOP, TP], I32)
            soft = sbuf(r1, "soft", [128, TILES, E])
            soft1 = sbuf(r1, "soft1", [128, 8, TILES])
            tab = sbuf(r1, "tab", [128, 8, E])
            tab_i = sbuf(r1, "tab_i", [128, 2, E], I32)
            tab_ge = sbuf(r1, "tab_ge", [128, 2, ETILES, E])
            tab_row = sbuf(r1, "tab_row", [128, 4, ETILES])
        with ExitStack() as r1:
            res_early = sbuf(r1, "res_early", [128, EARLY, TT, C])
            with ExitStack() as r2:
                e_x = sbuf(r2, "e_x", [128, 2, S // 128, XC])
                e_dest = sbuf(r2, "e_dest", [128, ETILES, S // 128], I32)
                w1_now = sbuf(r2, "w1_now", [128, 2, 2, CC, C], F32R)
                b1_now = sbuf(r2, "b1_now", [128, 2, CC])
                e_hi = sbuf(r2, "e_hi", [128, 2, CC, S], F32R)
                e_lo = sbuf(r2, "e_lo", [128, 2, CC, S], F32R)
                e_act = sbuf(r2, "e_act", [128, 2, CC, S])
                h_hi = sbuf(r2, "h_hi", [128, 2, CC, S], F32R)
                h_lo = sbuf(r2, "h_lo", [128, 2, CC, S], F32R)
                e_out = sbuf(r2, "e_out", [128, 2, S // 128, C])
                dest = sbuf(r2, "dest", [128, 2, S // 128], I32)
            with ExitStack() as r2:
                o_y = sbuf(r2, "o_y", [128, 2, TT, TOP, C])
                o_acc = sbuf(r2, "o_acc", [128, 2, TT, C])
                o_sum = sbuf(r2, "o_sum", [128, 2, TT, C])
                o_out = sbuf(r2, "o_out", [128, 2, CC, TC])

        with ExitStack() as r1:
            ps_tok = psum(r1, "ps_tok", [128, 2, R, C])
            ps_ch = psum(r1, "ps_ch", [128, CC, 512])
            ps_g = psum(r1, "ps_g", [128, 2, 512])
        with ExitStack() as r1:
            ps_f = psum(r1, "ps_f", [128, 2, 512])
            ps_ft = psum(r1, "ps_ft", [128, 2, 1024], F16)
        with ExitStack() as r1:
            ps_b = psum(r1, "ps_b", [128, 4, 512])
            ps_o = psum(r1, "ps_o", [128, CC, 512])
            ps_y = psum(r1, "ps_y", [128, CC, 512])
        with ExitStack() as r1:
            ps_ct = psum(r1, "ps_ct", [128, 2, 4, C])
            ps_cc = psum(r1, "ps_cc", [128, CC, 512])
            ps_r = psum(r1, "ps_r", [128, 512])
            ps_p = psum(r1, "ps_p", [128, 512])
        with ExitStack() as r1:
            ps_x = psum(r1, "ps_x", [128, 2, CC, S])
            ps_1 = psum(r1, "ps_1", [128, 2, CC, S])
            ps_2 = psum(r1, "ps_2", [128, 2, S // 128, C])
        with ExitStack() as r1:
            ps_t = psum(r1, "ps_t", [128, 2, CC, 512])

        consts_in, phase_left, phase_entered = sems("consts_in phase_left phase_entered")
        w_loaded, wp_loaded, w_hi_done, w_lo_done, w_stored = sems(
            "w_loaded wp_loaded w_hi_done w_lo_done w_stored")
        x_loaded = sems("x_loaded0 x_loaded1")
        tok_ready, mv_done, std_done, rstd_done, nmr_done = sems(
            "tok_ready mv_done std_done rstd_done nmr_done")
        xn_done, rows_hi_done, rows_lo_done, ch_ready, xc_hi_done, xc_lo_done = sems(
            "xn_done rows_hi_done rows_lo_done ch_ready xc_hi_done xc_lo_done")
        g_ready, g_copied, taps_centre, taps_near, taps_added = sems(
            "g_ready g_copied taps_centre taps_near taps_added")
        b_consts_in, shift_loaded = sems("b_consts_in shift_loaded")
        f_ready, f_max, f_dve, f_sub, f_exp, f_hi_done, f_split, ft_ready, ft_copied = sems(
            "f_ready f_max f_dve f_sub f_exp f_hi_done f_split ft_ready ft_copied")
        bc_ready, masked, band_hi_done, band_done, out_ready, cat_hi_done, cat_done = sems(
            "bc_ready masked band_hi_done band_done out_ready cat_hi_done cat_done")
        proj_done, y_done, y_seen = sems("proj_done y_done y_seen")
        y_stored = sems("y_stored0 y_stored1")
        gn_dve, gn_act, gn_pe, gn_late = sems("gn_dve gn_act gn_pe gn_late")
        c_loaded = sems("c_loaded00 c_loaded01 c_loaded10 c_loaded11")
        c_relu, c_x1, c_tok, c_mv, c_std, c_rstd, c_nmr, c_lnd = sems(
            "c_relu c_x1 c_tok c_mv c_std c_rstd c_nmr c_lnd")
        c_resd, c_cht, c_lntd, c_routed, c_either, c_ranked, c_pick, c_based, c_pos, c_gap = sems(
            "c_resd c_cht c_lntd c_routed c_either c_ranked c_pick c_based c_pos c_gap")
        c_stored = sems("c_stored0 c_stored1")
        c_slotted = sem("c_slotted")
        c_scattered = sems("c_scattered0 c_scattered1")
        passed, top_dve, top_exp, zeroed, cw_hi, cw_lo = sems("passed top_dve top_exp zeroed cw_hi cw_lo")
        e_loaded = sems("e_loaded0 e_loaded1")
        e_turned, e_hi_done, e_lo_done, e_used, w_ready, e_first, e_act_done = sems(
            "e_turned e_hi_done e_lo_done e_used w_ready e_first e_act_done")
        h_hi_done, h_lo_done, e_second, e_out_done, e_sent = sems("h_hi_done h_lo_done e_second e_out_done e_sent")
        e_scattered = sems("e_scattered0 e_scattered1")
        o_loaded = sems("o_loaded0 o_loaded1")
        res_loaded, b_loaded = sems("res_loaded b_loaded")
        o_first, o_summed, o_turned, o_copied = sems("o_first o_summed o_turned o_copied")
        o_stored = sems("o_stored0 o_stored1")

        N_ENG = 5
        sync = nc.sync

        def leave(eng):
            if eng is sync:
                eng.sem_inc(phase_left, 1)
            else:
                eng.drain().then_inc(phase_left, 1)

        def enter(eng, phases):
            eng.wait_ge(phase_left, phases)
            eng.sem_inc(phase_entered, 1)

        def at_value(eng, x):
            return x if isinstance(x, int) else eng.snap(x)

        def three_passes(eng, out, lhs, rhs, start, stop):
            for n, (p, q) in enumerate(((0, 0), (0, 1), (1, 0))):
                mm = eng.matmul(out, lhs[p], rhs[q], start=start and n == 0, stop=stop and n == 2)
            return mm

        N_CONST = 6
        MASKS = GROUPS * NB * 3
        STEPS = GROUPS * (NB + 1)
        CATS = STEPS * CC
        TOP_ENDS = 1
        UNSCALE = 1.0 / (SCALE * SCALE)
        counted = [
            b_consts_in, band_done, band_hi_done, bc_ready, c_based, c_cht, c_either, c_gap, c_lnd, c_lntd,
            c_mv, c_nmr, c_pick, c_pos, c_ranked, c_relu, c_resd, c_routed, c_rstd, c_slotted, c_std, c_tok,
            c_x1, cat_done, cat_hi_done, ch_ready, e_act_done, e_first, e_hi_done, e_lo_done, e_out_done,
            e_second, e_sent, e_turned, e_used, f_dve, f_exp, f_hi_done, f_max, f_ready, f_split, f_sub,
            ft_copied, ft_ready, g_copied, g_ready, h_hi_done, h_lo_done, masked, mv_done, nmr_done, o_copied,
            o_first, o_summed, o_turned, out_ready, proj_done, rows_hi_done, rows_lo_done, rstd_done,
            shift_loaded, std_done, taps_added, taps_centre, taps_near, tok_ready, w_ready, xc_hi_done,
            xc_lo_done, xn_done, y_done, y_seen, *c_loaded, *c_stored, *e_loaded, *o_loaded, *o_stored,
            *x_loaded, *y_stored,
        ]

        def wait(eng, signal, count):
            eng.wait_ge(signal, count + 1)

        def wait_first(eng, signal, count):
            wait(eng, signal, count)
            eng.sem_inc(passed, 1)

        block = ctx.enter_context(nc.Block())

        @block.sync
        def _(sp):
            for signal in counted:
                sp.sem_inc(signal, 1)
            for dst, src in ((ident[:], a["k_ident"]), (ident16[:], a["k_ident16"]),
                             (gn_par[:, 0], a["b_proj"]), (gn_par[:, 1], a["gamma"]), (gn_par[:, 2], a["beta"])):
                sp.dma_start(dst, src).then_inc(consts_in, 16)
            sp.dma_start(wg_stage[:], a["w_gen"]).then_inc(consts_in, 16)
            leave(sp)

            with sp.Fori(0, IMAGES) as m:
                enter(sp, m * (3 * N_ENG) + N_ENG)
                with sp.Fori(0, GROUPS // 2) as t:
                    for u in range(2):
                        off = sp.snap(t * (2 * T) + u * T)
                        img = sp.snap(m)
                        count = sp.snap(m * GROUPS + t * 2 + (u + 1))
                        wait(sp, tok_ready, count)
                        sp.dma_start(x_in[:, u], x_dram[img, :, :, ds(off, T)]).then_inc(x_loaded[u], 16)
                leave(sp)
                enter(sp, m * (3 * N_ENG) + 2 * N_ENG)
                sp.dma_start(shift[:], a["k_shift"]).then_inc(shift_loaded, 16)
                sp.dma_start(rot[:], a["k_rot"]).then_inc(shift_loaded, 16)
                leave(sp)
                enter(sp, m * (3 * N_ENG) + 3 * N_ENG)
                sp.wait_ge(w_stored, 32)
                for p in range(2):
                    sp.dma_start(wp[:, p].rearrange("p a g -> p (a g)").bitcast(F32), wp_dram[p]).then_inc(b_consts_in, 16)
                sp.dma_start(sel[:], a["k_sel"]).then_inc(b_consts_in, 16)
                sp.dma_start(band[:], a["k_band"]).then_inc(b_consts_in, 16)
                with sp.Fori(0, GROUPS // 2) as t:
                    for u in range(2):
                        off = sp.snap(t * (2 * T) + u * T)
                        img = sp.snap(m)
                        count = sp.snap(m * GROUPS + t * 2 + (u + 1))
                        wait(sp, y_done, count)
                        sp.dma_start(y_dram[img, :, :, ds(off, T)], y_out[:, u]).then_inc(y_stored[u], 16)
                for u in range(2):
                    wait(sp, y_stored[u], m * (8 * GROUPS) + 8 * GROUPS)
                leave(sp)

            enter(sp, 7 * N_ENG)

            def load(m, k, v):
                for u in range(2):
                    off, img = at_value(sp, k * (2 * TC) + u * TC), m
                    wait(sp, c_tok, k * 2 + (m * (2 * CPAIRS) + u + 1))
                    sp.dma_start(c_x[:, v, u], x_dram[img, :, :, ds(off, TC)]).then_inc(c_loaded[2 * v + u], 16)
                    sp.dma_start(c_y[:, v, u], y_dram[img, :, :, ds(off, TC)]).then_inc(c_loaded[2 * v + u], 16)

            def store(pair):
                for u in range(2):
                    grp = at_value(sp, pair * 2 + u)
                    wait(sp, c_resd, pair * 2 + (u + 1))
                    sp.dma_start(res_dram[grp], c_res[:, u].rearrange("p k c -> p (k c)")).then_inc(c_stored[u], 16)

            for dst, src in ((same[:], a["k_same"]), (router[:], a["router"]), (order[:], a["k_order"]),
                             (before[:], a["k_before"]), (region[:], a["k_region"]), (etiles[:], a["k_etiles"]),
                             (token[:], a["k_token"])):
                sp.dma_start(dst, src).then_inc(consts_in, 16)
            load(0, 0, 0)
            load(0, 1, 1)
            for m in range(IMAGES):
                if m:
                    sp.dma_start(w_stage[:].rearrange("p e c -> p (e c)"), a["w1"]).then_inc(w_loaded, 16)
                    sp.dma_start(b1[:], a["b1"]).then_inc(b_loaded, 16)
                    sp.dma_start(b2[:].rearrange("p e c -> p (e c)"), a["b2"].partition_broadcast(128)).then_inc(b_loaded, 16)
                    for e in range(E):
                        sp.dma_start(xs_dram[E * CAP + e * S:E * CAP + (e + 1) * S], a["k_fill"][E + e]).then_inc(zeroed, 16)
                with sp.Fori(1 - m, CPAIRS // 2) as t:
                    for v in range(2):
                        load(m, t * 2 + v, v)
                        store(t * 2 + (m * CPAIRS + v - 2))
            store(PAIRS - 2)
            sp.wait_ge(cw_lo, 1)
            sp.dma_start(w_stage[:].rearrange("p e c -> p (e c)"), a["w2"]).then_inc(w_loaded, 16)
            store(PAIRS - 1)
            for u in range(2):
                wait(sp, c_stored[u], 16 * PAIRS)
            sp.wait_ge(top_dve, TOP_ENDS)
            for e in range(E):
                end = sp.value_load(region_end[0:1, e:e + 1], min_val=e * CAP, max_val=e * CAP + TOKENS)
                sp.dma_start(xs_dram[ds(end, S)], a["k_fill"][e]).then_inc(zeroed, 16)
            sp.wait_ge(zeroed, 16 * 2 * E)
            wait(sp, c_slotted, PAIRS + KEPT)
            leave(sp)

            enter(sp, 8 * N_ENG)
            def load_tiles(t):
                for u in range(2):
                    row = sp.value_load(etable[0:1, 1, ds(t * 2 + u, 1)], min_val=0, max_val=XROWS - S)
                    wait(sp, e_used, t * 2 + (u + 1))
                    sp.dma_start(e_x[:, u].rearrange("p j c -> p (j c)"),
                                 xs_dram[ds(row, S)].rearrange("(p j) c -> p (j c)", p=128)).then_inc(e_loaded[u], 16)

            with sp.Fori(0, EARLY) as t:
                load_tiles(t)
                sp.dma_start(res_early[:, ds(t, 1)].rearrange("p o k c -> p (o k c)"), res_dram[t]).then_inc(res_loaded, 16)
            with sp.Fori(EARLY, ETILES // 2) as t:
                load_tiles(t)
            leave(sp)

            enter(sp, 9 * N_ENG)
            def load_outputs(t, residual):
                for u in range(2):
                    grp = sp.snap(t * 2 + u)
                    row = sp.snap(t * (4 * TC) + u * (2 * TC))
                    wait(sp, o_summed, t * 2 + (u + 1))
                    sp.dma_start(o_y[:, u].rearrange("p k z c -> p k (z c)"),
                                 ys_dram[ds(row, 2 * TC)].rearrange("(k p z) c -> p k (z c)", k=TT, p=128)
                                 ).then_inc(o_loaded[u], 16)
                    if residual:
                        sp.dma_start(o_acc[:, u].rearrange("p k c -> p (k c)"), res_dram[grp]).then_inc(o_loaded[u], 16)

            with sp.Fori(0, EARLY // 2) as t:
                load_outputs(t, False)
            with sp.Fori(EARLY // 2, PAIRS) as t:
                load_outputs(t, True)

        @block.tensor
        def _(pe):
            pe.sem_inc(tok_ready, 2)
            pe.sem_inc(proj_done, 2)
            pe.sem_inc(c_tok, 4)
            pe.sem_inc(o_turned, 2)
            leave(pe)
            pe.wait_ge(consts_in, 16 * N_CONST)
            with pe.Fori(0, IMAGES) as m:
                enter(pe, m * (3 * N_ENG) + N_ENG)
                at = lambda k: m * GROUPS + k

                def tokens(k, u):
                    wait(pe, x_loaded[u], m * (8 * GROUPS) + (k - u) * 8 + 16)
                    for r in range(R):
                        for c in range(CC):
                            mm = pe.transpose(ps_tok[0:W, u, r, c * 128:(c + 1) * 128],
                                              x_in[:, u, c, r * W:(r + 1) * W], ident[:])
                    mm.then_inc(tok_ready, 1)

                def channels(k, u):
                    wait(pe, xn_done, at(k) + 1)
                    wait(pe, xc_lo_done, at(k))
                    for r in range(R):
                        for c in range(CC):
                            mm = pe.transpose(ps_ch[:, c, r * W:(r + 1) * W],
                                              xn[:, u, r, c * 128:(c + 1) * 128], ident[0:W, 0:W])
                    mm.then_inc(ch_ready, 1)

                def tap_products(k, u, rows):
                    wait(pe, xc_lo_done, at(k) + 1)
                    for r in rows:
                        wait(pe, g_copied, at(k) * R + (r + 1))
                        for c in range(CC):
                            mm = three_passes(pe, ps_g[0:W, r % 2, 0:GCOL],
                                              [z[:, u, c, r * W:(r + 1) * W] for z in (xc_hi, xc_lo)],
                                              [wg[:, p, c] for p in range(2)], c == 0, c == CC - 1)
                        mm.then_inc(g_ready, 1)

                def step(k, u, first=False, last=False):
                    channels(k, u)
                    if not last:
                        tokens(k + 2, u)
                    if not first:
                        tap_products(k - 1, 1 - u, (2, 3))
                    tap_products(k, u, (0, 1))

                tokens(0, 0)
                tokens(1, 1)
                pe.wait_ge(w_lo_done, 1)
                step(0, 0, first=True)
                step(1, 1)
                with pe.Fori(1, GROUPS // 2 - 1) as t:
                    for u in range(2):
                        step(t * 2 + u, u)
                step(GROUPS - 2, 0, last=True)
                step(GROUPS - 1, 1, last=True)
                tap_products(GROUPS - 1, 1, (2, 3))
                leave(pe)
                enter(pe, m * (3 * N_ENG) + 2 * N_ENG)
                wait_first(pe, shift_loaded, m * 32 + 32)
                done = lambda k: m * BATCHES + k

                def logits(k, u):
                    row = at_value(pe, k * R2 + PAD)
                    out = ps_f[0:W, u, 0:R2 * FCOL].rearrange("p (r b k) -> p r b k", r=R2, b=NB)
                    wait(pe, f_sub, 0 if isinstance(k, int) and k < 2 else done(k) - 1)
                    for b in range(NB):
                        for s, j in enumerate((0, 2)):
                            pe.matmul(out[:, :, b, :], shift[:, 1 + 2 * b + s], taps[:, ds(row, R2), b, j, :],
                                      start=(b == 0 and s == 0), stop=False, skip_group_check=True)
                    pe.matmul(out, shift[:, 0], taps[:, ds(row, R2), :, 1, :], start=False, stop=True,
                              skip_group_check=True).then_inc(f_ready, 1)

                def turn(k):
                    wait(pe, f_split, done(k) + 1)
                    wait(pe, ft_copied, done(k))
                    for r in range(R2):
                        mm = pe.transpose(ps_ft[0:2 * FCOL, r // 6, (r % 6) * W:(r % 6 + 1) * W],
                                          f16[:, r].rearrange("p a f -> p (a f)"), ident16[:, 0])
                    mm.then_inc(ft_ready, 1)

                logits(0, 0)
                logits(1, 1)
                turn(0)
                with pe.Fori(0, BATCHES // 2 - 1) as t:
                    for v in range(2):
                        logits(t * 2 + (v + 2), v)
                        turn(t * 2 + (v + 1))
                turn(BATCHES - 1)
                leave(pe)
                enter(pe, m * (3 * N_ENG) + 3 * N_ENG)
                wait(pe, b_consts_in, m * 64 + 64)

                def broadcast(g, b):
                    for i in range(3):
                        k = (g * NB + b) * 3 + i
                        wait(pe, masked, m * MASKS + (k + 1))
                        pe.matmul(ps_b[0:W, k % 4, 0:T], sel[:, b * 3 + i], filt_t[:, g * T:(g + 1) * T],
                                  start=True, stop=True).then_inc(bc_ready, 1)

                def branch(g, b):
                    if b < NB:
                        wait(pe, band_done, m * MASKS + ((g * NB + b) * 3 + 3))
                    for c in range(CC):
                        k = (g * (NB + 1) + b) * 2 + c
                        wait(pe, cat_done, m * CATS + (k + 1))
                        for r in range(R):
                            y = g * R + r
                            if b == NB:
                                todo = [(y, p, ident16[:, 1]) for p in range(2)]
                            else:
                                todo = [(y + (i - 1) * DILS[b], p, bands[:, b % 2, q, i, r * W:(r + 1) * W])
                                        for i in range(3) for p, q in ((0, 0), (0, 1), (1, 0))
                                        if 0 <= y + (i - 1) * DILS[b] < H]
                            for n, (src, p, rhs) in enumerate(todo):
                                mm = pe.matmul(ps_o[:, c, r * W:(r + 1) * W], rows16[:, src, p, c * 128:(c + 1) * 128],
                                               rhs, start=n == 0, stop=n == len(todo) - 1)
                        mm.then_inc(out_ready, 1)

                def project(g, b):
                    s = g * (NB + 1) + b
                    wait(pe, cat_done, m * CATS + (2 * s + 4))
                    if b == 0:
                        wait(pe, y_done, m * GROUPS + g)
                    blk = (b + 1) % (NB + 1)
                    for o in range(CC):
                        for c in range(CC):
                            mm = three_passes(pe, ps_y[:, o, 0:T],
                                              [wp[:, p, blk * CC + c, o * 128:(o + 1) * 128] for p in range(2)],
                                              [z[:, s % 2, c] for z in (cat_hi, cat_lo)],
                                              b == 0 and c == 0, b == NB and c == CC - 1)
                    mm.then_inc(proj_done, 1)

                broadcast(0, 0)
                broadcast(0, 1)
                for g in range(GROUPS):
                    for b in range(NB):
                        if b + 2 < NB:
                            broadcast(g, b + 2)
                        elif g + 1 < GROUPS:
                            broadcast(g + 1, b + 2 - NB)
                        branch(g, b)
                        if b:
                            project(g, b - 1)
                        elif g:
                            project(g - 1, NB)
                    branch(g, NB)
                    project(g, NB - 1)
                project(GROUPS - 1, NB)
                leave(pe)

            enter(pe, 7 * N_ENG)
            pe.wait_ge(consts_in, 16 * (N_CONST + 7))
            pe.wait_ge(gn_dve, 1)
            pe.matmul(ps_p[:, 0:4], same[:], gn_mv[:, :, 0], start=True, stop=True).then_inc(gn_pe, 1)
            pe.wait_ge(gn_dve, 4)
            pe.matmul(ps_r[:, 0:4], same[:], gn_tmp[:, 2], start=True, stop=True).then_inc(gn_pe, 1)

            def rank(pair):
                wait(pe, c_either, pair + 1)
                pe.matmul(ps_p[:, 0:(TP + 1) * E], before[:, 0], either[:].rearrange("p t e -> p (t e)"),
                          start=True, stop=False, skip_group_check=True)
                for k in range(TP):
                    pe.matmul(ps_p[:, (k + 1) * E:(TP + 1) * E].rearrange("p (t e) -> p t e", e=E), before[:, 1],
                              either[:, k:k + 1].broadcast_to([128, TP - k, E]),
                              start=False, stop=False, skip_group_check=True)
                pe.matmul(ps_p[:, 0:(TP + 1) * E].rearrange("p (t e) -> p t e", e=E), before[:, 1],
                          either[:, TP:TP + 1].broadcast_to([128, TP + 1, E]),
                          start=False, stop=True, skip_group_check=True).then_inc(c_ranked, 1)

            def turn(pair, v, first=False):
                for u in range(2):
                    wait(pe, c_x1, pair * 2 + (u + 1))
                    if not first:
                        wait(pe, c_resd, pair * 2 + (u - 1))
                    for k in range(TT):
                        for c in range(CC):
                            mm = pe.transpose(ps_ct[:, u, k, c * 128:(c + 1) * 128],
                                              c_x[:, v % 2, u, c, k * 128:(k + 1) * 128], ident[:])
                    mm.then_inc(c_tok, 1)

            def route(pair, v, first=False):
                for u in range(2):
                    wait(pe, c_lnd, pair * 2 + (u + 1))
                    wait(pe, c_lntd, pair * 2 + u)
                    for k in range(TT):
                        for c in range(CC):
                            mm = pe.transpose(ps_cc[:, c, k * 128:(k + 1) * 128],
                                              c_ln[:, v, u, k, c * 128:(c + 1) * 128], ident[:])
                    mm.then_inc(c_cht, 1)
                wait(pe, c_lntd, pair * 2 + 2)
                if not first:
                    wait(pe, c_gap, pair * 2)
                for u in range(2):
                    for k in range(TT):
                        for c in range(CC):
                            mm = pe.matmul(ps_r[:, (u * TT + k) * E:(u * TT + k + 1) * E],
                                           c_lnt[:, u, c, k * 128:(k + 1) * 128], router[:, c],
                                           start=c == 0, stop=c == CC - 1)
                mm.then_inc(c_routed, 1)

            def step(pair, v):
                turn(pair, v)
                rank(pair - 3)
                route(pair - 1, (v - 1) % KEPT)

            turn(0, 0, True)
            turn(1, 1)
            route(0, 0, True)
            turn(2, 2)
            route(1, 1)
            with pe.Fori(0, PAIRS // KEPT - 1) as t:
                for k in range(3, 3 + KEPT):
                    step(t * KEPT + k, k % KEPT)
            for pair in range(PAIRS - 3, PAIRS):
                step(pair, pair % KEPT)
            rank(PAIRS - 3)
            route(PAIRS - 1, (PAIRS - 1) % KEPT)
            rank(PAIRS - 2)
            rank(PAIRS - 1)
            leave(pe)

            enter(pe, 8 * N_ENG)

            def turn_in(n, u):
                wait(pe, e_loaded[u], (n - u) * 8 + 16)
                for j in range(S // 128):
                    for c in range(CC):
                        mm = pe.transpose(ps_x[:, u, c, j * 128:(j + 1) * 128], e_x[:, u, j, c * 128:(c + 1) * 128],
                                          ident[:])
                mm.then_inc(e_turned, 1)

            def first_product(n, u):
                wait(pe, e_lo_done, n + 1)
                wait(pe, w_ready, n + 1)
                for f in range(CC):
                    for c in range(CC):
                        mm = three_passes(pe, ps_1[:, u, f], [w1_now[:, u, p, c, f * 128:(f + 1) * 128] for p in range(2)],
                                          [z[:, u, c] for z in (e_hi, e_lo)], c == 0, c == CC - 1)
                mm.then_inc(e_first, 1)

            def expert(n):
                return pe.value_load(etable[0:1, 0, ds(n, 1)], min_val=0, max_val=E - 1)

            def second_product(n, u, e):
                wait(pe, h_lo_done, n + 1)
                for j in range(S // 128):
                    for f in range(CC):
                        mm = three_passes(pe, ps_2[:, u, j], [z[:, u, f, j * 128:(j + 1) * 128] for z in (h_hi, h_lo)],
                                          [w2[:, ds(e, 1), p, f * C:(f + 1) * C].rearrange("p o f -> p (o f)")
                                           for p in range(2)], f == 0, f == CC - 1)
                mm.then_inc(e_second, 1)

            turn_in(0, 0)
            turn_in(1, 1)
            first_product(0, 0)
            turn_in(2, 0)
            with pe.Fori(0, (ETILES - 4) // 2) as t:
                for v in range(2):
                    n, u = t * 2 + (v + 1), (v + 1) % 2
                    e = expert(n - 1)
                    first_product(n, u)
                    turn_in(n + 2, u)
                    second_product(n - 1, 1 - u, e)
            n = ETILES - 3
            first_product(n, 1)
            turn_in(n + 2, 1)
            second_product(n - 1, 0, expert(n - 1))
            for n, u in ((ETILES - 2, 0), (ETILES - 1, 1)):
                first_product(n, u)
                second_product(n - 1, 1 - u, expert(n - 1))
            second_product(ETILES - 1, 1, expert(ETILES - 1))
            leave(pe)

            enter(pe, 9 * N_ENG)
            with pe.Fori(0, PAIRS) as t:
                for u in range(2):
                    wait(pe, o_summed, t * 2 + (u + 3))
                    wait(pe, o_copied, t * 2 + (u + 1))
                    for k in range(TT):
                        for c in range(CC):
                            mm = pe.transpose(ps_t[:, u, c, k * 128:(k + 1) * 128],
                                              o_sum[:, u, k, c * 128:(c + 1) * 128], ident[:])
                    mm.then_inc(o_turned, 1)

        @block.scalar
        def _(act):
            act.sem_inc(g_copied, 2)
            act.sem_inc(o_copied, 2)
            act.dma_start(wp_stage[:], a["w_proj"]).then_inc(wp_loaded, 16)
            leave(act)
            act.wait_ge(consts_in, 16 * N_CONST)
            flat = lambda z: z.rearrange("p a g -> p (a g)")
            act.activation(flat(wg[:, 0]), wg_stage[:], ACT.Copy).then_inc(w_hi_done, 1)
            act.wait_ge(wp_loaded, 16)
            act.activation(wp_split[:, 0], wp_stage[:], ACT.Copy).then_inc(w_hi_done, 1)
            with act.Fori(0, IMAGES) as m:
                enter(act, m * (3 * N_ENG) + N_ENG)
                at = lambda k: m * GROUPS + k

                def deviation(k, u):
                    wait(act, mv_done, at(k) + 1)
                    act.activation(std[0:W, u], mv[0:W, u, :, 1], ACT.Sqrt, bias=eps[0:W, 0:1]).then_inc(std_done, 1)

                def normalise(k, u, rows, wait_rows=True):
                    wait(act, nmr_done, at(k) + 1)
                    if wait_rows:
                        wait(act, rows_lo_done, at(k) - 1)
                    for r in rows:
                        last = act.activation(xn[:, u, r], ps_tok[0:W, u, r], ACT.Identity,
                                              bias=nmr[0:W, u, r:r + 1], scale=rstd[0:W, u, r:r + 1])
                    if R - 1 in rows:
                        last.then_inc(xn_done, 1)

                def keep_products(k, u, rows):
                    wait(act, taps_added, at(k))
                    for r in rows:
                        wait(act, g_ready, at(k) * R + (r + 1))
                        act.activation(g_rows[:, u, r].rearrange("p i b k -> p (i b k)"),
                                       ps_g[0:W, r % 2, 0:GCOL], ACT.Copy).then_inc(g_copied, 1)

                def step(k, u, first=False, last=0):
                    wait(act, ch_ready, at(k) + 1)
                    act.activation(xc_hi[:, u], ps_ch[:, :, 0:T], ACT.Copy).then_inc(xc_hi_done, 1)
                    if last < 2:
                        normalise(k + 1, 1 - u, (0, 1), not first)
                    if not first:
                        keep_products(k - 1, 1 - u, (2,))
                    if last < 2:
                        normalise(k + 1, 1 - u, (2, 3), not first)
                    if not first:
                        keep_products(k - 1, 1 - u, (3,))
                    if last < 1:
                        deviation(k + 2, u)
                    keep_products(k, u, (0, 1))

                deviation(0, 0)
                deviation(1, 1)
                normalise(0, 0, range(R), False)
                step(0, 0, first=True)
                step(1, 1)
                with act.Fori(1, GROUPS // 2 - 1) as t:
                    for u in range(2):
                        step(t * 2 + u, u)
                step(GROUPS - 2, 0, last=1)
                step(GROUPS - 1, 1, last=2)
                keep_products(GROUPS - 1, 1, (2, 3))
                leave(act)
                enter(act, m * (3 * N_ENG) + 2 * N_ENG)
                done = lambda k: m * BATCHES + k

                def exponentials(k, u):
                    wait(act, f_sub, done(k) + 1)
                    act.activation(f_pow[:, u], f_low[:, u], ACT.Exp).then_inc(f_exp, 1)

                def keep_filters(k):
                    cols = [at_value(act, k * (R2 * W) + h * (R2 * W // 2)) for h in range(2)]
                    wait_first(act, ft_ready, done(k) + 1)
                    for h, col in enumerate(cols):
                        last = act.activation(filt_t[:, ds(col, R2 * W // 2)], ps_ft[0:2 * FCOL, h, 0:R2 * W // 2], ACT.Copy)
                    last.then_inc(ft_copied, 1)

                exponentials(0, 0)
                with act.Fori(0, BATCHES // 2 - 1) as t:
                    for v in range(2):
                        exponentials(t * 2 + (v + 1), 1 - v)
                        keep_filters(t * 2 + v)
                exponentials(BATCHES - 1, 1)
                keep_filters(BATCHES - 2)
                keep_filters(BATCHES - 1)
                leave(act)
                enter(act, m * (3 * N_ENG) + 3 * N_ENG)
                def cat(g, u, b):
                    s = u * (NB + 1) + b
                    wait(act, proj_done, m * STEPS + g * (NB + 1) + (b + 1))
                    for c in range(CC):
                        wait(act, out_ready, m * CATS + g * (2 * NB + 2) + (2 * b + c + 1))
                        act.activation(cat_hi[:, s % 2, c], ps_o[:, c, 0:T], ACT.Copy, scale=UNSCALE).then_inc(cat_hi_done, 1)

                def projected(g, u):
                    wait(act, proj_done, m * STEPS + g * (NB + 1) + (NB + 3))
                    wait(act, y_stored[u], m * (8 * GROUPS) + (g - u) * 8)
                    wait(act, y_seen, m * GROUPS + g + 1)
                    for o in range(CC):
                        last = act.activation(y_out[:, u, o], ps_y[:, o, 0:T], ACT.Identity, bias=gn_par[:, 0, o:o + 1])
                    last.then_inc(y_done, 1)

                def band_hi(g, b):
                    prev = b - 2 if b >= 2 else b - 3
                    used = g * (2 * NB + 2) + (2 * prev + 2)
                    wait(act, out_ready, m * CATS + (max(used, 0) if isinstance(g, int) else used))
                    for i in range(3):
                        wait(act, masked, m * MASKS + g * (3 * NB) + (b * 3 + i + 5))
                        act.activation(bands[:, b % 2, 0, i], masked_w[:, i], ACT.Copy).then_inc(band_hi_done, 1)

                def group(g, u, first=False, last=False):
                    for b in range(NB):
                        cat(g, u, b)
                        if b + 2 < NB:
                            band_hi(g, b + 2)
                        elif not last:
                            band_hi(g + 1, b + 2 - NB)
                        if b == 0 and not first:
                            projected(g - 1, 1 - u)
                    cat(g, u, NB)

                band_hi(0, 0)
                band_hi(0, 1)
                group(0, 0, first=True)
                with act.Fori(0, GROUPS // 2 - 1) as t:
                    for v in range(2):
                        group(t * 2 + (v + 1), 1 - v)
                group(GROUPS - 1, 1, last=True)
                projected(GROUPS - 1, 1)
                leave(act)

            enter(act, 7 * N_ENG)
            act.wait_ge(gn_dve, 5)
            act.activation(gn_tmp[:, 4], gn_tmp[:, 3], ACT.Sqrt, bias=eps[:, 2:3]).then_inc(gn_act, 1)
            act.wait_ge(gn_dve, 10)

            def relu(pair, v):
                for u in range(2):
                    at = [at_value(act, pair * CC + c) for c in range(CC)]
                    wait_first(act, c_loaded[v % 2 * 2 + u], (pair - v % 2) * 16 + 32)
                    for c in range(CC):
                        last = act.activation(c_y[:, v % 2, u, c], c_y[:, v % 2, u, c], ACT.Relu,
                                              bias=pair_bias[:].rearrange("p n c -> p (n c)")[:, ds(at[c], 1)],
                                              scale=pair_scale[:].rearrange("p n c -> p (n c)")[:, ds(at[c], 1)])
                    last.then_inc(c_relu, 1)

            def to_route(pair, u):
                wait(act, c_cht, pair * 2 + (u + 1))
                act.activation(c_lnt[:, u], ps_cc[:, :, 0:TC], ACT.Copy).then_inc(c_lntd, 1)

            def norm(pair, v, route=True):
                if route:
                    to_route(pair - 1, 0)
                for u in range(2):
                    wait(act, c_mv, pair * 2 + (u + 1))
                    act.activation(std[:, u, 0:TT], mv[:, u, 0:TT, 1], ACT.Sqrt, bias=eps[:, 1:2]).then_inc(c_std, 1)
                if route:
                    to_route(pair - 1, 1)
                wait(act, c_slotted, pair + 1)
                for u in range(2):
                    wait(act, c_nmr, pair * 2 + (u + 1))
                    for k in range(TT):
                        last = act.activation(c_ln[:, v, u, k, 0:C], ps_ct[:, u, k], ACT.Identity,
                                              bias=nmr[:, u, k:k + 1], scale=rstd[:, u, k:k + 1])
                    last.then_inc(c_lnd, 1)

            def weights_hi(k, w):
                act.wait_ge(w_loaded, 16 * (k + 1))
                act.activation(w[:, :, 0], w_stage[:], ACT.Copy).then_inc(cw_hi, 1)

            def step(pair, v):
                relu(pair + 1, v + 1)
                norm(pair, v)

            relu(0, 0)
            norm(0, 0, False)
            relu(1, 1)
            step(1, 1)
            step(2, 2)
            with act.Fori(0, PAIRS // KEPT - 1) as t:
                for k in range(3, 3 + KEPT):
                    step(t * KEPT + k, k % KEPT)
            for pair in range(PAIRS - 3, PAIRS - 1):
                step(pair, pair % KEPT)
            weights_hi(0, w1)
            norm(PAIRS - 1, (PAIRS - 1) % KEPT)
            to_route(PAIRS - 1, 0)
            to_route(PAIRS - 1, 1)
            weights_hi(1, w2)
            act.wait_ge(top_dve, 1)
            act.activation(soft[:], gap[:], ACT.Exp)
            act.activation(soft1[:, 0:2], gap_two[:], ACT.Exp).then_inc(top_exp, 1)
            leave(act)

            enter(act, 8 * N_ENG)

            def input_hi(n, u):
                wait(act, e_turned, n + 1)
                act.activation(e_hi[:, u], ps_x[:, u], ACT.Copy).then_inc(e_hi_done, 1)

            def hidden(n, u):
                wait(act, e_first, n + 1)
                for f in range(CC):
                    last = act.activation(e_act[:, u, f], ps_1[:, u, f], ACT.Gelu, bias=b1_now[:, u, f:f + 1])
                last.then_inc(e_act_done, 1)
                wait(act, e_act_done, n + 1)
                act.activation(h_hi[:, u], e_act[:, u], ACT.Copy).then_inc(h_hi_done, 1)

            input_hi(0, 0)
            input_hi(1, 1)
            with act.Fori(0, (ETILES - 2) // 2) as t:
                for u in range(2):
                    hidden(t * 2 + u, u)
                    input_hi(t * 2 + (u + 2), u)
            hidden(ETILES - 2, 0)
            hidden(ETILES - 1, 1)
            leave(act)

            enter(act, 9 * N_ENG)
            for m in range(IMAGES):
                with act.Fori(0, CPAIRS) as t:
                    for u in range(2):
                        off, img = act.snap(t * (2 * TC) + u * TC), m
                        wait(act, o_turned, t * 2 + (m * (2 * CPAIRS) + u + 3))
                        wait(act, o_stored[u], t * 16 + m * (16 * CPAIRS))
                        act.activation(o_out[:, u], ps_t[:, u, :, 0:TC], ACT.Copy).then_inc(o_copied, 1)
                        wait(act, o_copied, t * 2 + (m * (2 * CPAIRS) + u + 3))
                        act.dma_start(out_dram[img, :, :, ds(off, TC)], o_out[:, u]).then_inc(o_stored[u], 16)
            for u in range(2):
                wait(act, o_stored[u], 16 * PAIRS)

        @block.vector
        def _(dve):
            dve.memset(eps[:, 0:1], LN1_EPS)
            dve.memset(eps[:, 1:2], LN2_EPS)
            dve.memset(eps[:, 2:3], GN_EPS)
            dve.sem_inc(masked, 4)
            dve.sem_inc(cat_done, 2)
            dve.sem_inc(y_seen, 2)
            dve.sem_inc(e_used, 2)
            dve.sem_inc(o_summed, 2)
            leave(dve)
            flat = lambda z: z.rearrange("p a g -> p (a g)")
            dve.wait_ge(w_hi_done, 1)
            dve.tensor_tensor(flat(wg[:, 1]), wg_stage[:], flat(wg[:, 0]).bitcast(F32), ALU.subtract).then_inc(w_lo_done, 1)
            dve.wait_ge(w_hi_done, 2)
            dve.tensor_tensor(wp_split[:, 1], wp_stage[:], wp_split[:, 0].bitcast(F32), ALU.subtract).then_inc(w_lo_done, 1)
            with dve.Fori(0, IMAGES) as m:
                enter(dve, m * (3 * N_ENG) + N_ENG)
                at = lambda k: m * GROUPS + k

                def statistics(k, u):
                    wait(dve, tok_ready, at(k) + 3)
                    for r in range(R):
                        dve.bn_stats(stats[0:W, u, r], ps_tok[0:W, u, r])
                    dve.drain()
                    for r in range(R):
                        last = dve.bn_aggr(mv[0:W, u, r], stats[0:W, u, r])
                    last.then_inc(mv_done, 1)

                def factors(k, u):
                    wait(dve, std_done, at(k) + 1)
                    dve.reciprocal(rstd[0:W, u], std[0:W, u]).then_inc(rstd_done, 1)
                    wait(dve, rstd_done, at(k) + 1)
                    dve.scalar_tensor_tensor(out=nmr[0:W, u], in0=mv[0:W, u, :, 0], scalar=-1.0, in1=rstd[0:W, u],
                                             op0=ALU.mult, op1=ALU.mult).then_inc(nmr_done, 1)

                def step(k, u, last=False):
                    row = at_value(dve, k * R)
                    wait(dve, xc_hi_done, at(k) + 1)
                    dve.tensor_tensor(xc_lo[:, u], ps_ch[:, :, 0:T], xc_hi[:, u].bitcast(F32),
                                      ALU.subtract).then_inc(xc_lo_done, 1)
                    wait(dve, xn_done, at(k) + 1)
                    dve.tensor_scalar(rows16[:, ds(row, R), 0, :], xn[:, u], SCALE, None,
                                      ALU.mult).then_inc(rows_hi_done, 1)
                    if not last:
                        statistics(k + 2, u)
                    wait(dve, rows_hi_done, at(k) + 1)
                    for r in range(R):
                        line = at_value(dve, k * R + r)
                        ins = dve.scalar_tensor_tensor(out=rows16[:, ds(line, 1), 1, :], in0=xn[:, u, r:r + 1],
                                                       scalar=SCALE, in1=rows16[:, ds(line, 1), 0, :],
                                                       op0=ALU.mult, op1=ALU.subtract)
                    ins.then_inc(rows_lo_done, 1)
                    if not last:
                        factors(k + 2, u)

                dve.wait_ge(w_stored, 32)
                statistics(0, 0)
                factors(0, 0)
                statistics(1, 1)
                factors(1, 1)
                with dve.Fori(0, GROUPS // 2 - 1) as t:
                    for u in range(2):
                        step(t * 2 + u, u)
                step(GROUPS - 2, 0, True)
                step(GROUPS - 1, 1, True)
                leave(dve)
                enter(dve, m * (3 * N_ENG) + 2 * N_ENG)
                nine = lambda z: z.rearrange("p (g k) -> p g k", k=TAPS)
                wait_first(dve, shift_loaded, m * 32 + 32)
                done = lambda k: m * BATCHES + k

                def lower(k, u):
                    wait(dve, f_ready, done(k) + 1)
                    logit = nine(ps_f[0:W, u, 0:R2 * FCOL])
                    dve.tensor_reduce(fred[:, 3 * u], logit, AX.X, ALU.max).then_inc(f_max, 1)
                    wait(dve, f_max, done(k) + 1)
                    dve.tensor_tensor(nine(f_low[:, u]), logit, fred[:, 3 * u].unsqueeze(2).broadcast_to([W, R2 * NB, TAPS]),
                                      ALU.subtract).then_inc(f_sub, 1)

                def weights(k, u, end=False):
                    base = at_value(dve, done(k) * 6)
                    wait(dve, f_exp, done(k) + 1)
                    dve.tensor_reduce(fred[:, 1], nine(f_pow[:, u]), AX.X, ALU.add).then_inc(f_dve, 1)
                    wait(dve, f_dve, base + 1)
                    dve.reciprocal(fred[:, 2], fred[:, 1]).then_inc(f_dve, 1)
                    wait(dve, f_dve, base + 2)
                    dve.scalar_tensor_tensor(out=nine(fa[:]), in0=nine(f_pow[:, u]), scalar=SCALE,
                                             in1=fred[:, 2].unsqueeze(2).broadcast_to([W, R2 * NB, TAPS]),
                                             op0=ALU.mult, op1=ALU.mult).then_inc(f_dve, 1)
                    wait(dve, f_dve, base + 3)
                    for j in range(3):
                        tap = fa[:].rearrange("p (r g j) -> p r g j", r=R2, j=3)[:, :, :, j:j + 1]
                        last = dve.tensor_tensor(
                            fr[:, j].rearrange("p (r g j) -> p r g j", r=R2, j=3),
                            tap.broadcast_to([W, R2, NB * 3, 3]),
                            rot[:, j].rearrange("p (r g j) -> p r g j", r=1, j=3).broadcast_to([W, R2, NB * 3, 3]), ALU.mult)
                    last.then_inc(f_dve, 1)
                    if not end:
                        lower(k + 1, 1 - u)
                    wait(dve, f_dve, base + 4)
                    dve.tensor_tensor(fa[:], fr[:, 0], fr[:, 1], ALU.add).then_inc(f_dve, 1)
                    wait(dve, f_dve, base + 5)
                    dve.tensor_tensor(fb[:], fa[:], fr[:, 2], ALU.add).then_inc(f_dve, 1)
                    wait(dve, f_dve, base + 6)
                    wait(dve, ft_ready, done(k))
                    flat = fb[:].rearrange("p (r f) -> p r f", r=R2)
                    dve.tensor_copy(f16[:, :, 0], flat).then_inc(f_hi_done, 1)
                    wait(dve, f_hi_done, done(k) + 1)
                    dve.tensor_tensor(f16[:, :, 1], flat, f16[:, :, 0], ALU.subtract).then_inc(f_split, 1)

                lower(0, 0)
                with dve.Fori(0, BATCHES // 2 - 1) as t:
                    for v in range(2):
                        weights(t * 2 + v, v)
                weights(BATCHES - 2, 0)
                weights(BATCHES - 1, 1, True)
                leave(dve)
                enter(dve, m * (3 * N_ENG) + 3 * N_ENG)

                wait_first(dve, b_consts_in, m * 64 + 64)

                def mask(g, u, b):
                    for i in range(3):
                        n = (u * NB + b) * 3 + i
                        done = m * MASKS + g * (3 * NB) + (b * 3 + i)
                        if not isinstance(g, int) or g or b:
                            wait(dve, band_done, done - 2)
                        wait(dve, bc_ready, done + 1)
                        dve.tensor_tensor(masked_w[:, i].rearrange("p (r w) -> p r w", r=R),
                                          ps_b[0:W, n % 4, 0:T].rearrange("p (r w) -> p r w", r=R),
                                          band[:, b:b + 1].broadcast_to([W, R, W]), ALU.mult).then_inc(masked, 1)

                def band_lo(g, b):
                    for i in range(3):
                        wait(dve, band_hi_done, m * MASKS + g * (3 * NB) + (b * 3 + i + 1))
                        dve.tensor_tensor(bands[:, b % 2, 1, i], masked_w[:, i], bands[:, b % 2, 0, i],
                                          ALU.subtract).then_inc(band_done, 1)

                def split(g, u, b):
                    for c in range(CC):
                        s = u * (NB + 1) + b
                        wait(dve, cat_hi_done, m * CATS + g * (2 * NB + 2) + (2 * b + c + 1))
                        dve.scalar_tensor_tensor(out=cat_lo[:, s % 2, c], in0=ps_o[:, c, 0:T], scalar=UNSCALE,
                                                 in1=cat_hi[:, s % 2, c].bitcast(F32),
                                                 op0=ALU.mult, op1=ALU.subtract).then_inc(cat_done, 1)

                def seen(g, u):
                    wait(dve, y_done, m * GROUPS + g + 1)
                    at = at_value(dve, g * 6)
                    image = [dve.snap(m * CC + o) for o in range(CC)]
                    for o in range(CC):
                        last = dve.bn_stats(gn_stat[:, ds(image[o], 1), ds(at, 6)], y_out[:, u, o])
                    last.then_inc(y_seen, 1)

                def group(g, u, first=False, last=False):
                    for b in range(NB):
                        if b + 1 < NB:
                            band_lo(g, b + 1)
                        elif not last:
                            band_lo(g + 1, 0)
                        if b == 1 and not first:
                            seen(g - 1, 1 - u)
                        split(g, u, b)
                        if b + 2 < NB:
                            mask(g, u, b + 2)
                        elif not last:
                            mask(g + 1, 1 - u, b + 2 - NB)
                    split(g, u, NB)

                mask(0, 0, 0)
                band_lo(0, 0)
                mask(0, 0, 1)
                group(0, 0, first=True)
                with dve.Fori(0, GROUPS // 2 - 1) as t:
                    for v in range(2):
                        group(t * 2 + (v + 1), 1 - v)
                group(GROUPS - 1, 1, last=True)
                seen(GROUPS - 1, 1)
                leave(dve)

            enter(dve, 7 * N_ENG)
            dve.memset(c_ln[:, :, :, :, MARK:XC], 0.0)
            dve.memset(either[:], 0.0)
            for k in range(IMAGES * CC):
                last = dve.bn_aggr(gn_mv[:, k], gn_stat[:, k])
            last.then_inc(gn_dve, 1)
            dve.wait_ge(gn_pe, 1)
            dve.tensor_tensor(gn_tmp[:, 0], gn_mv[:, :, 0], ps_p[:, 0:4], ALU.subtract).then_inc(gn_dve, 1)
            dve.wait_ge(gn_dve, 2)
            dve.tensor_tensor(gn_tmp[:, 1], gn_tmp[:, 0], gn_tmp[:, 0], ALU.mult).then_inc(gn_dve, 1)
            dve.wait_ge(gn_dve, 3)
            dve.tensor_tensor(gn_tmp[:, 2], gn_tmp[:, 1], gn_mv[:, :, 1], ALU.add).then_inc(gn_dve, 1)
            dve.wait_ge(gn_pe, 2)
            dve.tensor_copy(gn_tmp[:, 3], ps_r[:, 0:4]).then_inc(gn_dve, 1)
            dve.wait_ge(gn_act, 1)
            dve.reciprocal(gn_tmp[:, 5], gn_tmp[:, 4]).then_inc(gn_dve, 1)
            dve.wait_ge(gn_dve, 6)
            gamma = gn_par[:, 1:2].broadcast_to([128, IMAGES, CC])
            beta = gn_par[:, 2:3].broadcast_to([128, IMAGES, CC])
            pair = lambda z: z.rearrange("p (m c) -> p m c", m=IMAGES)
            dve.tensor_tensor(pair(gn_scale[:]), pair(gn_tmp[:, 5]), gamma, ALU.mult).then_inc(gn_dve, 1)
            dve.wait_ge(gn_dve, 7)
            dve.tensor_tensor(gn_tmp[:, 0], ps_p[:, 0:4], gn_scale[:], ALU.mult).then_inc(gn_late, 1)
            dve.wait_ge(gn_late, 1)
            dve.tensor_tensor(pair(gn_bias[:]), beta, pair(gn_tmp[:, 0]), ALU.subtract).then_inc(gn_dve, 1)
            dve.wait_ge(gn_dve, 8)
            for table, source in ((pair_scale, gn_scale), (pair_bias, gn_bias)):
                dve.tensor_copy(table[:].rearrange("p (m n) c -> p m n c", m=IMAGES),
                                source[:].rearrange("p (m n c) -> p m n c", m=IMAGES, n=1)
                                .broadcast_to([128, IMAGES, CPAIRS, CC])).then_inc(gn_dve, 1)
            dve.wait_ge(consts_in, 16 * (N_CONST + 7))
            dve.tensor_copy(next_slot[:], region[:])

            every = lambda z: z.unsqueeze(2).broadcast_to([128, TP, E])
            ranks = order[:].rearrange("p (o e) -> p o e", o=1).broadcast_to([128, TP, E])
            N_PICK = 12

            def compare(pair):
                tile = at_value(dve, pair * TP)
                logits = ps_r[:, 0:TP * E].rearrange("p (t e) -> p t e", e=E)
                wait(dve, c_routed, pair + 1)
                dve.tensor_reduce(largest[:, 0], logits, AX.X, ALU.max).then_inc(c_gap, 1)
                wait(dve, c_gap, pair * 2 + 1)
                dve.tensor_tensor(gap[:, ds(tile, TP)], logits, every(largest[:, 0]), ALU.subtract).then_inc(c_gap, 1)

            def choose(pair):
                tile = at_value(dve, pair * TP)
                count = [0]

                def step(ins):
                    ins.then_inc(c_pick, 1)
                    count[0] += 1
                    wait(dve, c_pick, pair * N_PICK + count[0])

                here = gap[:, ds(tile, TP)]
                wait(dve, c_gap, pair * 2 + 2)
                step(dve.scalar_tensor_tensor(out=pick[:, 0], in0=here, scalar=0.0, in1=ranks,
                                              op0=ALU.is_equal, op1=ALU.mult))
                step(dve.tensor_reduce(largest[:, 1], pick[:, 0], AX.X, ALU.max))
                step(dve.tensor_tensor(chosen[:, 0], ranks, every(largest[:, 1]), ALU.is_equal))
                step(dve.scalar_tensor_tensor(out=pick[:, 1], in0=chosen[:, 0], scalar=-BIG, in1=here,
                                              op0=ALU.mult, op1=ALU.add))
                second = largest[:, 3]
                step(dve.tensor_reduce(second, pick[:, 1], AX.X, ALU.max))
                step(dve.tensor_tensor(pick[:, 2], pick[:, 1], every(second), ALU.is_equal))
                step(dve.tensor_tensor(pick[:, 0], pick[:, 2], ranks, ALU.mult))
                step(dve.tensor_reduce(largest[:, 2], pick[:, 0], AX.X, ALU.max))
                step(dve.tensor_tensor(chosen[:, 1], ranks, every(largest[:, 2]), ALU.is_equal))
                step(dve.tensor_tensor(largest[:, 4], largest[:, 1], largest[:, 2], ALU.is_lt))
                step(dve.tensor_tensor(gap_two[:, 0, ds(tile, TP)], largest[:, 4], second, ALU.mult))
                step(dve.tensor_tensor(gap_two[:, 1, ds(tile, TP)], second, gap_two[:, 0, ds(tile, TP)], ALU.subtract))
                assert count[0] == N_PICK
                dve.tensor_tensor(either[:, 0:TP], chosen[:, 0], chosen[:, 1], ALU.add).then_inc(c_either, 1)

            def place(pair, v):
                tile = at_value(dve, pair * TP)
                wait(dve, c_ranked, pair + 1)
                wait(dve, c_slotted, pair + 1)
                counts = ps_p[:, 0:(TP + 1) * E].rearrange("p (t e) -> p t e", e=E)
                dve.tensor_tensor(slot[:], counts[:, 0:TP], next_slot[:].rearrange("p (o e) -> p o e", o=1)
                                  .broadcast_to([128, TP, E]), ALU.add).then_inc(c_based, 1)
                marks = c_ln[:, v].rearrange("p u k c -> p (u k) c")
                dve.tensor_tensor(marks[:, :, MARK], largest[:, 1], largest[:, 2], ALU.max)
                dve.tensor_copy(marks[:, :, MARK + 1], token[:, ds(tile, TP)])
                wait(dve, c_based, pair * 3 + 1)
                dve.tensor_tensor(next_slot[:], next_slot[:], counts[:, TP], ALU.add)
                dve.tensor_tensor(slot_of[:].rearrange("p a t e -> p a (t e)"),
                                  chosen[:].rearrange("p a t e -> p a (t e)"),
                                  slot[:].rearrange("p (a t) e -> p a (t e)", a=1).broadcast_to([128, TOP, TP * E]),
                                  ALU.mult).then_inc(c_based, 1)
                wait(dve, c_based, pair * 3 + 2)
                dve.tensor_reduce(pos_f[:].rearrange("p a t -> p (a t)"),
                                  slot_of[:].rearrange("p a t e -> p (a t) e"), AX.X, ALU.add).then_inc(c_based, 1)
                wait(dve, c_based, pair * 3 + 3)
                dve.tensor_copy(pos[:, v], pos_f[:]).then_inc(c_pos, 1)

            def residual(pair, v):
                for u in range(2):
                    wait(dve, c_relu, pair * 2 + (u + 1))
                    x = c_x[:, v % 2, u]
                    dve.tensor_tensor(x, x, c_y[:, v % 2, u], ALU.add).then_inc(c_x1, 1)

            def statistics(pair):
                for u in range(2):
                    wait(dve, c_tok, pair * 2 + (u + 5))
                    for k in range(TT):
                        dve.bn_stats(stats[:, u, k], ps_ct[:, u, k])
                dve.drain()
                for u in range(2):
                    for k in range(TT):
                        last = dve.bn_aggr(mv[:, u, k], stats[:, u, k])
                    last.then_inc(c_mv, 1)
                for u in range(2):
                    wait(dve, c_std, pair * 2 + (u + 1))
                    dve.reciprocal(rstd[:, u, 0:TT], std[:, u, 0:TT]).then_inc(c_rstd, 1)
                for u in range(2):
                    wait(dve, c_rstd, pair * 2 + (u + 1))
                    dve.scalar_tensor_tensor(out=nmr[:, u, 0:TT], in0=mv[:, u, 0:TT, 0], scalar=-1.0,
                                             in1=rstd[:, u, 0:TT], op0=ALU.mult, op1=ALU.mult).then_inc(c_nmr, 1)

            def keep(pair, v, stored=True):
                for u in range(2):
                    wait(dve, c_lnd, pair * 2 + (u + 1))
                    if stored:
                        wait(dve, c_stored[u], pair * 16)
                    dve.tensor_tensor(c_res[:, u], ps_ct[:, u, 0:TT], c_ln[:, v, u, :, 0:C], ALU.add).then_inc(c_resd, 1)

            def weights_lo(k, w):
                dve.wait_ge(cw_hi, k + 1)
                dve.tensor_tensor(w[:, :, 1], w_stage[:], w[:, :, 0].bitcast(F32), ALU.subtract).then_inc(cw_lo, 1)

            def step(pair, v, last=False):
                statistics(pair)
                compare(pair - 2)
                place(pair - 3, (v - 3) % KEPT)
                if not last:
                    residual(pair + 1, v + 1)
                keep(pair, v)
                choose(pair - 2)

            residual(0, 0)
            statistics(0)
            keep(0, 0, False)
            residual(1, 1)
            statistics(1)
            residual(2, 2)
            keep(1, 1)
            statistics(2)
            compare(0)
            residual(3, 3)
            keep(2, 2)
            choose(0)
            with dve.Fori(0, PAIRS // KEPT - 1) as t:
                for k in range(3, 3 + KEPT):
                    step(t * KEPT + k, k % KEPT)
            for pair in range(PAIRS - 3, PAIRS - 1):
                step(pair, pair % KEPT)
            weights_lo(0, w1)
            step(PAIRS - 1, (PAIRS - 1) % KEPT, True)
            place(PAIRS - 3, (PAIRS - 3) % KEPT)
            compare(PAIRS - 2)
            choose(PAIRS - 2)
            place(PAIRS - 2, (PAIRS - 2) % KEPT)
            compare(PAIRS - 1)
            choose(PAIRS - 1)
            place(PAIRS - 1, (PAIRS - 1) % KEPT)
            weights_lo(1, w2)

            steps = [0]

            def step(ins):
                ins.then_inc(top_dve, 1)
                steps[0] += 1
                dve.wait_ge(top_dve, steps[0])

            step(dve.tensor_copy(region_end[:], next_slot[0:1]))
            assert steps[0] == TOP_ENDS
            counts, whole, delta = tab[:, 0], tab[:, 1], tab[:, 2]
            step(dve.tensor_tensor(counts, next_slot[:], region[:], ALU.subtract))
            step(dve.tensor_scalar(tab_i[:, 0], counts, float(S - 1), None, ALU.add))
            step(dve.tensor_scalar(tab_i[:, 1], tab_i[:, 0], S.bit_length() - 1, None, ALU.logical_shift_right))
            step(dve.tensor_copy(whole, tab_i[:, 1]))
            step(dve.tensor_scalar(delta, whole, -float(S), float(CAP), ALU.mult, ALU.add))
            src = whole
            for n, d in enumerate((1, 2, 4)):
                dst = tab[:, 3 + n]
                step(dve.tensor_copy(dst[:, 0:d], src[:, 0:d]))
                step(dve.tensor_tensor(dst[:, d:E], src[:, d:E], src[:, 0:E - d], ALU.add))
                src = dst
            over = lambda z: z.rearrange("p (o e) -> p o e", o=1).broadcast_to([128, ETILES, E])
            step(dve.tensor_tensor(tab_ge[:, 0], etiles[:].unsqueeze(2).broadcast_to([128, ETILES, E]), over(src), ALU.is_ge))
            step(dve.tensor_reduce(tab_row[:, 0], tab_ge[:, 0], AX.X, ALU.add))
            step(dve.tensor_scalar(etable[:, 0], tab_row[0:1, 0], float(E - 1), None, ALU.min))
            step(dve.tensor_scalar(tab_row[:, 2], tab_row[:, 0], -1.0, float(E), ALU.mult, ALU.add))
            step(dve.tensor_scalar(erank[:], tab_row[:, 2], 1.0, None, ALU.max))
            step(dve.tensor_tensor(tab_ge[:, 1], tab_ge[:, 0], over(delta), ALU.mult))
            step(dve.tensor_reduce(tab_row[:, 1], tab_ge[:, 1], AX.X, ALU.add))
            step(dve.scalar_tensor_tensor(out=etable[:, 1], in0=etiles[0:1], scalar=float(S), in1=tab_row[0:1, 1],
                                          op0=ALU.mult, op1=ALU.add))
            dve.wait_ge(top_exp, 1)
            step(dve.tensor_reduce(soft1[:, 2], soft[:], AX.X, ALU.add))
            step(dve.reciprocal(soft1[:, 3], soft1[:, 2]))
            step(dve.tensor_tensor(soft1[:, 4], soft1[:, 0], soft1[:, 3], ALU.mult))
            step(dve.tensor_tensor(soft1[:, 5], soft1[:, 1], soft1[:, 3], ALU.mult))
            step(dve.tensor_tensor(soft1[:, 6], soft1[:, 4], soft1[:, 5], ALU.add))
            step(dve.tensor_scalar(soft1[:, 7], soft1[:, 6], 1e-12, None, ALU.max))
            step(dve.reciprocal(soft1[:, 2], soft1[:, 7]))
            dve.tensor_tensor(gate[:, 0], soft1[:, 4], soft1[:, 2], ALU.mult)
            dve.tensor_tensor(gate[:, 1], soft1[:, 5], soft1[:, 2], ALU.mult)
            leave(dve)

            enter(dve, 8 * N_ENG)

            def input_lo(n, u):
                at = at_value(dve, n)
                wait(dve, e_hi_done, n + 1)
                dve.tensor_tensor(e_lo[:, u], ps_x[:, u], e_hi[:, u].bitcast(F32), ALU.subtract).then_inc(e_lo_done, 1)
                dve.scalar_tensor_tensor(out=e_dest[:, ds(at, 1)], in0=e_x[:, u:u + 1, :, MARK], scalar=erank[:, ds(at, 1)],
                                         in1=e_x[:, u:u + 1, :, MARK + 1], op0=ALU.is_gt, op1=ALU.add).then_inc(e_used, 1)

            def weights(n, u):
                e = dve.value_load(etable[0:1, 0, ds(n, 1)], min_val=0, max_val=E - 1)
                if not isinstance(n, int) or n > 1:
                    wait(dve, e_act_done, n - 1)
                dve.tensor_copy(b1_now[:, u:u + 1], b1[:, ds(e, 1)])
                dve.tensor_copy(w1_now[:, u:u + 1].rearrange("p u a c f -> p u (a c f)"),
                                w1[:, ds(e, 1)].rearrange("p e a c -> p e (a c)")).then_inc(w_ready, 1)

            def hidden_lo(n, u):
                wait(dve, h_hi_done, n + 1)
                dve.tensor_tensor(h_lo[:, u], e_act[:, u], h_hi[:, u].bitcast(F32), ALU.subtract).then_inc(h_lo_done, 1)

            def output(n, u):
                e = dve.value_load(etable[0:1, 0, ds(n, 1)], min_val=0, max_val=E - 1)
                at = at_value(dve, n)
                wait(dve, e_sent, n + 1)
                wait(dve, e_used, n + 3)
                dve.tensor_copy(dest[:, u:u + 1], e_dest[:, ds(at, 1)])
                wait(dve, e_second, n + 1)
                dve.tensor_tensor(e_out[:, u], ps_2[:, u], b2[:, ds(e, 1)].broadcast_to([128, S // 128, C]),
                                  ALU.add).then_inc(e_out_done, 1)

            dve.wait_ge(b_loaded, 32)
            weights(0, 0)
            weights(1, 1)
            input_lo(0, 0)
            input_lo(1, 1)
            hidden_lo(0, 0)
            input_lo(2, 0)
            weights(2, 0)
            with dve.Fori(0, (ETILES - 4) // 2) as t:
                for v in range(2):
                    n, u = t * 2 + (v + 1), (v + 1) % 2
                    hidden_lo(n, u)
                    input_lo(n + 2, u)
                    weights(n + 2, u)
                    output(n - 1, 1 - u)
            n = ETILES - 3
            hidden_lo(n, 1)
            input_lo(n + 2, 1)
            weights(n + 2, 1)
            output(n - 1, 0)
            for n, u in ((ETILES - 2, 0), (ETILES - 1, 1)):
                hidden_lo(n, u)
                output(n - 1, 1 - u)
            output(ETILES - 1, 1)
            leave(dve)

            enter(dve, 9 * N_ENG)

            def combine(t, u, early):
                at = [at_value(dve, t * TP + (u * TT + k)) for k in range(TT)]
                grp = at_value(dve, t * 2 + u)
                if early:
                    wait(dve, o_loaded[u], t * 16 + 16)
                    residual = lambda k: res_early[:, ds(grp, 1), k]
                else:
                    wait(dve, o_loaded[u], t * 32 + (32 - 8 * EARLY))
                    residual = lambda k: o_acc[:, u:u + 1, k]
                for k in range(TT):
                    dve.scalar_tensor_tensor(out=o_acc[:, u:u + 1, k], in0=o_y[:, u:u + 1, k, 0], scalar=gate[:, 0, ds(at[k], 1)],
                                             in1=residual(k), op0=ALU.mult, op1=ALU.add).then_inc(o_first, 1)
                wait(dve, o_turned, t * 2 + (u + 1))
                for k in range(TT):
                    wait(dve, o_first, t * TP + (u * TT + k + 1))
                    last = dve.scalar_tensor_tensor(out=o_sum[:, u, k], in0=o_y[:, u, k, 1],
                                                    scalar=gate[:, 1, ds(at[k], 1)], in1=o_acc[:, u, k],
                                                    op0=ALU.mult, op1=ALU.add)
                last.then_inc(o_summed, 1)

            dve.wait_ge(res_loaded, 16 * EARLY)
            with dve.Fori(0, EARLY // 2) as t:
                for u in range(2):
                    combine(t, u, True)
            with dve.Fori(EARLY // 2, PAIRS) as t:
                for u in range(2):
                    combine(t, u, False)

        @block.gpsimd
        def _(pool):
            pool.sem_inc(c_slotted, KEPT)
            pool.sem_inc(taps_added, 1)
            pool.sem_inc(e_sent, 2)
            leave(pool)
            pool.wait_ge(w_lo_done, 2)
            for p in range(2):
                pool.dma_start(wp_dram[p], wp_split[:, p].bitcast(F32)).then_inc(w_stored, 16)
            with pool.Fori(0, IMAGES) as m:
                enter(pool, m * (3 * N_ENG) + N_ENG)
                flat = taps[:].rearrange("p y b j k -> p y (b j k)")
                wide = 3 * TAPS
                pool.memset(taps[:], 0.0)
                pool.drain()
                with pool.Fori(0, GROUPS // 2) as t:
                    for u in range(2):
                        n = m * GROUPS + t * 2 + u

                        def add(i, b, nb):
                            d = DILS[b] if i != 1 else 0
                            row = pool.snap(t * (2 * R) + (u * R + PAD - (i - 1) * d))
                            at = flat[:, ds(row, R), b * wide:(b + nb) * wide]
                            return pool.tensor_tensor(at, at, g_rows[:, u, :, i, b:b + nb].rearrange("p r b k -> p r (b k)"),
                                                      ALU.add)

                        wait(pool, taps_added, n + 1)
                        wait(pool, g_copied, n * R + (R + 2))
                        add(1, 0, NB).then_inc(taps_centre, 1)
                        for b in range(NB - 1, 0, -1):
                            add(0, b, 1)
                            add(2, b, 1)
                        wait(pool, taps_centre, n + 1)
                        add(0, 0, 1).then_inc(taps_near, 1)
                        wait(pool, taps_near, n + 1)
                        add(2, 0, 1).then_inc(taps_added, 1)
                leave(pool)
                enter(pool, m * (3 * N_ENG) + 2 * N_ENG)
                leave(pool)
                enter(pool, m * (3 * N_ENG) + 3 * N_ENG)
                leave(pool)
            enter(pool, 7 * N_ENG)
            ROUND = 16 * TP * TOP

            def scatter(pair, v, before):
                wait_first(pool, c_pos, pair + 1)
                for k in range(TP):
                    for z in range(TOP):
                        at = pos[:, v, z, k:k + 1]
                        pool.indirect_dma_start(out=xs_dram, out_offset=bass.IndirectOffsetOnAxis(ap=at, axis=0),
                                                in_=c_ln[:, v, k // TT, k % TT], in_offset=None).then_inc(c_scattered[v % 2], 16)
                    if k == 1 and before is not None:
                        pool.wait_ge(c_scattered[1 - v % 2], before)
                        pool.sem_inc(c_slotted, 1)

            scatter(0, 0, None)
            with pool.Fori(0, PAIRS // KEPT - 1) as t:
                for k in range(1, 1 + KEPT):
                    scatter(t * KEPT + k, k % KEPT, t * (KEPT // 2 * ROUND) + ((k - 1) // 2 + 1) * ROUND)
            for pair in range(PAIRS - KEPT + 1, PAIRS):
                scatter(pair, pair % KEPT, ((pair - 1) // 2 + 1) * ROUND)
            pool.wait_ge(c_scattered[(PAIRS - 1) % 2], PAIRS // 2 * ROUND)
            pool.sem_inc(c_slotted, 1)
            pool.sem_inc(phase_left, 1)
            enter(pool, 8 * N_ENG)

            def send(n, u, sent):
                wait_first(pool, e_out_done, n + 1)
                for j in range(S // 128):
                    at = dest[:, u, j:j + 1]
                    pool.indirect_dma_start(out=ys_dram, out_offset=bass.IndirectOffsetOnAxis(ap=at, axis=0),
                                            in_=e_out[:, u, j], in_offset=None).then_inc(e_scattered[u], 16)
                    if j == 0 and sent is not None:
                        pool.wait_ge(e_scattered[1 - u], sent)
                        pool.sem_inc(e_sent, 1)

            BATCH = 16 * (S // 128)
            send(0, 0, None)
            with pool.Fori(0, (ETILES - 2) // 2) as t:
                for v in range(2):
                    send(t * 2 + (v + 1), (v + 1) % 2, t * BATCH + BATCH)
            send(ETILES - 1, 1, BATCH * ETILES // 2)
            pool.wait_ge(e_scattered[1], BATCH * ETILES // 2)
            pool.sem_inc(phase_left, 1)
            enter(pool, 9 * N_ENG)


_INS = [
    ("x", lambda i: i["x"]),
    ("w_gen", lambda i: np.stack([i[f"L0_conv_w_{z}"] for z in "abcd"])
        .reshape(NB, TAPS, CC, 128, 3, 3).transpose(3, 2, 4, 0, 5, 1).reshape(128, CC * GCOL)),
    ("w_proj", lambda i: i["L0_conv_w_proj"].reshape(C, 5 * CC, 128).transpose(2, 1, 0).reshape(128, -1)),
    ("b_proj", lambda i: i["L0_conv_b_proj"].reshape(CC, 128).T),
    ("gamma", lambda i: i["L0_conv_gn_gamma"].reshape(CC, 128).T),
    ("beta", lambda i: i["L0_conv_gn_beta"].reshape(CC, 128).T),
    ("router", lambda i: i["L0_ffn_router_w"].reshape(E, CC, 128).transpose(2, 1, 0)),
    ("w1", lambda i: i["L0_ffn_w1"].reshape(E, CC, 128, C).transpose(2, 0, 1, 3).reshape(128, -1)),
    ("b1", lambda i: i["L0_ffn_b1"].reshape(E, CC, 128).transpose(2, 0, 1)),
    ("w2", lambda i: i["L0_ffn_w2"].reshape(E, CC, 128, C).transpose(2, 0, 1, 3).reshape(128, -1)),
    ("b2", lambda i: i["L0_ffn_b2"].reshape(-1)),
]


def kernel(**inputs):
    import numpy as _np
    import concourse.bacc as _bacc
    from concourse import mybir as _mybir
    from concourse.bass_utils import run_bass_kernel_spmd as _run

    nc = _bacc.Bacc("TRN2", target_bir_lowering=False, num_devices=1)
    host = {k: _np.asarray(v) for k, v in inputs.items()}
    given = {name: _np.ascontiguousarray(lay(host)) for name, lay in _INS}
    given.update(shape_constants())
    arrays, aps = {}, {}
    for name, array in given.items():
        arrays[f"in_{name}"] = array
        aps[name] = nc.dram_tensor(f"in_{name}", array.shape, _mybir.dt.from_np(array.dtype), kind="ExternalInput").ap()
    aps["out"] = nc.dram_tensor("out_0", (IMAGES, C, H, W), F32, kind="ExternalOutput").ap()
    build(nc, aps)
    r = _run(nc, [arrays], core_ids=[0])
    return r.results[0]["out_0"]
```
